# Optimizing a Trainium2 kernel written in Bass

```python
import numpy as np
import jax
import jax.numpy as jnp

def _softmax(x, axis=-1):
    return jax.nn.softmax(x, axis=axis)

def _gelu(x):
    return jax.nn.gelu(x, approximate=True)

def _silu(x):
    return jax.nn.silu(x)

def _sigmoid(x):
    return jax.nn.sigmoid(x)

def _layernorm(x, axis=-1, eps=1e-05):
    m = jnp.mean(x, axis=axis, keepdims=True)
    v = jnp.var(x, axis=axis, keepdims=True)
    return (x - m) / jnp.sqrt(v + eps)

def _scatter_add(tgt, idx, src, axis=0):
    return tgt.at[idx].add(src)

def _segment_sum(src, seg, n):
    return jax.ops.segment_sum(src, seg, n)
kernel_name = 'mk_decoder_preln_d2_seqx_r4_a18694'

def setup_inputs(seed: int=0):
    np.random.seed(seed)
    _w = jnp.asarray

    def _rec_inputs():
        import jax
        import jax.numpy as jnp
        _rk = jax.random.key(seed)
        x = -0.0002928 + 1 * jax.random.normal(jax.random.fold_in(_rk, 1), (2, 1024, 256), jnp.float32)
        _lenS = 1024 - jax.random.randint(jax.random.fold_in(_rk, 7), (2,), 0, max(1, 1024 // 4) + 1, jnp.int32)
        _lenS2 = 77 - jax.random.randint(jax.random.fold_in(_rk, 8), (2,), 0, max(1, 77 // 4) + 1, jnp.int32)
        _ctx_1024P = jax.random.normal(jax.random.fold_in(_rk, 11), (2, 16, 256), jnp.float32)
        _ctx_1024c = jax.random.dirichlet(jax.random.fold_in(_rk, 511), 0.3 * jnp.ones((16,), jnp.float32), (2, 77))
        _ctx_1024t = jnp.einsum('bsk,bkd->bsd', _ctx_1024c, _ctx_1024P)
        _ctx_1024t = _ctx_1024t * jax.lax.rsqrt(jnp.mean(jnp.square(_ctx_1024t)) + 1e-12) * 0.953939
        ctx_1024 = -1.39393e-06 + 0.999914 * (_ctx_1024t + 0.3 * jax.random.normal(jax.random.fold_in(_rk, 611), (2, 77, 256), jnp.float32))
        _validS = jnp.arange(1024)[None, :] < _lenS[:, None]
        _validS2 = jnp.arange(77)[None, :] < _lenS2[:, None]
        _causal = jnp.tril(jnp.ones((1024, 1024), dtype=bool))
        mask_Bx1xS2_if1 = jnp.where(jnp.ones((2, 1, 77), dtype=bool), 1, 0).astype(jnp.int32)
        return (x, ctx_1024, mask_Bx1xS2_if1)
    x, ctx_1024, mask_Bx1xS2_if1 = _rec_inputs()

    def _L0_attn_setup():
        import jax, jax.numpy as jnp
        import numpy as np
        N_HEAD = 16
        ROPE_THETA = 10000.0

        def _rope(x):
            T, D = (x.shape[-2], x.shape[-1])
            inv_freq = 1.0 / ROPE_THETA ** (jnp.arange(0, D, 2, dtype=jnp.float32) / D)
            freqs = jnp.arange(T, dtype=jnp.float32)[:, None] * inv_freq[None, :]
            emb = jnp.repeat(freqs, 2, axis=-1)
            cos, sin = (jnp.cos(emb), jnp.sin(emb))
            xr = x.reshape(*x.shape[:-1], D // 2, 2)
            x1, x2 = (xr[..., 0], xr[..., 1])
            rot = jnp.stack((-x2, x1), axis=-1).reshape(x.shape)
            return x * cos + rot * sin
        key = jax.random.key(seed)
        k0, k1, k2 = jax.random.split(key, 3)
        B, T, C = (2, 512, 256)
        s = 0.02
        return {'x': jax.random.normal(k0, (B, T, C), jnp.float32), 'w_attn': jax.random.normal(k1, (C, 3 * C), jnp.float32) * s, 'b_attn': jnp.zeros((3 * C,), jnp.float32), 'w_proj': jax.random.normal(k2, (C, C), jnp.float32) * s, 'b_proj': jnp.zeros((C,), jnp.float32)}
    _L0_attn_all = _L0_attn_setup()
    _L0_attn_in = {k: v for k, v in _L0_attn_all.items() if k in ('w_attn', 'b_attn', 'w_proj', 'b_proj')}
    del _L0_attn_all

    def _L0_xattn_setup():
        import jax, jax.numpy as jnp
        import numpy as np
        H = 16
        D_MODEL = 256
        D_K = D_MODEL // H
        key = jax.random.key(seed)
        ks = jax.random.split(key, 12)
        B, S = (2, 512)
        scale = 1.0 / np.sqrt(D_MODEL)
        inp = {'query': jax.random.normal(ks[0], (B, S, D_MODEL), jnp.float32), 'key': jax.random.normal(ks[1], (B, S, D_MODEL), jnp.float32), 'value': jax.random.normal(ks[2], (B, S, D_MODEL), jnp.float32), 'mask': jnp.ones((B, 1, S), jnp.int32), 'Wq': jax.random.normal(ks[3], (D_MODEL, D_MODEL), jnp.float32) * scale, 'bq': jnp.zeros((D_MODEL,), jnp.float32), 'Wk': jax.random.normal(ks[4], (D_MODEL, D_MODEL), jnp.float32) * scale, 'bk': jnp.zeros((D_MODEL,), jnp.float32), 'Wv': jax.random.normal(ks[5], (D_MODEL, D_MODEL), jnp.float32) * scale, 'bv': jnp.zeros((D_MODEL,), jnp.float32), 'Wo': jax.random.normal(ks[6], (D_MODEL, D_MODEL), jnp.float32) * scale, 'bo': jnp.zeros((D_MODEL,), jnp.float32)}
        return inp
    _L0_xattn_all = _L0_xattn_setup()
    _L0_xattn_in = {k: v for k, v in _L0_xattn_all.items() if k in ('Wq', 'bq', 'Wk', 'bk', 'Wv', 'bv', 'Wo', 'bo')}
    del _L0_xattn_all

    def _L0_ffn_setup():
        import jax, jax.numpy as jnp
        import numpy as np
        E, D, F = (8, 256, 1024)
        LN_EPS = 1e-05
        key = jax.random.key(seed)
        k = jax.random.split(key, 8)
        x = jax.random.normal(k[0], (4, 512, D), jnp.float32)
        centroids = jax.random.normal(k[1], (E, D), jnp.float32) * 0.1
        ln_g = jnp.ones((E, D), jnp.float32)
        ln_b = jnp.zeros((E, D), jnp.float32)
        w1 = jax.random.normal(k[2], (E, F, D), jnp.float32) * (1.0 / np.sqrt(D))
        b1 = jnp.zeros((E, F), jnp.float32)
        w2 = jax.random.normal(k[3], (E, D, F), jnp.float32) * (1.0 / np.sqrt(F))
        b2 = jnp.zeros((E, D), jnp.float32)
        return {'input_features': x, 'centroids': centroids, 'ln_g': ln_g, 'ln_b': ln_b, 'w1': w1, 'b1': b1, 'w2': w2, 'b2': b2}
    _L0_ffn_all = _L0_ffn_setup()
    _L0_ffn_in = {k: v for k, v in _L0_ffn_all.items() if k in ('centroids', 'ln_g', 'ln_b', 'w1', 'b1', 'w2', 'b2')}
    del _L0_ffn_all

    def _L1_attn_setup():
        import jax, jax.numpy as jnp
        import numpy as np
        N, L, D_IN, H, HD, D_OUT = (4, 512, 256, 16, 64, 256)
        DIM = H * HD
        key = jax.random.key(seed)
        ks = jax.random.split(key, 5)
        s_in = 1.0 / np.sqrt(D_IN)
        s_d = 1.0 / np.sqrt(DIM)
        return {'data': jax.random.normal(ks[0], (N, L, D_IN), jnp.float32), 'W_qkv': jax.random.uniform(ks[1], (D_IN, 3 * DIM), jnp.float32, -s_in, s_in), 'b_qkv': jax.random.uniform(ks[2], (3 * DIM,), jnp.float32, -s_in, s_in), 'W_out': jax.random.uniform(ks[3], (DIM, D_OUT), jnp.float32, -s_d, s_d), 'b_out': jax.random.uniform(ks[4], (D_OUT,), jnp.float32, -s_d, s_d)}
    _L1_attn_all = _L1_attn_setup()
    _L1_attn_in = {k: v for k, v in _L1_attn_all.items() if k in ('W_qkv', 'b_qkv', 'W_out', 'b_out')}
    del _L1_attn_all

    def _L1_xattn_setup():
        import jax, jax.numpy as jnp
        import numpy as np
        D_MODEL = 256
        NUM_HEADS = 16
        D_K = D_MODEL // NUM_HEADS
        B, S = (4, 512)

        def _split_heads(x):
            b, s, _ = x.shape
            return x.reshape(b, s, NUM_HEADS, D_K).transpose(0, 2, 1, 3)
        key = jax.random.key(seed)
        ks = jax.random.split(key, 11)
        scale = 1.0 / np.sqrt(D_MODEL)
        inp = {'query': jax.random.normal(ks[0], (B, S, D_MODEL), jnp.float32), 'key_': jax.random.normal(ks[1], (B, S, D_MODEL), jnp.float32), 'value': jax.random.normal(ks[2], (B, S, D_MODEL), jnp.float32), 'w_q': jax.random.normal(ks[3], (D_MODEL, D_MODEL), jnp.float32) * scale, 'b_q': jnp.zeros((D_MODEL,), jnp.float32), 'w_k': jax.random.normal(ks[4], (D_MODEL, D_MODEL), jnp.float32) * scale, 'b_k': jnp.zeros((D_MODEL,), jnp.float32), 'w_v': jax.random.normal(ks[5], (D_MODEL, D_MODEL), jnp.float32) * scale, 'b_v': jnp.zeros((D_MODEL,), jnp.float32), 'w_o': jax.random.normal(ks[6], (D_MODEL, D_MODEL), jnp.float32) * scale, 'b_o': jnp.zeros((D_MODEL,), jnp.float32)}
        return inp
    _L1_xattn_all = _L1_xattn_setup()
    _L1_xattn_in = {k: v for k, v in _L1_xattn_all.items() if k in ('w_q', 'b_q', 'w_k', 'b_k', 'w_v', 'b_v', 'w_o', 'b_o')}
    del _L1_xattn_all

    def _L1_ffn_setup():
        import jax, jax.numpy as jnp
        import numpy as np
        EPS = 1e-05
        TOP_K = 2

        def _rmsnorm(x, w):
            xf = x.astype(jnp.float32)
            rms = jax.lax.rsqrt(jnp.mean(xf * xf, axis=-1, keepdims=True) + EPS)
            return (xf * rms).astype(x.dtype) * w

        def _attention(x, wq, wk, wv, wo, num_heads=16):
            B, S, H = x.shape
            D = H // num_heads
            q = (x @ wq.T).reshape(B, S, num_heads, D)
            k = (x @ wk.T).reshape(B, S, num_heads, D)
            v = (x @ wv.T).reshape(B, S, num_heads, D)
            scale = 1.0 / jnp.sqrt(jnp.float32(D)).astype(x.dtype)
            scores = jnp.einsum('bqhd,bkhd->bhqk', q, k) * scale
            probs = jax.nn.softmax(scores, axis=-1)
            out = jnp.einsum('bhqk,bkhd->bqhd', probs, v).reshape(B, S, H)
            return out @ wo.T

        def _moe(x, gate_w, w1, w2, w3):
            B, S, H = x.shape
            xf = x.reshape(-1, H)
            logits = xf @ gate_w.T
            rw, sel = jax.lax.top_k(logits, TOP_K)
            rw = jax.nn.softmax(rw.astype(jnp.float32), axis=-1).astype(x.dtype)
            E = gate_w.shape[0]
            out = jnp.zeros_like(xf)
            for e in range(E):
                we = jnp.sum(jnp.where(sel == e, rw, 0.0), axis=-1)
                h = jax.nn.silu(xf @ w1[e].T) * (xf @ w3[e].T)
                out = out + h @ w2[e].T * we[:, None]
            return out.reshape(B, S, H)
        key = jax.random.key(seed)
        ks = jax.random.split(key, 10)
        H, I, E, NH = (256, 512, 8, 16)
        B, S = (2, 512)
        s = 0.02
        return {'x': jax.random.normal(ks[0], (B, S, H), jnp.float32), 'ln1_w': jnp.ones((H,), jnp.float32), 'ln2_w': jnp.ones((H,), jnp.float32), 'wq': jax.random.normal(ks[1], (H, H), jnp.float32) * s, 'wk': jax.random.normal(ks[2], (H, H), jnp.float32) * s, 'wv': jax.random.normal(ks[3], (H, H), jnp.float32) * s, 'wo': jax.random.normal(ks[4], (H, H), jnp.float32) * s, 'gate_w': jax.random.normal(ks[5], (E, H), jnp.float32) * s, 'w1': jax.random.normal(ks[6], (E, I, H), jnp.float32) * s, 'w2': jax.random.normal(ks[7], (E, H, I), jnp.float32) * s, 'w3': jax.random.normal(ks[8], (E, I, H), jnp.float32) * s}
    _L1_ffn_all = _L1_ffn_setup()
    _L1_ffn_in = {k: v for k, v in _L1_ffn_all.items() if k in ('ln1_w', 'ln2_w', 'wq', 'wk', 'wv', 'wo', 'gate_w', 'w1', 'w2', 'w3')}
    del _L1_ffn_all
    return {'x': x, 'ctx_1024': ctx_1024, 'mask_Bx1xS2_if1': mask_Bx1xS2_if1, 'L0_attn_w_attn': _L0_attn_in['w_attn'], 'L0_attn_b_attn': _L0_attn_in['b_attn'], 'L0_attn_w_proj': _L0_attn_in['w_proj'], 'L0_attn_b_proj': _L0_attn_in['b_proj'], 'L0_xattn_Wq': _L0_xattn_in['Wq'], 'L0_xattn_bq': _L0_xattn_in['bq'], 'L0_xattn_Wk': _L0_xattn_in['Wk'], 'L0_xattn_bk': _L0_xattn_in['bk'], 'L0_xattn_Wv': _L0_xattn_in['Wv'], 'L0_xattn_bv': _L0_xattn_in['bv'], 'L0_xattn_Wo': _L0_xattn_in['Wo'], 'L0_xattn_bo': _L0_xattn_in['bo'], 'L0_ffn_centroids': _L0_ffn_in['centroids'], 'L0_ffn_ln_g': _L0_ffn_in['ln_g'], 'L0_ffn_ln_b': _L0_ffn_in['ln_b'], 'L0_ffn_w1': _L0_ffn_in['w1'], 'L0_ffn_b1': _L0_ffn_in['b1'], 'L0_ffn_w2': _L0_ffn_in['w2'], 'L0_ffn_b2': _L0_ffn_in['b2'], 'L1_attn_W_qkv': _L1_attn_in['W_qkv'], 'L1_attn_b_qkv': _L1_attn_in['b_qkv'], 'L1_attn_W_out': _L1_attn_in['W_out'], 'L1_attn_b_out': _L1_attn_in['b_out'], 'L1_xattn_w_q': _L1_xattn_in['w_q'], 'L1_xattn_b_q': _L1_xattn_in['b_q'], 'L1_xattn_w_k': _L1_xattn_in['w_k'], 'L1_xattn_b_k': _L1_xattn_in['b_k'], 'L1_xattn_w_v': _L1_xattn_in['w_v'], 'L1_xattn_b_v': _L1_xattn_in['b_v'], 'L1_xattn_w_o': _L1_xattn_in['w_o'], 'L1_xattn_b_o': _L1_xattn_in['b_o'], 'L1_ffn_ln1_w': _L1_ffn_in['ln1_w'], 'L1_ffn_ln2_w': _L1_ffn_in['ln2_w'], 'L1_ffn_wq': _L1_ffn_in['wq'], 'L1_ffn_wk': _L1_ffn_in['wk'], 'L1_ffn_wv': _L1_ffn_in['wv'], 'L1_ffn_wo': _L1_ffn_in['wo'], 'L1_ffn_gate_w': _L1_ffn_in['gate_w'], 'L1_ffn_w1': _L1_ffn_in['w1'], 'L1_ffn_w2': _L1_ffn_in['w2'], 'L1_ffn_w3': _L1_ffn_in['w3']}

def reference(x, ctx_1024, mask_Bx1xS2_if1, L0_attn_w_attn, L0_attn_b_attn, L0_attn_w_proj, L0_attn_b_proj, L0_xattn_Wq, L0_xattn_bq, L0_xattn_Wk, L0_xattn_bk, L0_xattn_Wv, L0_xattn_bv, L0_xattn_Wo, L0_xattn_bo, L0_ffn_centroids, L0_ffn_ln_g, L0_ffn_ln_b, L0_ffn_w1, L0_ffn_b1, L0_ffn_w2, L0_ffn_b2, L1_attn_W_qkv, L1_attn_b_qkv, L1_attn_W_out, L1_attn_b_out, L1_xattn_w_q, L1_xattn_b_q, L1_xattn_w_k, L1_xattn_b_k, L1_xattn_w_v, L1_xattn_b_v, L1_xattn_w_o, L1_xattn_b_o, L1_ffn_ln1_w, L1_ffn_ln2_w, L1_ffn_wq, L1_ffn_wk, L1_ffn_wv, L1_ffn_wo, L1_ffn_gate_w, L1_ffn_w1, L1_ffn_w2, L1_ffn_w3):
    import jax
    import jax.numpy as jnp

    def _L0_attn_ref(x, w_attn, b_attn, w_proj, b_proj):
        import jax, jax.numpy as jnp
        import numpy as np
        N_HEAD = 16
        ROPE_THETA = 10000.0

        def _rope(x):
            T, D = (x.shape[-2], x.shape[-1])
            inv_freq = 1.0 / ROPE_THETA ** (jnp.arange(0, D, 2, dtype=jnp.float32) / D)
            freqs = jnp.arange(T, dtype=jnp.float32)[:, None] * inv_freq[None, :]
            emb = jnp.repeat(freqs, 2, axis=-1)
            cos, sin = (jnp.cos(emb), jnp.sin(emb))
            xr = x.reshape(*x.shape[:-1], D // 2, 2)
            x1, x2 = (xr[..., 0], xr[..., 1])
            rot = jnp.stack((-x2, x1), axis=-1).reshape(x.shape)
            return x * cos + rot * sin
        B, T, C = x.shape
        H = N_HEAD
        D = C // H
        qkv = x @ w_attn + b_attn
        q, k, v = jnp.split(qkv, 3, axis=-1)

        def heads(t):
            return t.reshape(B, T, H, D).transpose(0, 2, 1, 3)
        q, k, v = (heads(q), heads(k), heads(v))
        q = _rope(q)
        k = _rope(k)
        att = jnp.einsum('bhqd,bhkd->bhqk', q, k) * (1.0 / np.sqrt(D))
        causal = jnp.tril(jnp.ones((T, T), dtype=bool))
        att = jnp.where(causal, att, -jnp.inf)
        att = jax.nn.softmax(att, axis=-1)
        y = jnp.einsum('bhqk,bhkd->bhqd', att, v)
        y = y.transpose(0, 2, 1, 3).reshape(B, T, C)
        return y @ w_proj + b_proj

    def _L0_xattn_ref(query, key, value, mask, Wq, bq, Wk, bk, Wv, bv, Wo, bo):
        import jax, jax.numpy as jnp
        import numpy as np
        H = 16
        D_MODEL = 256
        D_K = D_MODEL // H
        B, S, _ = query.shape

        def proj(x, W, b):
            y = x @ W.T + b
            return y.reshape(B, -1, H, D_K).transpose(0, 2, 1, 3)
        q = proj(query, Wq, bq)
        k = proj(key, Wk, bk)
        v = proj(value, Wv, bv)
        scores = jnp.einsum('bhqd,bhkd->bhqk', q, k) / np.sqrt(D_K)
        m = mask[:, None, :, :]
        scores = jnp.where(m == 0, jnp.float32(-1000000000.0), scores)
        p_attn = jax.nn.softmax(scores, axis=-1)
        x = jnp.einsum('bhqk,bhkd->bhqd', p_attn, v)
        x = x.transpose(0, 2, 1, 3).reshape(B, -1, H * D_K)
        return x @ Wo.T + bo

    def _L0_ffn_ref(input_features, centroids, ln_g, ln_b, w1, b1, w2, b2):
        import jax, jax.numpy as jnp
        import numpy as np
        E, D, F = (8, 256, 1024)
        LN_EPS = 1e-05
        x = input_features.reshape(-1, D)
        aff = jax.lax.stop_gradient(x) @ centroids.T
        assign = jnp.argmax(aff, axis=1)
        onehot = jax.nn.one_hot(assign, E, dtype=x.dtype)
        mu = jnp.mean(x, axis=-1, keepdims=True)
        var = jnp.mean((x - mu) ** 2, axis=-1, keepdims=True)
        xhat = (x - mu) * jax.lax.rsqrt(var + LN_EPS)
        xn = xhat[None, :, :] * ln_g[:, None, :] + ln_b[:, None, :]
        h = jax.nn.relu(jnp.einsum('etd,efd->etf', xn, w1) + b1[:, None, :])
        y = x[None, :, :] + jnp.einsum('etf,edf->etd', h, w2) + b2[:, None, :]
        alpha = jax.nn.sigmoid(x @ centroids.T)
        a = alpha.T[:, :, None]
        gated = a * y + (1.0 - a) * x[None, :, :]
        out = jnp.einsum('te,etd->td', onehot, gated)
        return out.reshape(input_features.shape)

    def _L1_attn_ref(data, W_qkv, b_qkv, W_out, b_out):
        import jax, jax.numpy as jnp
        import numpy as np
        N, L, D_IN, H, HD, D_OUT = (4, 512, 256, 16, 64, 256)
        DIM = H * HD
        n, l = (data.shape[0], data.shape[1])
        qkv = data @ W_qkv + b_qkv
        q = qkv[:, :, :DIM].reshape(n, l, H, HD)
        k = qkv[:, :, DIM:2 * DIM].reshape(n, l, H, HD)
        v = qkv[:, :, 2 * DIM:].reshape(n, l, H, HD)
        scores = jnp.einsum('nqhd,nkhd->nhqk', q, k)
        attention = jax.nn.softmax(scores / jnp.sqrt(jnp.float32(HD)), axis=3)
        out = jnp.einsum('nhql,nlhd->nqhd', attention, v).reshape(n, l, DIM)
        return out @ W_out + b_out

    def _L1_xattn_ref(query, key_, value, w_q, b_q, w_k, b_k, w_v, b_v, w_o, b_o):
        import jax, jax.numpy as jnp
        import numpy as np
        D_MODEL = 256
        NUM_HEADS = 16
        D_K = D_MODEL // NUM_HEADS
        B, S = (4, 512)

        def _split_heads(x):
            b, s, _ = x.shape
            return x.reshape(b, s, NUM_HEADS, D_K).transpose(0, 2, 1, 3)
        Q = _split_heads(query @ w_q.T + b_q)
        K = _split_heads(key_ @ w_k.T + b_k)
        V = _split_heads(value @ w_v.T + b_v)
        scores = jnp.einsum('bhqd,bhkd->bhqk', Q, K) / jnp.sqrt(jnp.float32(D_K))
        probs = jax.nn.softmax(scores, axis=-1)
        attn = jnp.einsum('bhqk,bhkd->bhqd', probs, V)
        attn = attn.transpose(0, 2, 1, 3).reshape(query.shape[0], query.shape[1], D_MODEL)
        return attn @ w_o.T + b_o

    def _L1_ffn_ref(x, ln1_w, ln2_w, wq, wk, wv, wo, gate_w, w1, w2, w3):
        import jax, jax.numpy as jnp
        import numpy as np
        EPS = 1e-05
        TOP_K = 2

        def _rmsnorm(x, w):
            xf = x.astype(jnp.float32)
            rms = jax.lax.rsqrt(jnp.mean(xf * xf, axis=-1, keepdims=True) + EPS)
            return (xf * rms).astype(x.dtype) * w

        def _attention(x, wq, wk, wv, wo, num_heads=16):
            B, S, H = x.shape
            D = H // num_heads
            q = (x @ wq.T).reshape(B, S, num_heads, D)
            k = (x @ wk.T).reshape(B, S, num_heads, D)
            v = (x @ wv.T).reshape(B, S, num_heads, D)
            scale = 1.0 / jnp.sqrt(jnp.float32(D)).astype(x.dtype)
            scores = jnp.einsum('bqhd,bkhd->bhqk', q, k) * scale
            probs = jax.nn.softmax(scores, axis=-1)
            out = jnp.einsum('bhqk,bkhd->bqhd', probs, v).reshape(B, S, H)
            return out @ wo.T

        def _moe(x, gate_w, w1, w2, w3):
            B, S, H = x.shape
            xf = x.reshape(-1, H)
            logits = xf @ gate_w.T
            rw, sel = jax.lax.top_k(logits, TOP_K)
            rw = jax.nn.softmax(rw.astype(jnp.float32), axis=-1).astype(x.dtype)
            E = gate_w.shape[0]
            out = jnp.zeros_like(xf)
            for e in range(E):
                we = jnp.sum(jnp.where(sel == e, rw, 0.0), axis=-1)
                h = jax.nn.silu(xf @ w1[e].T) * (xf @ w3[e].T)
                out = out + h @ w2[e].T * we[:, None]
            return out.reshape(B, S, H)
        h = x + _attention(_rmsnorm(x, ln1_w), wq, wk, wv, wo)
        h = h + _moe(_rmsnorm(h, ln2_w), gate_w, w1, w2, w3)
        return h
    x = x + _L0_attn_ref(_layernorm(x, axis=-1), L0_attn_w_attn, L0_attn_b_attn, L0_attn_w_proj, L0_attn_b_proj)
    x = x + _L0_xattn_ref(_layernorm(x, axis=-1), ctx_1024, ctx_1024, mask_Bx1xS2_if1, L0_xattn_Wq, L0_xattn_bq, L0_xattn_Wk, L0_xattn_bk, L0_xattn_Wv, L0_xattn_bv, L0_xattn_Wo, L0_xattn_bo)
    x = x + _L0_ffn_ref(_layernorm(x, axis=-1), L0_ffn_centroids, L0_ffn_ln_g, L0_ffn_ln_b, L0_ffn_w1, L0_ffn_b1, L0_ffn_w2, L0_ffn_b2)
    x = x + _L1_attn_ref(_layernorm(x, axis=-1), L1_attn_W_qkv, L1_attn_b_qkv, L1_attn_W_out, L1_attn_b_out)
    x = x + _L1_xattn_ref(_layernorm(x, axis=-1), ctx_1024, ctx_1024, L1_xattn_w_q, L1_xattn_b_q, L1_xattn_w_k, L1_xattn_b_k, L1_xattn_w_v, L1_xattn_b_v, L1_xattn_w_o, L1_xattn_b_o)
    x = x + _L1_ffn_ref(_layernorm(x, axis=-1), L1_ffn_ln1_w, L1_ffn_ln2_w, L1_ffn_wq, L1_ffn_wk, L1_ffn_wv, L1_ffn_wo, L1_ffn_gate_w, L1_ffn_w1, L1_ffn_w2, L1_ffn_w3)
    return x

_drawn_inputs = setup_inputs


def setup_inputs(seed=0):
    import zlib

    import numpy as np

    out = dict(_drawn_inputs(seed))
    spreads = {'L0_attn_b_attn': (0.0, 0.1),
     'L0_attn_b_proj': (0.0, 0.1),
     'L0_xattn_bq': (0.0, 0.1),
     'L0_xattn_bk': (0.0, 0.8),
     'L0_xattn_bv': (0.0, 0.1),
     'L0_xattn_bo': (0.0, 0.1),
     'L0_ffn_ln_g': (1.0, 0.2),
     'L0_ffn_ln_b': (0.0, 0.341),
     'L0_ffn_b1': (0.0, 0.343),
     'L0_ffn_b2': (0.0, 0.1),
     'L1_xattn_b_q': (0.0, 0.8),
     'L1_xattn_b_k': (0.0, 0.8),
     'L1_xattn_b_v': (0.0, 0.1),
     'L1_xattn_b_o': (0.0, 0.1),
     'L1_ffn_ln1_w': (1.0, 0.6),
     'L1_ffn_ln2_w': (1.0, 0.6)}
    factors = {'L0_attn_w_attn': 2.856,
     'L1_attn_b_qkv': 6.754,
     'L1_attn_b_out': 8.0,
     'L1_ffn_wq': 8.0,
     'L1_ffn_wk': 8.0,
     'L1_ffn_wv': 2.931,
     'L1_ffn_wo': 2.955,
     'L1_ffn_gate_w': 8.0,
     'L1_ffn_w1': 8.0,
     'L1_ffn_w2': 8.0,
     'L1_ffn_w3': 8.0}
    for name, (base, spread) in spreads.items():
        noise = np.random.default_rng([zlib.crc32(name.encode()), seed]).standard_normal(out[name].shape)
        drawn = base * np.exp(spread * noise) if base else spread * noise
        out[name] = jnp.asarray(drawn.astype(out[name].dtype))
    for name, factor in factors.items():
        out[name] = (out[name] * factor).astype(out[name].dtype)
    return out
```

```python
import numpy as np
import concourse.bass as bass
from concourse import mybir
from contextlib import ExitStack

F32 = mybir.dt.float32
BF16 = mybir.dt.bfloat16
I32 = mybir.dt.int32
ALU = mybir.AluOpType
ACT = mybir.ActivationFunctionType
AX = mybir.AxisListType

B, S, D = 2, 1024, 256
T = B * S
P = 128
NT = T // P
KD = D // P
C = 256
NC = T // C
CT = C // P
SC = 77
HEADS = 16
E = 8
R = 256
NEG = -1.0e30
MASKED = -4.0e9
EPS = 1e-5


def two_halves(eng, n, step):
    step((0, 0, 0), None)
    step((1, 1, 0), (0, 0, 0))
    with eng.Fori(0, n // 2 - 1) as i:
        step((2 * i + 2, 0, i + 1), (2 * i + 1, 1, i))
        step((2 * i + 3, 1, i + 1), (2 * i + 2, 0, i + 1))
    step(None, (n - 1, 1, n // 2 - 1))


def wait(eng, sem, value):
    if not isinstance(value, int) or value > 0:
        eng.wait_ge(sem, value)


class Stage:

    def __init__(self, nc, name):
        self.nc, self.name, self.ctx, self.sems = nc, name, ExitStack(), []

    def __enter__(self):
        return self

    def __exit__(self, *_):
        if self.sems:
            self.nc.clear_and_free_semaphores(self.sems)
            self.nc.all_engine_barrier()
        self.ctx.close()

    def sb(self, name, shape, dt=F32):
        return self.ctx.enter_context(self.nc.sbuf_tensor(f"{self.name}_{name}", shape, dt))

    def ps(self, name, shape, dt=F32):
        return self.ctx.enter_context(self.nc.psum_tensor(f"{self.name}_{name}", shape, dt))

    def sem(self, name):
        self.sems.append(self.nc.alloc_semaphore(name=f"{self.name}_{name}"))
        return self.sems[-1]

    def block(self):
        return self.nc.Block()



def setup_stage(nc, G, x):
    with Stage(nc, "init") as st:
        filled, shaped, loaded, done = st.sem("filled"), st.sem("shaped"), st.sem("loaded"), st.sem("done")
        mS = st.sb("maskS", [P, P])
        mT = st.sb("maskT", [P, P])
        with st.block() as block:
            @block.sync
            def _(sp):
                sp.dma_start(G["X"][:], x.rearrange("(t p) d -> p t d", p=P)).then_inc(loaded, 16)
                sp.wait_ge(loaded, 16)

            @block.gpsimd
            def _(pool):
                for t in (G["ident"], mS, mT, G["sel16"], G["sel64"]):
                    pool.memset(t[:], 0.0).then_inc(filled, 1)
                pool.memset(G["eps"][:], EPS)
                pool.memset(G["lower"][:], 1.0).then_inc(filled, 1)
                pool.memset(G["ones"][:], 1.0)
                pool.wait_ge(filled, 6)

                def select(t, view, pattern, base, mult, op, fill):
                    pool.affine_select(out=view, in_=view, compare_op=op, fill=fill, base=base,
                                       pattern=pattern, channel_multiplier=mult).then_inc(shaped, 1)

                select(None, G["ident"][:], [[-1, P]], 0, 1, ALU.not_equal, 1.0)
                select(None, mS[:], [[-1, P]], 0, 1, ALU.is_ge, NEG)
                select(None, mT[:], [[1, P]], 0, -1, ALU.is_ge, NEG)
                select(None, G["sel16"][:].rearrange("p (a r) -> p a r", r=32), [[-32, 4], [0, 32]], -16, 1,
                       ALU.not_equal, 1.0)
                select(None, G["sel64"][:], [[0, 64]], -64, 1, ALU.not_equal, 1.0)
                select(None, G["lower"][:], [[1, P]], 0, -1, ALU.is_gt, 0.0)

            @block.vector
            def _(dve):
                dve.wait_ge(shaped, 6)
                dve.tensor_copy(G["identb"][:], G["ident"][:])
                dve.tensor_copy(G["maskS"][:], mS[:])
                dve.tensor_copy(G["maskT"][:], mT[:]).then_inc(done, 1)



def token_stage(nc, G, tag, *, norm, attn=None, resid=None, units=(), rope=False, split=0, wide=False,
                wf=None, bf=None, fscale=None, wv=None, bv=None, heads_group=4, hd=16, outs=None, gate=None,
                ln2=None):
    kf = attn[0].shape[0] // P if attn else 0
    n_units = len(units)
    n_rot = n_units if rope else 0
    v_cols = wv.shape[1] if wv is not None else 0
    v_parts = max(1, v_cols // 512)
    n_rows_units = CT * v_parts if wv is not None else (CT if gate is not None else 0)
    NU = n_units + n_rot + n_rows_units
    SETS = [list(range(s, min(s + 4, n_units))) for s in range(0, n_units, 4)]
    NS = len(SETS)
    USET = len(SETS[0]) if SETS else 0
    RP = 4 if NU >= 4 else 2
    assert 2 * NU % RP == 0 and (NS <= 1 or NS % 2 == 0)
    passes = 1 if norm in ("ln", "rms") else 2
    dve_frees = [u >= n_units + n_rot or rope for u in range(NU)]

    with Stage(nc, tag) as st:
        if attn:
            ot = [st.sb(f"attnT{p}", [P, kf, C]) for p in range(2)]
            wo = st.sb("wo", [P, kf, D])
            bo = st.sb("bo", [P, CT, D])
        nf = wf.shape[1] if wf is not None else 0
        wfs = st.sb("wf", [P, KD, nf]) if nf else None
        bfs = st.sb("bf", [P, nf // P]) if bf is not None else None
        fsc = st.sb("fscale", [P, KD]) if fscale is not None else None
        wvs = st.sb("wv", [P, KD, v_cols]) if wv is not None else None
        bvs = st.sb("bv", [P, v_cols]) if bv is not None else None
        wg = st.sb("wg", [P, KD, E]) if gate is not None else None
        ln2s = st.sb("ln2", [P, CT, D]) if ln2 is not None else None
        if rope:
            cos = st.sb("cos", [P, T])
            sin = st.sb("sin", [P, T])
            t1 = st.sb("t1", [P, 4, C])
            t2 = st.sb("t2", [P, 4, C])
        xn = [st.sb(f"xn{p}", [P, CT, D]) for p in range(2)]
        xT = [st.sb(f"xT{p}", [P, KD, C]) for p in range(2)]
        stats = st.sb("stats", [P, CT, 6])
        mv = st.sb("mv", [P, CT, 2])
        ms = st.sb("ms", [P, CT, 2])
        sd = st.sb("sd", [P, CT, 1])
        rs = st.sb("rs", [P, CT, 1])
        if NS:
            fo = [st.sb(f"f{p}", [P, USET, C]) for p in range(2)]
            rr = [st.sb(f"r{p}", [P, USET, C]) for p in range(2)]
            parts = [st.sb(f"parts{p}", [P, USET, 3, C], BF16) for p in range(2)]
        HPG = v_cols // hd if wv is not None else 0
        if HPG:
            vst = [st.sb(f"v{p}", [P, CT, HPG, hd + 1]) for p in range(2)]
        psY = [st.ps(f"psY{p}", [P, CT, D]) for p in range(2)]
        psX = [st.ps(f"psX{p}", [P, CT, KD, P]) for p in range(2)]
        psP = [st.ps(f"psP{p}", [P, 512]) for p in range(RP)]

        w_ld, o_ld = st.sem("weights_loaded"), [st.sem(f"attn_loaded{p}") for p in range(2)]
        y_ready, y_free = st.sem("y_ready"), st.sem("y_free")
        var_ready, sd_ready = st.sem("var_ready"), st.sem("sd_ready")
        xn_ready, turned, xT_ready = st.sem("xn_ready"), st.sem("turned"), st.sem("xT_ready")
        pu_ready, act_free, dve_free = st.sem("proj_ready"), st.sem("proj_free_act"), st.sem("proj_free_dve")
        f_ready, h_ready, r_ready, m_ready = st.sem("f_ready"), st.sem("h_ready"), st.sem("r_ready"), st.sem("m_ready")
        parts_ready = st.sem("parts_ready")
        f_out = [st.sem(f"f_stored{p}") for p in range(2)]
        v_out = [st.sem(f"v_stored{p}") for p in range(2)]
        kept = st.sem("kept")

        loads = []
        if attn:
            loads += [(wo[:], attn[1].rearrange("(k p) n -> p k n", p=P))]
            if attn[2] is not None:
                loads += [(bo[:, t, :], attn[2].partition_broadcast(P)) for t in range(CT)]
        if nf:
            loads += [(wfs[:], wf.rearrange("(k p) n -> p k n", p=P))]
        if bf is not None:
            loads += [(bfs[:], bf)]
        if fscale is not None:
            loads += [(fsc[:], fscale)]
        if wv is not None:
            loads += [(wvs[:], wv.rearrange("(k p) n -> p k n", p=P))]
        if bv is not None:
            loads += [(bvs[:], bv.partition_broadcast(P))]
        if gate is not None:
            loads += [(wg[:], gate.rearrange("(k p) n -> p k n", p=P))]
        if ln2 is not None:
            loads += [(ln2s[:, t, :], ln2.partition_broadcast(P)) for t in range(CT)]
        if rope:
            loads += [(cos[:], G["cos"]), (sin[:], G["sin"])]
        n_loads = 16 * len(loads)

        def set_buffer(piece, s):
            c, p, r = piece
            return (p, r) if NS == 1 else (s % 2, c * (NS // 2) + s // 2)

        def stores(piece, s):
            c, p, r = piece
            b = set_buffer(piece, s)[0]
            for i, u in enumerate(SETS[s]):
                for dst, lo, hi in units[u]["parts"]:
                    yield dst[:, :, bass.ds(c * C, C)].rearrange("a p t -> p a t"), parts[b][:, i, lo:hi, :]
                if wide:
                    yield units[u]["f32"][:, bass.ds(c * C, C)], fo[b][:, i, :]

        n_store = [16 * sum(len(units[u]["parts"]) + wide for u in us) for us in SETS]
        store_per_use = n_store[0] if SETS else 0
        assert all(n == store_per_use for n in n_store)

        def store(eng, piece):
            c, p, r = piece
            for s in range(NS):
                b = set_buffer(piece, s)[0]
                eng.wait_ge({1: h_ready, 2: m_ready, 3: parts_ready}[split], c * NS + s + 1)
                for dst, src in stores(piece, s):
                    eng.dma_start(dst, src).then_inc(f_out[b], 16)
            if wv is not None:
                eng.wait_ge(dve_free, (c + 1) * sum(dve_frees))
                for t in range(CT):
                    eng.dma_start(outs[:, :, bass.ds(c * CT + t, 1), :].rearrange("g p t x -> p g (t x)"),
                                  vst[p][:, t].rearrange("p (g h) x -> p g (h x)", h=heads_group)
                                  ).then_inc(v_out[p], 16)

        def all_stored(eng):
            for p in range(2):
                if NS:
                    eng.wait_ge(f_out[p], (NC // 2 if NS == 1 else NC * NS // 2) * store_per_use)
                if wv is not None:
                    eng.wait_ge(v_out[p], NC // 2 * 16 * CT)

        with st.block() as block:
            @block.sync
            def _(sp):
                for dst, src in loads:
                    sp.dma_start(dst, src).then_inc(w_ld, 16)

                def step(front, back):
                    if front and attn:
                        c, p, r = front
                        wait(sp, y_ready, c - 1)
                        sp.dma_start(ot[p][:], attn[0][:, bass.ds(c * C, C)].rearrange("(k p) t -> p k t", p=P)
                                     ).then_inc(o_ld[p], 16)
                    if back and wide:
                        store(sp, back)

                two_halves(sp, NC, step)
                if wide:
                    all_stored(sp)
                sp.wait_ge(w_ld, n_loads)

            @block.gpsimd
            def _(pool):
                if outs is None and not NS or wide:
                    return
                two_halves(pool, NC, lambda front, back: store(pool, back) if back else None)
                all_stored(pool)

            @block.tensor
            def _(pe):
                def freed(piece, u):
                    c, p, r = piece
                    if u < 0:
                        c, u = c - 1, u + NU
                    same = dve_frees[u]
                    count = c * dve_frees.count(same) + dve_frees[:u + 1].count(same)
                    return (dve_free if same else act_free), count

                def step(front, back):
                    if front and attn:
                        c, p, r = front
                        if isinstance(c, int) and c == 0:
                            pe.wait_ge(w_ld, n_loads)
                        pe.wait_ge(o_ld[p], 16 * (r + 1))
                        wait(pe, y_free, c - 1)
                        for t in range(CT):
                            for k in range(kf):
                                mm = pe.matmul(psY[p][:, t, :], ot[p][:, k, t * P:(t + 1) * P], wo[:, k, :],
                                               start=(k == 0), stop=(k == kf - 1))
                        mm.then_inc(y_ready, 1)
                    if back:
                        c, p, r = back
                        if isinstance(c, int) and c == 0:
                            pe.wait_ge(w_ld, n_loads)
                        pe.wait_ge(xT_ready, c + 1)
                        jobs = []
                        for u in range(n_units):
                            jobs.append(("f", u))
                            if rope:
                                jobs.append(("f", n_units + u))
                        for t in range(CT):
                            for v in range(v_parts):
                                jobs.append(("v", t, v))
                        for n, job in enumerate(jobs[:NU]):
                            slot = (p * NU + n) % RP
                            if not (isinstance(c, int) and c == 0 and n < RP):
                                pe.wait_ge(*freed(back, n - RP))
                            for k in range(KD):
                                if job[0] == "f":
                                    m = job[1]
                                    mm = pe.matmul(psP[slot][:, 0:C], wfs[:, k, m * P:(m + 1) * P], xT[p][:, k, :],
                                                   start=(k == 0), stop=(k == KD - 1))
                                elif wv is not None:
                                    w = min(512, v_cols)
                                    _, t, v = job
                                    mm = pe.matmul(psP[slot][:, 0:w], xT[p][:, k, t * P:(t + 1) * P],
                                                   wvs[:, k, v * w:(v + 1) * w], start=(k == 0), stop=(k == KD - 1))
                                else:
                                    t = job[1]
                                    mm = pe.matmul(psP[slot][:, 0:E], xT[p][:, k, t * P:(t + 1) * P], wg[:, k, :],
                                                   start=(k == 0), stop=(k == KD - 1))
                            mm.then_inc(pu_ready, 1)
                    if front:
                        c, p, r = front
                        pe.wait_ge(xn_ready, c + 1)
                        wait(pe, xT_ready, c - 1)
                        for t in range(CT):
                            for k in range(KD):
                                mm = pe.transpose(psX[p][:, t, k, :], xn[p][:, t, k * P:(k + 1) * P], G["ident"][:])
                        mm.then_inc(turned, 1)

                two_halves(pe, NC, step)

            @block.scalar
            def _(act):
                def step(front, back):
                    if front:
                        c, p, r = front
                        for q in range(passes):
                            act.wait_ge(var_ready, c * passes + q + 1)
                            src = mv[:, :, 1:2] if not (norm == "rms" or (norm == "ln_rms" and q)) else ms[:, :, 1:2]
                            act.activation(sd[:], src, ACT.Sqrt, bias=G["eps"][:]).then_inc(sd_ready, 1)
                    if back:
                        c, p, r = back
                        if isinstance(c, int) and c == 0:
                            act.wait_ge(w_ld, n_loads)
                        for s in range(NS):
                            b, uses = set_buffer(back, s)
                            us = SETS[s]
                            if not rope:
                                wait(act, f_out[b], uses * store_per_use)
                                for i, u in enumerate(us):
                                    act.wait_ge(pu_ready, c * NU + u + 1)
                                    slot = (p * NU + u) % RP
                                    bias = bfs[:, u:u + 1] if bf is not None else 0.0
                                    act.activation(fo[b][:, i, :], psP[slot][:, 0:C], ACT.Identity if bf is not None
                                                   else ACT.Copy, bias=bias).then_inc(act_free, 1)
                                act.drain()
                            else:
                                act.wait_ge(f_ready, c * NS + s + 1)
                                wait(act, f_out[b], uses * store_per_use)
                            act.activation(parts[b][:, :, 0, :], fo[b][:], ACT.Copy).then_inc(h_ready, 1)
                            if split >= 2:
                                act.wait_ge(r_ready, c * NS + s + 1)
                                act.activation(parts[b][:, :, 1, :], rr[b][:], ACT.Copy).then_inc(m_ready, 1)
                    if front:
                        c, p, r = front
                        act.wait_ge(turned, c + 1)
                        wait(act, pu_ready, (c - 1) * NU)
                        if fscale is None:
                            act.activation(xT[p][:].rearrange("p k (t q) -> p t k q", q=P), psX[p][:], ACT.Copy
                                           ).then_inc(xT_ready, 1)
                        else:
                            act.activation(xT[p][:, 0, :].rearrange("p (t q) -> p t q", q=P), psX[p][:, :, 0, :],
                                           ACT.Copy, scale=fsc[:, 0:1])
                            act.activation(xT[p][:, 1, :].rearrange("p (t q) -> p t q", q=P), psX[p][:, :, 1, :],
                                           ACT.Copy, scale=fsc[:, 1:2]).then_inc(xT_ready, 1)

                two_halves(act, NC, step)

            @block.vector
            def _(dve):
                if HPG:
                    for p in range(2):
                        dve.memset(vst[p][:, :, :, hd:hd + 1], 1.0)
                dve.wait_ge(w_ld, n_loads)
                dve.drain()

                def moments(src, c, q, rms):
                    for t in range(CT):
                        dve.bn_stats(stats[:, t, :], src(t))
                    dve.drain()
                    for t in range(CT):
                        ins = dve.bn_aggr(mv[:, t, :], stats[:, t, :])
                    if rms:
                        dve.drain()
                        dve.tensor_tensor(ms[:, :, 0:1], mv[:, :, 0:1], mv[:, :, 0:1], ALU.mult)
                        dve.drain()
                        ins = dve.tensor_tensor(ms[:, :, 1:2], ms[:, :, 0:1], mv[:, :, 1:2], ALU.add)
                    ins.then_inc(var_ready, 1)
                    dve.wait_ge(sd_ready, c * passes + q + 1)
                    dve.reciprocal(rs[:], sd[:])
                    dve.drain()

                def step(front, back):
                    if front:
                        c, p, r = front
                        rows = resid[:, bass.ds(c * CT, CT), :]
                        row = lambda t: resid[:, bass.ds(c * CT + t, 1), :].rearrange("p t d -> p (t d)")
                        if attn:
                            dve.wait_ge(y_ready, c + 1)
                            dve.tensor_tensor(rows, psY[p][:], rows, ALU.add).then_inc(y_free, 1)
                            if attn[2] is not None:
                                dve.drain()
                                dve.tensor_tensor(rows, rows, bo[:], ALU.add)
                            dve.drain()
                        keep = None
                        moments(row, c, 0, norm == "rms")
                        wait(dve, turned, c - 1)
                        for t in range(CT):
                            if norm == "rms":
                                ins = dve.tensor_scalar(xn[p][:, t, :], row(t), rs[:, t, :], None, ALU.mult)
                            else:
                                ins = dve.tensor_scalar(xn[p][:, t, :], row(t), mv[:, t, 0:1], rs[:, t, :],
                                                        ALU.subtract, ALU.mult)
                        if norm == "ln":
                            ins.then_inc(xn_ready, 1)
                        elif norm == "rms":
                            dve.drain()
                            dve.tensor_tensor(xn[p][:], xn[p][:], ln2s[:], ALU.mult).then_inc(xn_ready, 1)
                            dve.drain()
                            dve.tensor_copy(G["Z"][:, bass.ds(c * CT, CT), :], xn[p][:])
                        elif norm == "ln_ln":
                            ins.then_inc(xn_ready, 1)
                            dve.drain()
                            dve.tensor_copy(G["Y"][:, bass.ds(c * CT, CT), :], xn[p][:])
                            moments(lambda t: xn[p][:, t, :], c, 1, False)
                            for t in range(CT):
                                dve.tensor_scalar(G["Z"][:, bass.ds(c * CT + t, 1), :], xn[p][:, t:t + 1, :],
                                                  mv[:, t, 0:1], rs[:, t, :], ALU.subtract, ALU.mult)
                        elif norm == "ln_rms":
                            dve.drain()
                            dve.tensor_copy(G["Y"][:, bass.ds(c * CT, CT), :], xn[p][:])
                            moments(lambda t: xn[p][:, t, :], c, 1, True)
                            for t in range(CT):
                                ins = dve.tensor_scalar(xn[p][:, t, :], xn[p][:, t, :], rs[:, t, :], None, ALU.mult)
                            ins.then_inc(xn_ready, 1)
                        dve.drain()
                    if back:
                        c, p, r = back
                        for s in range(NS):
                            b, uses = set_buffer(back, s)
                            if rope:
                                for i, u in enumerate(SETS[s]):
                                    for k, (tt, tab) in enumerate(((t1, cos), (t2, sin))):
                                        n = 2 * u + k
                                        dve.wait_ge(pu_ready, c * NU + n + 1)
                                        slot = (p * NU + n) % RP
                                        m = u + k * n_units
                                        dve.scalar_tensor_tensor(tt[:, i, :], psP[slot][:, 0:C], bfs[:, m:m + 1],
                                                                 tab[:, bass.ds(c * C, C)], ALU.add, ALU.mult
                                                                 ).then_inc(dve_free, 1)
                                dve.drain()
                                wait(dve, h_ready, c - 1)
                                dve.tensor_tensor(fo[b][:], t1[:], t2[:], ALU.add).then_inc(f_ready, 1)
                            dve.wait_ge(h_ready, c * NS + s + 1)
                            if split >= 2:
                                dve.tensor_tensor(rr[b][:], fo[b][:], parts[b][:, :, 0, :], ALU.subtract
                                                  ).then_inc(r_ready, 1)
                                dve.wait_ge(m_ready, c * NS + s + 1)
                            if split == 3:
                                dve.tensor_tensor(parts[b][:, :, 2, :], rr[b][:], parts[b][:, :, 1, :],
                                                        ALU.subtract).then_inc(parts_ready, 1)
                        if wv is not None:
                            wait(dve, v_out[p], r * 16 * CT)
                        if n_rows_units:
                            for t in range(CT):
                                for v in range(v_parts):
                                    n = n_units + n_rot + t * v_parts + v
                                    dve.wait_ge(pu_ready, c * NU + n + 1)
                                    slot = (p * NU + n) % RP
                                    if wv is not None:
                                        w = min(512, v_cols)
                                        hp = w // hd
                                        out = vst[p][:, t, v * hp:(v + 1) * hp, 0:hd]
                                        src = psP[slot][:, 0:w].rearrange("p (h r) -> p h r", r=hd)
                                        if bv is not None:
                                            dve.tensor_tensor(out, src, bvs[:, v * w:(v + 1) * w].rearrange(
                                                "p (h r) -> p h r", r=hd), ALU.add).then_inc(dve_free, 1)
                                        else:
                                            dve.tensor_copy(out, src).then_inc(dve_free, 1)
                                    else:
                                        dve.tensor_copy(G["logits"][:, bass.ds(c * CT + t, 1), :],
                                                        psP[slot][:, 0:E].rearrange("p (a e) -> p a e", a=1)
                                                        ).then_inc(dve_free, 1)
                        dve.drain()

                two_halves(dve, NC, step)



def context_stage(nc, G, tag, ctxT, wk, bk, wv, bv, mask, k_out, v_out, mask_out):
    W = B * SC
    with Stage(nc, tag) as st:
        cT, wks, wvs = st.sb("ctxT", [P, KD, W]), st.sb("wk", [P, KD, D]), st.sb("wv", [P, KD, D])
        bks, bvs = st.sb("bk", [P, KD]), st.sb("bv", [SC, D])
        f, r = st.sb("f", [P, KD, W]), st.sb("r", [P, KD, W])
        parts = st.sb("parts", [P, KD, 3, W], BF16)
        v = st.sb("v", [SC, B, HEADS, 17])
        psK = [st.ps(f"psK{m}", [P, 512]) for m in range(KD)]
        psV = [st.ps(f"psV{b}", [P, 512]) for b in range(B)]
        loaded, ready, stored, done = st.sem("loaded"), st.sem("ready"), st.sem("stored"), st.sem("done")
        n = 6
        if mask is not None:
            mi, mf = st.sb("mi", [P, W], I32), st.sb("mf", [P, W])
            mb = st.sb("mb", [1, B, 4, SC], BF16)
            n += 1
        with st.block() as block:
            @block.sync
            def _(sp):
                sp.dma_start(cT[:], ctxT.rearrange("(k p) t -> p k t", p=P)).then_inc(loaded, 16)
                sp.dma_start(wks[:], wk.rearrange("(k p) n -> p k n", p=P)).then_inc(loaded, 16)
                sp.dma_start(wvs[:], wv.rearrange("(k p) n -> p k n", p=P)).then_inc(loaded, 16)
                sp.dma_start(bks[:], bk).then_inc(loaded, 16)
                sp.dma_start(bvs[:], bv.partition_broadcast(SC)).then_inc(loaded, 16)
                if mask is not None:
                    sp.dma_start(mi[:], mask.rearrange("b a s -> (b a s)").partition_broadcast(P)).then_inc(loaded, 16)
                sp.wait_ge(done, 1)
                for m in range(KD):
                    sp.dma_start(k_out[:, m * P:(m + 1) * P, :].rearrange("a p t -> p a t"), parts[:, m]
                                 ).then_inc(stored, 16)
                for b in range(B):
                    sp.dma_start(v_out[:, :, b, :].rearrange("g p x -> p g x"),
                                 v[:, b].rearrange("p (g h) x -> p g (h x)", h=4)).then_inc(stored, 16)
                if mask is not None:
                    sp.dma_start(mask_out.rearrange("(a b) h s -> a b h s", a=1), mb[:]).then_inc(stored, 16)
                sp.wait_ge(stored, 16 * (KD + B + (mask is not None)))

            @block.tensor
            def _(pe):
                pe.wait_ge(loaded, 16 * (n - 1))
                for m in range(KD):
                    for k in range(KD):
                        pe.matmul(psK[m][:, 0:W], wks[:, k, m * P:(m + 1) * P], cT[:, k, :], start=(k == 0),
                                  stop=(k == KD - 1))
                for b in range(B):
                    for k in range(KD):
                        mm = pe.matmul(psV[b][0:SC, 0:D], cT[:, k, b * SC:(b + 1) * SC], wvs[:, k, :],
                                       start=(k == 0), stop=(k == KD - 1))
                mm.then_inc(ready, 1)

            @block.vector
            def _(dve):
                dve.memset(v[:, :, :, 16:17], 1.0)
                dve.wait_ge(loaded, 16 * (n - 1))
                if mask is not None:
                    dve.tensor_scalar(mf[:], mi[:], 0.0, None, ALU.not_equal)
                    dve.drain()
                    for b in range(B):
                        for h in range(4):
                            dve.tensor_scalar(mb[:, b, h, :], mf[0:1, b * SC:(b + 1) * SC], -MASKED, MASKED,
                                              ALU.mult, ALU.add)
                dve.wait_ge(ready, 1)
                for m in range(KD):
                    dve.tensor_scalar(f[:, m, :], psK[m][:, 0:W], bks[:, m:m + 1], None, ALU.add)
                    if mask is not None:
                        dve.drain()
                        dve.tensor_tensor(f[:, m, :], f[:, m, :], mf[:], ALU.mult)
                dve.drain()
                dve.tensor_copy(parts[:, :, 0, :], f[:])
                dve.drain()
                dve.tensor_tensor(r[:], f[:], parts[:, :, 0, :], ALU.subtract)
                dve.drain()
                dve.tensor_copy(parts[:, :, 1, :], r[:])
                dve.drain()
                dve.tensor_tensor(parts[:, :, 2, :], r[:], parts[:, :, 1, :], ALU.subtract)
                for b in range(B):
                    ins = dve.tensor_tensor(v[:, b, :, 0:16], psV[b][0:SC, 0:D].rearrange("p (h r) -> p h r", r=16),
                                            bvs[:].rearrange("p (h r) -> p h r", r=16), ALU.add)
                dve.drain()
                dve.memset(G["tick"][:], 0.0).then_inc(done, 1)



Q_PARTS = (0, 0, 1, 1, 0, 2)
K_PARTS = (0, 1, 0, 1, 2, 0)


def attention_stage(nc, G, tag, *, q, k, v, o, wide=False, causal=False, cross=False, mask=None):
    H = 1 if wide else 4
    hd = 64 if wide else 16
    n_groups = (HEADS // H) * B
    KT = [(0, SC)] if cross else [(i * P, P) for i in range(S // P)]
    NK = SC if cross else S
    QT = S // P
    scale = float(hd) ** -0.5
    base = len(Q_PARTS) * 16
    K1 = P if wide else base + (mask is not None)
    K2 = 65 if wide else K1 + 3
    MR = 1 if wide else 3
    units1 = [(None, h) for h in range(H)] if cross else [(t, h) for t in range(QT) for h in range(H)]
    NS = len(units1)
    ugs = [(qh, i, max(0, k0 - 512 * qh) if causal else 0) for qh in range(2) for i, (k0, _) in enumerate(KT)
           if not causal or k0 < 512 * (qh + 1)]
    NUG, NST = len(ugs), len(ugs) * H
    RING = 3 if H == 4 else 4
    VC = H * (hd + 1)
    VT = 1 if cross else QT
    OM = 65 if wide else P
    NM = 64 if wide else P
    dst_dt = F32 if wide else BF16

    with Stage(nc, tag) as st:
        qs = [st.sb(f"qs{p}", [P, H, S], BF16) for p in range(2)]
        ks = [st.sb(f"ks{p}", [P, H, NK], BF16) for p in range(2)]
        if wide:
            qf = [st.sb(f"qf{p}", [65, 1, S]) for p in range(2)]
            kf = [st.sb(f"kf{p}", [65, 1, S]) for p in range(2)]
        vs = [st.sb(f"vs{p}", [P, VT, H, hd + 1]) for p in range(2)]
        pr = [st.sb(f"probs{r}", [P, H, 512]) for r in range(RING)]
        osb = st.sb("osb", [P, S])
        rec = st.sb("rec", [P, S])
        on = [st.sb(f"on{p}", [P, S]) for p in range(2)]
        mx = st.sb("mx", [P, H * QT])
        neg = [st.sb(f"neg{p}", [H * QT, P]) for p in range(2)]
        nres = st.sb("nres", [H * QT, P])
        nparts = [st.sb(f"nparts{p}", [H * QT, 3, P], BF16) for p in range(2)]
        ps1 = [st.ps(f"rows{p}", [P, S]) for p in range(2)]
        ps2 = [st.ps(f"cols{p}", [P, 512]) for p in range(2)]
        psO = st.ps("out", [P, S])
        ld = [st.sem(f"loaded{p}") for p in range(2)]
        mld = [st.sem(f"max_placed{p}") for p in range(2)]
        ones_set = st.sem("ones_set")
        s_ready, s_free = st.sem("rows_ready"), st.sem("rows_free")
        mt_ready, mt_done, neg_ready = st.sem("max_turned"), st.sem("max_read"), st.sem("neg_ready")
        st_ready, ex_done, pv_done = st.sem("cols_ready"), st.sem("exp_done"), st.sem("pv_done")
        o_copied, lb_ready, lb_done, o_done = (st.sem("out_copied"), st.sem("sums_ready"), st.sem("sums_read"),
                                               st.sem("out_done"))
        stored = [st.sem(f"stored{p}") for p in range(2)]
        n_ld = 6 if wide else 13 + (mask is not None)
        n_st = 1 if wide else 4

        with st.block() as block:
            @block.sync
            def _(sp):
                sp.wait_ge(ones_set, 1)

                def load(p, hg):
                    t0 = p * S
                    if wide:
                        feats = bass.ds(hg * 64, 64)
                        yield qs[p][0:64, 0, :], q["parts"][0, feats, t0:t0 + S]
                        yield qs[p][64:128, 0, :], q["parts"][1, feats, t0:t0 + S]
                        yield ks[p][0:64, 0, :], k["parts"][0, feats, t0:t0 + S]
                        yield ks[p][64:128, 0, :], k["parts"][0, feats, t0:t0 + S]
                        yield qf[p][0:64, 0, :], q["f32"][feats, t0:t0 + S]
                        yield kf[p][0:64, 0, :], k["f32"][feats, t0:t0 + S]
                    else:
                        feats = bass.ds(hg * 64, 64)
                        for i in range(len(Q_PARTS)):
                            rows = slice(16 * i, 16 * i + 16)
                            yield (qs[p][rows, :, :],
                                   q["parts"][Q_PARTS[i], feats, t0:t0 + S].rearrange("(h r) t -> r h t", r=16))
                            yield (ks[p][rows, :, :],
                                   k["parts"][K_PARTS[i], feats, p * NK:p * NK + NK].rearrange("(h r) t -> r h t", r=16))
                        if mask is not None:
                            yield ks[p][base:base + 1, :, :], mask[p:p + 1, :, :]
                    if not wide and cross:
                        yield (vs[p][0:SC, 0].rearrange("p h x -> p (h x)"),
                               v[bass.ds(hg, 1), :, p, :].rearrange("g p x -> p (g x)"))
                    elif not wide:
                        yield (vs[p][:].rearrange("p t h x -> p (t h x)"),
                               v[bass.ds(hg, 1), :, p * QT:(p + 1) * QT, :].rearrange("g p t x -> p (g t x)"))

                def step(front, back):
                    if front:
                        g, p, r = front
                        wait(sp, lb_ready, g - 1)
                        for dst, src in load(p, r):
                            sp.dma_start(dst, src).then_inc(ld[p], 16)
                        if wide:
                            sp.dma_start(vs[p][:].rearrange("p t h x -> p (t h x)"),
                                         v[bass.ds(r, 1), :, p * QT:(p + 1) * QT, :].rearrange("g p t x -> p (g t x)")
                                         ).then_inc(ld[p], 16)
                        sp.wait_ge(neg_ready, g + 1)
                        for i in range(MR):
                            dst = qf[p][64:65, 0, :] if wide else qs[p][K1 + i:K1 + i + 1, :, :]
                            dst = (dst.rearrange("p (t q) -> p t q", q=P) if wide
                                   else dst.rearrange("p h (t q) -> p (h t) q", q=P))
                            sp.dma_start(dst, neg[p][:] if wide else nparts[p][:, i, :]).then_inc(mld[p], 16)

                two_halves(sp, n_groups, step)

            @block.gpsimd
            def _(pool):
                def step(front, back):
                    if back:
                        g, p, r = back
                        pool.wait_ge(o_done, g + 1)
                        for h in range(n_st):
                            pool.dma_start(o[bass.ds(r * 64 + h * 16, 64 if wide else 16), p * S:(p + 1) * S],
                                           on[p][0:64, :] if wide else on[p][32 * h:32 * h + 16, :]
                                           ).then_inc(stored[p], 16)

                two_halves(pool, n_groups, step)
                for p in range(2):
                    pool.wait_ge(stored[p], n_groups // 2 * n_st * 16)

            n_loaded = 16 * (7 if wide else n_ld)

            @block.tensor
            def _(pe):
                pe.wait_ge(ones_set, 1)

                def rows_unit(front, s):
                    g, p, r = front
                    t, h = units1[s]
                    dst = ps1[s % 2]
                    if s >= 2:
                        pe.wait_ge(s_free, g * NS + s - 1)
                    elif s == 1:
                        wait(pe, mt_done, g)
                    else:
                        wait(pe, lb_done, g - 1)
                    if cross:
                        for t in range(QT):
                            at = 512 * (t // 4) + SC * (t % 4)
                            mm = pe.matmul(dst[:, at:at + SC], qs[p][0:K1, h, t * P:(t + 1) * P], ks[p][0:K1, h, :],
                                           start=True, stop=True)
                    else:
                        n = (t + 1) * P if causal else S
                        for a in range(0, n, 512):
                            b = min(n, a + 512)
                            diag = causal and b == n
                            mm = pe.matmul(dst[:, a:b], qs[p][0:K1, h, t * P:(t + 1) * P], ks[p][0:K1, h, a:b],
                                           start=True, stop=not diag)
                            if diag:
                                mm = pe.matmul(dst[:, n - P:n], G["identb"][:], G["maskS"][:], start=False, stop=True)
                    mm.then_inc(s_ready, 1)

                def cols_unit(back, u):
                    g, p, r = back
                    qh, i, c0 = ugs[u // H]
                    h = u % H
                    k0, rows = KT[i]
                    dst = ps2[u % 2]
                    if u >= 2:
                        pe.wait_ge(ex_done, g * NST + u - 1)
                    kk, qq = (kf[p], qf[p]) if wide else (ks[p], qs[p])
                    diag = causal and k0 >= 512 * qh
                    mm = pe.matmul(dst[0:rows, 0:512 - c0], kk[0:K2, h, k0:k0 + rows],
                                   qq[0:K2, h, 512 * qh + c0:512 * (qh + 1)], start=True, stop=not diag)
                    if diag:
                        mm = pe.matmul(dst[:, 0:P], G["identb"][:], G["maskT"][:], start=False, stop=True)
                    mm.then_inc(st_ready, 1)

                def values_unit(back, ug):
                    g, p, r = back
                    qh, i, c0 = ugs[ug]
                    rows = KT[i][1]
                    last = ug + 1 == NUG or ugs[ug + 1][0] != qh
                    pe.wait_ge(ex_done, g * NST + (ug + 1) * H)
                    for h in range(H):
                        mm = pe.matmul(psO[32 * h:32 * h + hd + 1, 512 * qh + c0:512 * (qh + 1)],
                                       vs[p][0:rows, i, h, :], pr[ug % RING][0:rows, h, c0:512],
                                       start=(i == 0), stop=last)
                    mm.then_inc(pv_done, 1)

                def step(front, back):
                    if front:
                        pe.wait_ge(ld[front[1]], n_loaded * (front[2] + 1))
                    if back:
                        pe.wait_ge(mld[back[1]], 16 * MR * (back[2] + 1))
                    s = 0
                    for u in range(NST if back else 0):
                        cols_unit(back, u)
                        if u % H == H - 1 and u // H >= 1:
                            values_unit(back, u // H - 1)
                        due = NS * (u + 1) // (NST - NST // 8)
                        while front and s < min(NS, due):
                            rows_unit(front, s)
                            s += 1
                    while front and s < NS:
                        rows_unit(front, s)
                        s += 1
                    if back:
                        values_unit(back, NUG - 1)
                    if front:
                        g = front[0]
                        pe.wait_ge(s_free, (g + 1) * NS)
                        pe.transpose(ps1[1][0:H * QT, 0:P], mx[:], G["ident"][:]).then_inc(mt_ready, 1)
                    if back:
                        g = back[0]
                        pe.wait_ge(o_copied, g + 1)
                        for a in range(0, S, 512):
                            mm = pe.matmul(ps1[0][0:NM, a:a + 512], G["sel64"][0:OM, :] if wide else G["sel16"][:],
                                           osb[0:OM, a:a + 512], start=True, stop=True)
                        mm.then_inc(lb_ready, 1)

                two_halves(pe, n_groups, step)

            @block.scalar
            def _(act):
                def step(front, back):
                    if not back:
                        return
                    g, p, r = back
                    for u in range(NST):
                        ug, h = u // H, u % H
                        qh, i, c0 = ugs[ug]
                        rows = KT[i][1]
                        act.wait_ge(st_ready, g * NST + u + 1)
                        if h == 0 and ug >= RING:
                            act.wait_ge(pv_done, g * NUG + ug - RING + 1)
                        act.activation(pr[ug % RING][0:rows, h, c0:512], ps2[u % 2][0:rows, 0:512 - c0], ACT.Exp,
                                       scale=scale).then_inc(ex_done, 1)
                    act.wait_ge(pv_done, (g + 1) * NUG)
                    wait(act, o_done, g)
                    act.activation(osb[0:OM, :], psO[0:OM, :], ACT.Copy).then_inc(o_copied, 1)

                two_halves(act, n_groups, step)

            @block.vector
            def _(dve):
                for p in range(2):
                    if wide:
                        dve.memset(kf[p][64:65, :, :], 1.0)
                    else:
                        dve.memset(ks[p][base:K2, :, :], 1.0)
                        dve.memset(qs[p][base:K2, :, :], 1.0)
                dve.memset(psO[:], 0.0)
                dve.drain()
                dve.memset(G["tick"][:], 0.0).then_inc(ones_set, 1)

                def step(front, back):
                    if front:
                        g, p, r = front
                        for s, (t, h) in enumerate(units1):
                            dve.wait_ge(s_ready, g * NS + s + 1)
                            if cross:
                                view = ps1[s % 2][:].rearrange("p (a n) -> p a n", a=2)[:, :, 0:4 * SC]
                                dve.tensor_reduce(mx[:, h * QT:(h + 1) * QT].rearrange("p (a b) -> p a b", a=2),
                                                  view.rearrange("p a (b n) -> p a b n", b=4), AX.X,
                                                  ALU.max).then_inc(s_free, 1)
                            else:
                                n = (t + 1) * P if causal else S
                                dve.tensor_reduce(mx[:, h * QT + t:h * QT + t + 1], ps1[s % 2][:, 0:n], AX.X,
                                                  ALU.max).then_inc(s_free, 1)
                        wait(dve, mld[p], 16 * MR * r)
                        dve.wait_ge(mt_ready, g + 1)
                        ins = dve.tensor_scalar(neg[p][:], ps1[1][0:H * QT, 0:P], -1.0, None, ALU.mult)
                        ins.then_inc(mt_done, 1)
                        dve.drain()
                        if not wide:
                            dve.tensor_copy(nparts[p][:, 0, :], neg[p][:])
                            dve.drain()
                            dve.tensor_tensor(nres[:], neg[p][:], nparts[p][:, 0, :], ALU.subtract)
                            dve.drain()
                            dve.tensor_copy(nparts[p][:, 1, :], nres[:])
                            dve.drain()
                            dve.tensor_tensor(nparts[p][:, 2, :], nres[:], nparts[p][:, 1, :],
                                              ALU.subtract).then_inc(neg_ready, 1)
                        else:
                            dve.memset(G["tick"][:], 0.0).then_inc(neg_ready, 1)
                        dve.drain()
                    if back:
                        g, p, r = back
                        dve.wait_ge(lb_ready, g + 1)
                        dve.reciprocal(rec[0:NM, :], ps1[0][0:NM, :]).then_inc(lb_done, 1)
                        dve.drain()
                        wait(dve, stored[p], r * n_st * 16)
                        dve.tensor_tensor(on[p][0:NM, :], osb[0:NM, :], rec[0:NM, :], ALU.mult).then_inc(o_done, 1)
                        dve.drain()

                two_halves(dve, n_groups, step)



def n_pieces(K):
    n = K * T // R + E - 1
    return n + n % 2


def route_stage(nc, G, tag, K, rows, sorted_rows, table, place, weight):
    NJ = n_pieces(K)
    KN = K * NT
    with Stage(nc, tag) as st:
        lg = G["logits"]
        iota_i, iota = st.sb("iota_i", [P, NT, E], I32), st.sb("iota", [P, NT, E])
        start_i, starts = st.sb("start_i", [P, NJ], I32), st.sb("starts", [P, NJ])
        top = st.sb("top", [P, K, NT])
        eq, cand, l2 = st.sb("eq", [P, NT, E]), st.sb("cand", [P, NT, E]), st.sb("l2", [P, NT, E])
        first = st.sb("first", [P, NT])
        oh = st.sb("onehot", [P, KN, E])
        tot = [st.sb(f"tot{i}", [P, KN, E]) for i in range(2)]
        count, count_i = st.sb("count", [P, E]), st.sb("count_i", [P, E], I32)
        basee = st.sb("base", [P, E])
        pos = st.sb("pos", [P, KN, E])
        posr = st.sb("posr", [P, KN])
        ex, owner = st.sb("ex", [P, NT]), st.sb("owner", [P, NJ])
        ge = st.sb("ge", [P, NJ])
        zero = st.sb("zero", [P, 2, D])
        psB, psT_ = st.ps("before", [P, KN * E]), st.ps("totals", [P, KN * E])
        iotas, oh_ready, counted = st.sem("iotas"), st.sem("oh_ready"), st.sem("counted")
        exp_in, exp_out = st.sem("exp_in"), st.sem("exp_out")
        zeroed, cleared, placed, sent = st.sem("zeroed"), st.sem("cleared"), st.sem("placed"), st.sem("sent")

        with st.block() as block:
            @block.gpsimd
            def _(pool):
                pool.iota(iota_i[:], pattern=[[0, NT], [1, E]], base=0, channel_multiplier=0)
                pool.iota(start_i[:], pattern=[[R, NJ]], base=0, channel_multiplier=0).then_inc(iotas, 1)
                pool.wait_ge(placed, 1)
                pool.wait_ge(cleared, NJ * 16)
                for k in range(K):
                    for t in range(NT):
                        pool.indirect_dma_start(
                            sorted_rows, bass.IndirectOffsetOnAxis(ap=place[:, k * NT + t:k * NT + t + 1], axis=0),
                            rows[:, t, :], None).then_inc(sent, 16)
                pool.wait_ge(sent, K * NT * 16)

            @block.sync
            def _(sp):
                sp.wait_ge(zeroed, 1)
                for j in range(NJ):
                    sp.dma_start(sorted_rows[j * R:(j + 1) * R, :].rearrange("(t p) d -> p t d", p=P), zero[:]
                                 ).then_inc(cleared, 16)
                sp.wait_ge(cleared, NJ * 16)

            @block.tensor
            def _(pe):
                pe.wait_ge(oh_ready, 1)
                flat = oh[:].rearrange("p s e -> p (s e)")
                pe.matmul(psB[:], G["lower"][:], flat, start=True, stop=True)
                pe.matmul(psT_[:], G["ones"][:], flat, start=True, stop=True).then_inc(counted, 1)

            @block.scalar
            def _(act):
                act.wait_ge(exp_in, 1)
                act.activation(ex[:], first[:], ACT.Exp).then_inc(exp_out, 1)

            @block.vector
            def _(dve):
                def op(ins):
                    dve.drain()

                op(dve.memset(zero[:], 0.0))
                dve.memset(G["tick"][:], 0.0).then_inc(zeroed, 1)
                dve.wait_ge(iotas, 1)
                op(dve.tensor_copy(iota[:], iota_i[:]))
                op(dve.tensor_copy(starts[:], start_i[:]))
                op(dve.tensor_copy(l2[:], lg[:]))
                for k in range(K):
                    sel = oh[:, k * NT:(k + 1) * NT, :]
                    op(dve.tensor_reduce(top[:, k, :], l2[:], AX.X, ALU.max))
                    op(dve.tensor_tensor(eq[:], l2[:], top[:, k, :].unsqueeze(2).broadcast_to([P, NT, E]), ALU.is_equal))
                    op(dve.tensor_scalar(cand[:], iota[:], -float(E), None, ALU.add))
                    op(dve.tensor_tensor(cand[:], cand[:], eq[:], ALU.mult))
                    op(dve.tensor_reduce(first[:], cand[:], AX.X, ALU.min))
                    op(dve.tensor_scalar(first[:], first[:], float(E), None, ALU.add))
                    op(dve.tensor_tensor(sel, iota[:], first[:].unsqueeze(2).broadcast_to([P, NT, E]), ALU.is_equal))
                    if k + 1 < K:
                        op(dve.scalar_tensor_tensor(l2[:].rearrange("p t e -> p (t e)"), sel.rearrange("p t e -> p (t e)"),
                                                    NEG, l2[:].rearrange("p t e -> p (t e)"), ALU.mult, ALU.add))
                dve.memset(G["tick"][:], 0.0).then_inc(oh_ready, 1)
                if K == 1:
                    op(dve.tensor_scalar(first[:], top[:, 0, :], -1.0, None, ALU.mult))
                else:
                    op(dve.tensor_tensor(first[:], top[:, 1, :], top[:, 0, :], ALU.subtract))
                dve.memset(G["tick"][:], 0.0).then_inc(exp_in, 1)
                dve.wait_ge(counted, 1)
                op(dve.tensor_copy(tot[0][:].rearrange("p s e -> p (s e)"), psT_[:]))
                a, d = 0, 1
                while d < KN:
                    dve.tensor_copy(tot[1 - a][:, 0:d, :], tot[a][:, 0:d, :])
                    op(dve.tensor_tensor(tot[1 - a][:, d:, :], tot[a][:, d:, :], tot[a][:, 0:KN - d, :], ALU.add))
                    a, d = 1 - a, 2 * d
                op(dve.tensor_scalar(count_i[:], tot[a][:, KN - 1, :], float(R - 1), None, ALU.add))
                shift = R.bit_length() - 1
                op(dve.tensor_scalar(count_i[:], count_i[:], shift, shift, ALU.logical_shift_right,
                                     ALU.logical_shift_left))
                op(dve.tensor_copy(count[:], count_i[:]))
                op(dve.memset(basee[:], 0.0))
                for e in range(1, E):
                    op(dve.tensor_tensor(basee[:, e:e + 1], basee[:, e - 1:e], count[:, e - 1:e], ALU.add))
                op(dve.tensor_tensor(pos[:], psB[:].rearrange("p (s e) -> p s e", e=E),
                                     basee[:].unsqueeze(1).broadcast_to([P, KN, E]), ALU.add))
                op(dve.tensor_tensor(pos[:, 1:, :], pos[:, 1:, :], tot[a][:, 0:KN - 1, :], ALU.add))
                op(dve.tensor_tensor(pos[:], pos[:], oh[:], ALU.mult))
                op(dve.tensor_reduce(posr[:], pos[:], AX.X, ALU.add))
                op(dve.tensor_copy(place[:], posr[:]))
                dve.memset(G["tick"][:], 0.0).then_inc(placed, 1)
                op(dve.memset(owner[:], 0.0))
                for e in range(1, E):
                    op(dve.tensor_scalar(ge[:], starts[:], basee[:, e:e + 1], None, ALU.is_ge))
                    op(dve.tensor_tensor(owner[:], owner[:], ge[:], ALU.add))
                op(dve.tensor_copy(table[:], owner[0:1, :]))
                dve.wait_ge(exp_out, 1)
                op(dve.tensor_scalar(first[:], ex[:], 1.0, None, ALU.add))
                op(dve.reciprocal(weight[:, 0, :], first[:]))
                if K == 2:
                    op(dve.tensor_tensor(weight[:, 1, :], ex[:], weight[:, 0, :], ALU.mult))


def expert_stage(nc, G, tag, K, sorted_rows, results, table, *, F, w1, w2, w3=None, b1=None, b2=None, g=None, b=None):
    NJ = n_pieces(K)
    NF = F // P
    RT = R // P
    UP = NF * (2 if w3 is not None else 1)
    affine = g is not None
    with Stage(nc, tag) as st:
        xg = [st.sb(f"xg{p}", [P, RT, D]) for p in range(2)]
        xT = [st.sb(f"xT{p}", [P, KD, R]) for p in range(2)]
        w1s = [st.sb(f"w1_{p}", [P, KD, F]) for p in range(2)]
        w3s = [st.sb(f"w3_{p}", [P, KD, F]) for p in range(2)] if w3 is not None else None
        w2s = [st.sb(f"w2_{p}", [P, NF, D]) for p in range(2)]
        if affine:
            gb = [st.sb(f"gb{p}", [P, 2, KD]) for p in range(2)]
            b1s = [st.sb(f"b1_{p}", [P, NF]) for p in range(2)]
            b2s = [st.sb(f"b2_{p}", [P, RT, D]) for p in range(2)]
        gate = st.sb("gated", [P, 2, R])
        h = [st.sb(f"h{p}", [P, NF, R]) for p in range(2)]
        yo = [st.sb(f"y{p}", [P, RT, D]) for p in range(2)]
        psX = [st.ps(f"psX{p}", [P, RT, KD, P]) for p in range(2)]
        psU = [st.ps(f"psU{i}", [P, 512]) for i in range(4)]
        psD = [st.ps(f"psD{p}", [P, RT, D]) for p in range(2)]
        ld = [st.sem(f"loaded{p}") for p in range(2)]
        turned, xT_ready = st.sem("turned"), st.sem("xT_ready")
        u_ready, u_free, gated = st.sem("up_ready"), st.sem("up_free"), st.sem("gate_ready")
        d_ready, y_ready = st.sem("down_ready"), st.sem("y_ready")
        stored = [st.sem(f"stored{p}") for p in range(2)]
        n_ld = 16 * (4 if not affine else 8)

        with st.block() as block:
            @block.sync
            def _(sp):
                def step(front, back):
                    if front:
                        j, p, r = front
                        e = sp.value_load(table[0:1, bass.ds(j, 1)], min_val=0, max_val=E - 1)
                        wait(sp, d_ready, j - 1)
                        sp.dma_start(xg[p][:], sorted_rows[bass.ds(j * R, R), :].rearrange("(t p) d -> p t d", p=P)
                                     ).then_inc(ld[p], 16)
                        pairs = [(w1s[p], w1)] + ([(w3s[p], w3)] if w3 is not None else []) + [(w2s[p], w2)]
                        for dst, src in pairs:
                            sp.dma_start(dst[:], src[bass.ds(e, 1), :, :].rearrange("e (k p) n -> p (e k) n", p=P)
                                         ).then_inc(ld[p], 16)
                        if affine:
                            for i, src in enumerate((g, b)):
                                sp.dma_start(gb[p][:, i, :], src[bass.ds(e, 1), :, :].rearrange("e p k -> p (e k)")
                                             ).then_inc(ld[p], 16)
                            sp.dma_start(b1s[p][:], b1[bass.ds(e, 1), :, :].rearrange("e p k -> p (e k)")
                                         ).then_inc(ld[p], 16)
                            for t in range(RT):
                                sp.dma_start(b2s[p][:, t, :], b2[bass.ds(e, 1), :].broadcast_to([P, D])
                                             ).then_inc(ld[p], 16)
                    if back:
                        j, p, r = back
                        sp.wait_ge(y_ready, j + 1)
                        sp.dma_start(results[bass.ds(j * R, R), :].rearrange("(t p) d -> p t d", p=P), yo[p][:]
                                     ).then_inc(stored[p], 16)

                two_halves(sp, NJ, step)
                for p in range(2):
                    sp.wait_ge(stored[p], NJ // 2 * 16)

            @block.tensor
            def _(pe):
                def step(front, back):
                    if front:
                        j, p, r = front
                        pe.wait_ge(ld[p], n_ld * (r + 1))
                        wait(pe, xT_ready, j - 1)
                        for t in range(RT):
                            for k in range(KD):
                                mm = pe.transpose(psX[p][:, t, k, :], xg[p][:, t, k * P:(k + 1) * P], G["ident"][:])
                        mm.then_inc(turned, 1)
                    if back:
                        j, p, r = back
                        pe.wait_ge(xT_ready, j + 1)
                        for n in range(UP):
                            if not (isinstance(j, int) and j == 0 and n < 4):
                                pe.wait_ge(u_free, j * UP + n - 3)
                            ws = w1s if w3 is None or n % 2 == 0 else w3s
                            m = n if w3 is None else n // 2
                            for k in range(KD):
                                mm = pe.matmul(psU[n % 4][:, 0:R], ws[p][:, k, m * P:(m + 1) * P], xT[p][:, k, :],
                                               start=(k == 0), stop=(k == KD - 1))
                            mm.then_inc(u_ready, 1)
                        pe.wait_ge(u_free, (j + 1) * UP)
                        wait(pe, y_ready, j - 1) if p else (wait(pe, y_ready, j - 1) if not isinstance(j, int) or j > 1
                                                             else None)
                        for t in range(RT):
                            for m in range(NF):
                                mm = pe.matmul(psD[p][:, t, :], h[p][:, m, t * P:(t + 1) * P], w2s[p][:, m, :],
                                               start=(m == 0), stop=(m == NF - 1))
                        mm.then_inc(d_ready, 1)

                two_halves(pe, NJ, step)

            @block.scalar
            def _(act):
                def step(front, back):
                    if front:
                        j, p, r = front
                        act.wait_ge(turned, j + 1)
                        wait(act, d_ready, j - 1)
                        for k in range(KD):
                            dst = xT[p][:, k, :].rearrange("p (t q) -> p t q", q=P)
                            if affine:
                                ins = act.activation(dst, psX[p][:, :, k, :], ACT.Identity, scale=gb[p][:, 0, k:k + 1],
                                                     bias=gb[p][:, 1, k:k + 1])
                            else:
                                ins = act.activation(dst, psX[p][:, :, k, :], ACT.Copy)
                        ins.then_inc(xT_ready, 1)
                    if back:
                        j, p, r = back
                        if w3 is None:
                            return
                        for m in range(NF):
                            act.wait_ge(u_ready, j * UP + 2 * m + 1)
                            if m >= 2:
                                act.wait_ge(u_free, j * UP + 2 * (m - 1))
                            act.activation(gate[:, m % 2, :], psU[2 * m % 4][:, 0:R], ACT.Silu).then_inc(gated, 1)

                two_halves(act, NJ, step)

            @block.vector
            def _(dve):
                def step(front, back):
                    if not back:
                        return
                    j, p, r = back
                    if w3 is None:
                        for n in range(UP):
                            dve.wait_ge(u_ready, j * UP + n + 1)
                            dve.tensor_scalar(h[p][:, n, :], psU[n % 4][:, 0:R], b1s[p][:, n:n + 1], 0.0, ALU.add,
                                              ALU.max).then_inc(u_free, 1)
                    else:
                        for m in range(NF):
                            dve.wait_ge(gated, j * NF + m + 1)
                            dve.wait_ge(u_ready, j * UP + 2 * m + 2)
                            dve.tensor_tensor(h[p][:, m, :], psU[(2 * m + 1) % 4][:, 0:R], gate[:, m % 2, :],
                                              ALU.mult).then_inc(u_free, 2)
                    dve.wait_ge(d_ready, j + 1)
                    wait(dve, stored[p], 16 * r)
                    if affine:
                        dve.tensor_tensor(yo[p][:], psD[p][:], b2s[p][:], ALU.add).then_inc(y_ready, 1)
                    else:
                        dve.tensor_copy(yo[p][:], psD[p][:]).then_inc(y_ready, 1)

                two_halves(dve, NJ, step)


def combine_stage(nc, G, tag, K, results, place, weight, add, out=None):
    with Stage(nc, tag) as st:
        got = st.sb("got", [P, K * NT, D])
        fetched, ready, stored = st.sem("fetched"), st.sem("ready"), st.sem("stored")
        X = G["X"]
        with st.block() as block:
            @block.gpsimd
            def _(pool):
                for t in range(NT):
                    for k in range(K):
                        pool.indirect_dma_start(
                            got[:, t * K + k, :], None, results,
                            bass.IndirectOffsetOnAxis(ap=place[:, k * NT + t:k * NT + t + 1], axis=0)
                        ).then_inc(fetched, 16)

            @block.vector
            def _(dve):
                dve.tensor_tensor(X[:], X[:], add[:], ALU.add)
                dve.drain()
                dve.wait_ge(fetched, 16 * K * NT)
                for k in range(K):
                    for t in range(NT):
                        ins = dve.scalar_tensor_tensor(X[:, t, :], got[:, t * K + k, :], weight[:, k, t:t + 1],
                                                       X[:, t, :], ALU.mult, ALU.add)
                        if k == K - 1:
                            ins.then_inc(ready, 1)
                    dve.drain()

            @block.sync
            def _(sp):
                if out is not None:
                    for t in range(NT):
                        sp.wait_ge(ready, t + 1)
                        sp.dma_start(out[t * P:(t + 1) * P, :], X[:, t, :]).then_inc(stored, 16)
                    sp.wait_ge(stored, 16 * NT)



def decoder(nc, A, out):
    G = {"cos": A["cos"], "sin": A["sin"]}
    Q16 = nc.dram_tensor("q16_scratch", (3, D, T), BF16, kind="Internal").ap()
    K16 = nc.dram_tensor("k16_scratch", (3, D, T), BF16, kind="Internal").ap()
    V16 = nc.dram_tensor("v16_scratch", (HEADS // 4, P, NT, 4 * 17), F32, kind="Internal").ap()
    QW = nc.dram_tensor("qw_scratch", (2, 1024, T), BF16, kind="Internal").ap()
    KW = nc.dram_tensor("kw_scratch", (1, 1024, T), BF16, kind="Internal").ap()
    QF = nc.dram_tensor("qf_scratch", (1024, T), F32, kind="Internal").ap()
    KF = nc.dram_tensor("kf_scratch", (1024, T), F32, kind="Internal").ap()
    VW = nc.dram_tensor("vw_scratch", (HEADS, P, NT, 65), F32, kind="Internal").ap()
    CK = [nc.dram_tensor(f"ctx_k_scratch{i}", (3, D, B * SC), BF16, kind="Internal").ap() for i in range(2)]
    CV = [nc.dram_tensor(f"ctx_v_scratch{i}", (HEADS // 4, SC, B, 4 * 17), F32, kind="Internal").ap() for i in range(2)]
    CM = nc.dram_tensor("mask_scratch", (B, 4, SC), BF16, kind="Internal").ap()
    OA = nc.dram_tensor("attn_scratch", (D, T), F32, kind="Internal").ap()
    OW = nc.dram_tensor("attn_wide_scratch", (1024, T), F32, kind="Internal").ap()
    SR = nc.dram_tensor("sorted_scratch", (n_pieces(2) * R, D), F32, kind="Internal").ap()
    RE = nc.dram_tensor("results_scratch", (n_pieces(2) * R, D), F32, kind="Internal").ap()

    def narrow(scr, m):
        return {"parts": [(scr[:, m * P:(m + 1) * P, :], 0, 3)]}

    qk16 = [narrow(Q16, 0), narrow(Q16, 1), narrow(K16, 0), narrow(K16, 1)]
    q16 = [narrow(Q16, 0), narrow(Q16, 1)]
    wide_units = ([{"parts": [(QW[:, m * P:(m + 1) * P, :], 0, 2)], "f32": QF[m * P:(m + 1) * P, :]} for m in range(8)]
                  + [{"parts": [(KW[:, m * P:(m + 1) * P, :], 0, 1)], "f32": KF[m * P:(m + 1) * P, :]} for m in range(8)])
    a16 = dict(q={"parts": Q16}, k={"parts": K16}, v=V16, o=OA)

    with Stage(nc, "g") as g:
        for name in ("X", "Y", "Z"):
            G[name] = g.sb(name, [P, NT, D])
        G["ident"], G["lower"], G["ones"], G["sel16"] = (g.sb(n, [P, P]) for n in ("ident", "lower", "ones", "sel16"))
        G["sel64"] = g.sb("sel64", [P, 64])
        G["identb"], G["maskS"], G["maskT"] = (g.sb(n, [P, P], BF16) for n in ("identb", "maskSb", "maskTb"))
        G["eps"], G["tick"] = g.sb("eps", [P, 1]), g.sb("tick", [1, 1])
        G["logits"] = g.sb("logits", [P, NT, E])
        place = [g.sb(f"place{k}", [P, k * NT], I32) for k in (1, 2)]
        weight = [g.sb(f"weight{k}", [P, k, NT]) for k in (1, 2)]
        table = [g.sb(f"table{k}", [1, n_pieces(k)], I32) for k in (1, 2)]

        setup_stage(nc, G, A["x"])
        token_stage(nc, G, "t0", norm="ln", resid=G["X"], units=qk16, rope=True, split=3, wf=A["wf0"], bf=A["bf0"],
                    wv=A["wv0"], bv=A["bv0"], outs=V16)
        attention_stage(nc, G, "a0", causal=True, **a16)
        context_stage(nc, G, "c1", A["ctxT"], A["wk1"], A["bk1"], A["wv1"], A["bv1"], A["mask"], CK[0], CV[0], CM)
        token_stage(nc, G, "t1", norm="ln", attn=(OA, A["wo0"], A["bo0"]), resid=G["X"], units=q16, split=3,
                    wf=A["wq1"], bf=A["bq1"])
        attention_stage(nc, G, "a1", q={"parts": Q16}, k={"parts": CK[0]}, v=CV[0], o=OA, cross=True, mask=CM)
        token_stage(nc, G, "t2", norm="ln_ln", attn=(OA, A["wo1"], A["bo1"]), resid=G["X"], gate=A["cent"])
        route_stage(nc, G, "r2", 1, G["Z"], SR[0:n_pieces(1) * R, :], table[0], place[0], weight[0])
        expert_stage(nc, G, "e2", 1, SR, RE, table[0], F=1024, w1=A["w1_2"], w2=A["w2_2"], b1=A["b1_2"], b2=A["b2_2"],
                     g=A["g_2"], b=A["b_2"])
        combine_stage(nc, G, "m2", 1, RE[0:n_pieces(1) * R, :], place[0], weight[0], G["Y"])
        token_stage(nc, G, "t3", norm="ln", resid=G["X"], units=wide_units, split=2, wide=True, wf=A["wf3"],
                    bf=A["bf3"], wv=A["wv3"], bv=A["bv3"], outs=VW, heads_group=1, hd=64)
        attention_stage(nc, G, "a3", wide=True, q={"parts": QW, "f32": QF}, k={"parts": KW, "f32": KF}, v=VW, o=OW)
        context_stage(nc, G, "c4", A["ctxT"], A["wk4"], A["bk4"], A["wv4"], A["bv4"], None, CK[1], CV[1], None)
        token_stage(nc, G, "t4", norm="ln", attn=(OW, A["wo3"], A["bo3"]), resid=G["X"], units=q16, split=3,
                    wf=A["wq4"], bf=A["bq4"])
        attention_stage(nc, G, "a4", q={"parts": Q16}, k={"parts": CK[1]}, v=CV[1], o=OA, cross=True)
        token_stage(nc, G, "t5", norm="ln_rms", attn=(OA, A["wo4"], A["bo4"]), resid=G["X"], units=qk16, split=3,
                    wf=A["wf5"], fscale=A["ln1"], wv=A["wv5"], outs=V16)
        attention_stage(nc, G, "a5", **a16)
        token_stage(nc, G, "t6", norm="rms", attn=(OA, A["wo5"], None), resid=G["Y"], ln2=A["ln2"], gate=A["gate"])
        route_stage(nc, G, "r6", 2, G["Z"], SR, table[1], place[1], weight[1])
        expert_stage(nc, G, "e6", 2, SR, RE, table[1], F=512, w1=A["w1_6"], w3=A["w3_6"], w2=A["w2_6"])
        combine_stage(nc, G, "m6", 2, RE, place[1], weight[1], G["Y"], out)



def layout(inputs):
    a = {k: np.asarray(v) for k, v in inputs.items()}
    c = np.ascontiguousarray
    per_part = lambda v: c(v.reshape(-1, P).T)
    swap = np.arange(D) ^ 1
    w, bias = a["L0_attn_w_attn"], a["L0_attn_b_attn"]
    wq, wk, bq, bk = w[:, :D], w[:, D:2 * D], bias[:D], bias[D:2 * D]
    hd = D // HEADS
    inv = (np.float32(1.0) / np.float32(10000.0) ** (np.arange(0, hd, 2, dtype=np.float32) / np.float32(hd))
           ).astype(np.float32)
    freqs = np.repeat(np.arange(S, dtype=np.float32)[:, None] * inv[None, :], 2, axis=-1)
    sign = np.where(np.arange(hd) % 2 == 0, -1.0, 1.0).astype(np.float32)
    table = lambda t: c(np.tile(t.T.astype(np.float32), (P // hd, B)))
    out = {
        "x": c(a["x"].reshape(T, D)),
        "ctxT": c(a["ctx_1024"].reshape(B * SC, D).T),
        "mask": c(a["mask_Bx1xS2_if1"]),
        "cos": table(np.cos(freqs)), "sin": table(np.sin(freqs) * sign),
        "wf0": c(np.concatenate([wq, wk, wq[:, swap], wk[:, swap]], 1)),
        "bf0": per_part(np.concatenate([bq, bk, bq[swap], bk[swap]])),
        "wv0": c(w[:, 2 * D:]), "bv0": c(bias[2 * D:]),
        "wo0": a["L0_attn_w_proj"], "bo0": a["L0_attn_b_proj"],
        "wq1": c(a["L0_xattn_Wq"].T), "bq1": per_part(a["L0_xattn_bq"]),
        "wk1": c(a["L0_xattn_Wk"].T), "bk1": per_part(a["L0_xattn_bk"]),
        "wv1": c(a["L0_xattn_Wv"].T), "bv1": a["L0_xattn_bv"],
        "wo1": c(a["L0_xattn_Wo"].T), "bo1": a["L0_xattn_bo"],
        "cent": c(a["L0_ffn_centroids"].T),
        "w1_2": c(a["L0_ffn_w1"].transpose(0, 2, 1)), "w2_2": c(a["L0_ffn_w2"].transpose(0, 2, 1)),
        "b1_2": c(a["L0_ffn_b1"].reshape(E, -1, P).transpose(0, 2, 1)), "b2_2": a["L0_ffn_b2"],
        "g_2": c(a["L0_ffn_ln_g"].reshape(E, -1, P).transpose(0, 2, 1)),
        "b_2": c(a["L0_ffn_ln_b"].reshape(E, -1, P).transpose(0, 2, 1)),
        "wf3": c(a["L1_attn_W_qkv"][:, :2048]), "bf3": per_part(a["L1_attn_b_qkv"][:2048]),
        "wv3": c(a["L1_attn_W_qkv"][:, 2048:]), "bv3": c(a["L1_attn_b_qkv"][2048:]),
        "wo3": a["L1_attn_W_out"], "bo3": a["L1_attn_b_out"],
        "wq4": c(a["L1_xattn_w_q"].T), "bq4": per_part(a["L1_xattn_b_q"]),
        "wk4": c(a["L1_xattn_w_k"].T), "bk4": per_part(a["L1_xattn_b_k"]),
        "wv4": c(a["L1_xattn_w_v"].T), "bv4": a["L1_xattn_b_v"],
        "wo4": c(a["L1_xattn_w_o"].T), "bo4": a["L1_xattn_b_o"],
        "ln1": per_part(a["L1_ffn_ln1_w"]), "ln2": a["L1_ffn_ln2_w"],
        "wf5": c(np.concatenate([a["L1_ffn_wq"].T, a["L1_ffn_wk"].T], 1)), "wv5": c(a["L1_ffn_wv"].T),
        "wo5": c(a["L1_ffn_wo"].T), "gate": c(a["L1_ffn_gate_w"].T),
        "w1_6": c(a["L1_ffn_w1"].transpose(0, 2, 1)), "w3_6": c(a["L1_ffn_w3"].transpose(0, 2, 1)),
        "w2_6": c(a["L1_ffn_w2"].transpose(0, 2, 1)),
    }
    return out


def kernel(**inputs):
    import concourse.bacc as bacc
    from concourse.bass_utils import run_bass_kernel_spmd

    nc = bacc.Bacc("TRN2", target_bir_lowering=False, num_devices=1)
    arrays, args = {}, {}
    for name, a in layout(inputs).items():
        arrays[f"in_{name}"] = a
        args[name] = nc.dram_tensor(f"in_{name}", a.shape, mybir.dt.from_np(a.dtype), kind="ExternalInput").ap()
    out = nc.dram_tensor("out", (T, D), F32, kind="ExternalOutput").ap()
    decoder(nc, args, out)
    r = run_bass_kernel_spmd(nc, [arrays], core_ids=[0])
    return r.results[0]["out"].reshape(B, S, D)
```

```python
import numpy as np
import concourse.bass as bass
from concourse import mybir
from contextlib import ExitStack

F32 = mybir.dt.float32
BF16 = mybir.dt.bfloat16
I32 = mybir.dt.int32
ALU = mybir.AluOpType
ACT = mybir.ActivationFunctionType
AX = mybir.AxisListType

B, S, D = 2, 1024, 256
T = B * S
P = 128
NT = T // P
KD = D // P
C = 256
NC = T // C
CT = C // P
SC = 77
HEADS = 16
E = 8
R = 256
NEG = -1.0e30
MASKED = -4.0e9
EPS = 1e-5


def two_halves(eng, n, step):
    step((0, 0, 0), None)
    step((1, 1, 0), (0, 0, 0))
    with eng.Fori(0, n // 2 - 1) as i:
        step((2 * i + 2, 0, i + 1), (2 * i + 1, 1, i))
        step((2 * i + 3, 1, i + 1), (2 * i + 2, 0, i + 1))
    step(None, (n - 1, 1, n // 2 - 1))


def in_thirds(eng, n, step):
    assert (n - 2) % 3 == 0
    step((0, 0, 0), None)
    step((1, 1, 0), (0, 0, 0))
    with eng.Fori(0, (n - 2) // 3) as i:
        step((3 * i + 2, 2, i), (3 * i + 1, 1, i))
        step((3 * i + 3, 0, i + 1), (3 * i + 2, 2, i))
        step((3 * i + 4, 1, i + 1), (3 * i + 3, 0, i + 1))
    step(None, (n - 1, 1, (n - 2) // 3))


def wait(eng, sem, value):
    if not isinstance(value, int) or value > 0:
        eng.wait_ge(sem, value)


class Stage:

    def __init__(self, nc, name):
        self.nc, self.name, self.ctx, self.sems = nc, name, ExitStack(), []

    def __enter__(self):
        return self

    def __exit__(self, *_):
        if self.sems:
            self.nc.clear_and_free_semaphores(self.sems)
            self.nc.all_engine_barrier()
        self.ctx.close()

    def sb(self, name, shape, dt=F32):
        return self.ctx.enter_context(self.nc.sbuf_tensor(f"{self.name}_{name}", shape, dt))

    def ps(self, name, shape, dt=F32):
        return self.ctx.enter_context(self.nc.psum_tensor(f"{self.name}_{name}", shape, dt))

    def sem(self, name):
        self.sems.append(self.nc.alloc_semaphore(name=f"{self.name}_{name}"))
        return self.sems[-1]

    def block(self):
        return self.nc.Block()



def setup_stage(nc, G, x):
    with Stage(nc, "init") as st:
        filled, shaped, loaded, done = st.sem("filled"), st.sem("shaped"), st.sem("loaded"), st.sem("done")
        mS = st.sb("maskS", [P, P])
        mT = st.sb("maskT", [P, P])
        with st.block() as block:
            @block.sync
            def _(sp):
                sp.dma_start(G["X"][:], x.rearrange("(t p) d -> p t d", p=P)).then_inc(loaded, 16)
                sp.wait_ge(loaded, 16)

            @block.gpsimd
            def _(pool):
                for t in (G["ident"], mS, mT, G["sel16"], G["sel64"]):
                    pool.memset(t[:], 0.0).then_inc(filled, 1)
                pool.memset(G["eps"][:], EPS)
                pool.memset(G["lower"][:], 1.0).then_inc(filled, 1)
                pool.memset(G["ones"][:], 1.0)
                pool.wait_ge(filled, 6)

                def select(t, view, pattern, base, mult, op, fill):
                    pool.affine_select(out=view, in_=view, compare_op=op, fill=fill, base=base,
                                       pattern=pattern, channel_multiplier=mult).then_inc(shaped, 1)

                select(None, G["ident"][:], [[-1, P]], 0, 1, ALU.not_equal, 1.0)
                select(None, mS[:], [[-1, P]], 0, 1, ALU.is_ge, NEG)
                select(None, mT[:], [[1, P]], 0, -1, ALU.is_ge, NEG)
                select(None, G["sel16"][:].rearrange("p (a r) -> p a r", r=32), [[-32, 4], [0, 32]], -16, 1,
                       ALU.not_equal, 1.0)
                select(None, G["sel64"][:], [[0, 64]], -64, 1, ALU.not_equal, 1.0)
                select(None, G["lower"][:], [[1, P]], 0, -1, ALU.is_gt, 0.0)

            @block.vector
            def _(dve):
                dve.wait_ge(shaped, 6)
                dve.tensor_copy(G["identb"][:], G["ident"][:])
                dve.tensor_copy(G["maskS"][:], mS[:])
                dve.tensor_copy(G["maskT"][:], mT[:]).then_inc(done, 1)



def token_stage(nc, G, tag, *, norm, attn=None, resid=None, units=(), rope=False, wide=None,
                wf=None, bf=None, fscale=None, wv=None, bv=None, heads_group=4, hd=16, outs=None, gate=None,
                ln2=None):
    kf = attn[1].shape[0] // P if attn else 0
    narrow = attn is not None and len(attn[0].shape) == 4
    n_units = len(units)
    n_rot = n_units if rope else 0
    v_cols = wv.shape[1] if wv is not None else 0
    v_parts = max(1, v_cols // 512)
    n_rows_units = CT * v_parts if wv is not None else (CT if gate is not None else 0)
    NU = n_units + n_rot + n_rows_units
    SETS = [list(range(s, min(s + 4, n_units))) for s in range(0, n_units, 4)]
    NS = len(SETS)
    USET = len(SETS[0]) if SETS else 0
    RP = 4 if NU >= 4 else 2
    assert 2 * NU % RP == 0 and (NS <= 1 or NS % 2 == 0)
    passes = 1 if norm in ("ln", "rms") else 2
    dve_frees = [u >= n_units + n_rot or rope for u in range(NU)]

    with Stage(nc, tag) as st:
        if attn:
            ot = [st.sb(f"attnT{p}", [P, kf, C]) for p in range(2)]
            wo = st.sb("wo", [P, kf, D])
            bo = st.sb("bo", [P, CT, D])
        nf = wf.shape[1] if wf is not None else 0
        wfs = st.sb("wf", [P, KD, nf]) if nf else None
        bfs = st.sb("bf", [P, nf // P]) if bf is not None else None
        fsc = st.sb("fscale", [P, KD]) if fscale is not None else None
        wvs = st.sb("wv", [P, KD, v_cols]) if wv is not None else None
        bvs = st.sb("bv", [P, v_cols]) if bv is not None else None
        wg = st.sb("wg", [P, KD, E]) if gate is not None else None
        ln2s = st.sb("ln2", [P, CT, D]) if ln2 is not None else None
        if rope:
            cos = st.sb("cos", [P, T])
            sin = st.sb("sin", [P, T])
            t1 = st.sb("t1", [P, 4, C])
            t2 = st.sb("t2", [P, 4, C])
        xn = [st.sb(f"xn{p}", [P, CT, D]) for p in range(2)]
        xT = [st.sb(f"xT{p}", [P, KD, C]) for p in range(2)]
        stats = st.sb("stats", [P, CT, 6])
        mv = st.sb("mv", [P, CT, 2])
        ms = st.sb("ms", [P, CT, 2])
        sd = st.sb("sd", [P, CT, 1])
        rs = st.sb("rs", [P, CT, 1])
        if NS:
            fo = [st.sb(f"f{p}", [P, USET, C]) for p in range(2)]
        if NS and wide is None:
            rr = [st.sb(f"r{p}", [P, USET, C]) for p in range(2)]
            parts = [st.sb(f"parts{p}", [P, USET, 3, C], BF16) for p in range(2)]
        HPG = v_cols // hd if wv is not None else 0
        if HPG:
            vst = [st.sb(f"v{p}", [P, CT, HPG, hd + 1]) for p in range(2)]
        psY = [st.ps(f"psY{p}", [P, CT, D]) for p in range(2)]
        psX = [st.ps(f"psX{p}", [P, CT, KD, P]) for p in range(2)]
        psP = [st.ps(f"psP{p}", [P, 512]) for p in range(RP)]

        w_ld, o_ld = st.sem("weights_loaded"), [st.sem(f"attn_loaded{p}") for p in range(2)]
        y_ready, y_free = st.sem("y_ready"), st.sem("y_free")
        var_ready, sd_ready = st.sem("var_ready"), st.sem("sd_ready")
        xn_ready, turned, xT_ready = st.sem("xn_ready"), st.sem("turned"), st.sem("xT_ready")
        pu_ready, act_free, dve_free = st.sem("proj_ready"), st.sem("proj_free_act"), st.sem("proj_free_dve")
        f_ready, h_ready, r_ready, m_ready = st.sem("f_ready"), st.sem("h_ready"), st.sem("r_ready"), st.sem("m_ready")
        parts_ready = st.sem("parts_ready")
        f_out = [st.sem(f"f_stored{p}") for p in range(2)]
        v_out = [st.sem(f"v_stored{p}") for p in range(2)]
        kept = st.sem("kept")

        loads = []
        if attn:
            loads += [(wo[:], attn[1].rearrange("(k p) n -> p k n", p=P))]
            if attn[2] is not None:
                loads += [(bo[:, t, :], attn[2].partition_broadcast(P)) for t in range(CT)]
        if nf:
            loads += [(wfs[:], wf.rearrange("(k p) n -> p k n", p=P))]
        if bf is not None:
            loads += [(bfs[:], bf)]
        if fscale is not None:
            loads += [(fsc[:], fscale)]
        if wv is not None:
            loads += [(wvs[:], wv.rearrange("(k p) n -> p k n", p=P))]
        if bv is not None:
            loads += [(bvs[:], bv.partition_broadcast(P))]
        if gate is not None:
            loads += [(wg[:], gate.rearrange("(k p) n -> p k n", p=P))]
        if ln2 is not None:
            loads += [(ln2s[:, t, :], ln2.partition_broadcast(P)) for t in range(CT)]
        if rope:
            loads += [(cos[:], G["cos"]), (sin[:], G["sin"])]
        n_loads = 16 * len(loads)

        def set_buffer(piece, s):
            c, p, r = piece
            return (p, r) if NS == 1 else (s % 2, c * (NS // 2) + s // 2)

        def stores(piece, s):
            c, p, r = piece
            b = set_buffer(piece, s)[0]
            if wide is not None:
                dst = wide[SETS[s][0] * P:(SETS[s][-1] + 1) * P, bass.ds(c * C, C)]
                yield dst.rearrange("(i p) t -> p i t", p=P), fo[b][:]
                return
            for i, u in enumerate(SETS[s]):
                for e, dst in enumerate(units[u]):
                    yield (dst[:, bass.ds(r, 1), :, C * p:C * (p + 1)].rearrange("i o f t -> f (i o) t"),
                           parts[b][64 * e:64 * (e + 1), i, :, :])

        n_store = [16 if wide is not None else 16 * sum(len(units[u]) for u in us) for us in SETS]
        store_per_use = n_store[0] if SETS else 0
        assert all(n == store_per_use for n in n_store)

        def store(eng, piece):
            c, p, r = piece
            for s in range(NS):
                b = set_buffer(piece, s)[0]
                if wide is not None:
                    eng.wait_ge(act_free, c * n_units + SETS[s][-1] + 1)
                else:
                    eng.wait_ge(parts_ready, c * NS + s + 1)
                for dst, src in stores(piece, s):
                    eng.dma_start(dst, src).then_inc(f_out[b], 16)
            if wv is not None:
                eng.wait_ge(dve_free, (c + 1) * sum(dve_frees))
                for t in range(CT):
                    dst = (outs[:, :, bass.ds(c * CT + t, 1), :].rearrange("g p t x -> p g (t x)") if wide is not None
                           else outs[:, bass.ds(r, 1), :, p * CT + t, :].rearrange("g o p x -> p g (o x)"))
                    eng.dma_start(dst,
                                  vst[p][:, t].rearrange("p (g h) x -> p g (h x)", h=heads_group)
                                  ).then_inc(v_out[p], 16)

        def all_stored(eng):
            for p in range(2):
                if NS:
                    eng.wait_ge(f_out[p], (NC // 2 if NS == 1 else NC * NS // 2) * store_per_use)
                if wv is not None:
                    eng.wait_ge(v_out[p], NC // 2 * 16 * CT)

        with st.block() as block:
            @block.sync
            def _(sp):
                for dst, src in loads:
                    sp.dma_start(dst, src).then_inc(w_ld, 16)

                def step(front, back):
                    if front and attn:
                        c, p, r = front
                        wait(sp, y_ready, c - 1)
                        if narrow:
                            view = attn[0].rearrange("(k e) o f t -> e k o f t", e=2)
                            for e in range(2):
                                sp.dma_start(ot[p][64 * e:64 * (e + 1), :, :],
                                             view[e, :, bass.ds(r, 1), :, C * p:C * (p + 1)].rearrange(
                                                 "k o f t -> f (k o) t")).then_inc(o_ld[p], 16)
                        else:
                            sp.dma_start(ot[p][:], attn[0][:, bass.ds(c * C, C)].rearrange("(k p) t -> p k t", p=P)
                                         ).then_inc(o_ld[p], 16)
                    if back and wide is not None:
                        store(sp, back)

                two_halves(sp, NC, step)
                if wide is not None:
                    all_stored(sp)
                sp.wait_ge(w_ld, n_loads)

            @block.gpsimd
            def _(pool):
                if outs is None and not NS or wide is not None:
                    return
                two_halves(pool, NC, lambda front, back: store(pool, back) if back else None)
                all_stored(pool)

            @block.tensor
            def _(pe):
                def freed(piece, u):
                    c, p, r = piece
                    if u < 0:
                        c, u = c - 1, u + NU
                    same = dve_frees[u]
                    count = c * dve_frees.count(same) + dve_frees[:u + 1].count(same)
                    return (dve_free if same else act_free), count

                def step(front, back):
                    if front and attn:
                        c, p, r = front
                        if isinstance(c, int) and c == 0:
                            pe.wait_ge(w_ld, n_loads)
                        pe.wait_ge(o_ld[p], 16 * (1 + narrow) * (r + 1))
                        wait(pe, y_free, c - 1)
                        for t in range(CT):
                            for k in range(kf):
                                mm = pe.matmul(psY[p][:, t, :], ot[p][:, k, t * P:(t + 1) * P], wo[:, k, :],
                                               start=(k == 0), stop=(k == kf - 1))
                        mm.then_inc(y_ready, 1)
                    if back:
                        c, p, r = back
                        if isinstance(c, int) and c == 0:
                            pe.wait_ge(w_ld, n_loads)
                        pe.wait_ge(xT_ready, c + 1)
                        jobs = []
                        for u in range(n_units):
                            jobs.append(("f", u))
                            if rope:
                                jobs.append(("f", n_units + u))
                        for t in range(CT):
                            for v in range(v_parts):
                                jobs.append(("v", t, v))
                        for n, job in enumerate(jobs[:NU]):
                            slot = (p * NU + n) % RP
                            if not (isinstance(c, int) and c == 0 and n < RP):
                                pe.wait_ge(*freed(back, n - RP))
                            for k in range(KD):
                                if job[0] == "f":
                                    m = job[1]
                                    mm = pe.matmul(psP[slot][:, 0:C], wfs[:, k, m * P:(m + 1) * P], xT[p][:, k, :],
                                                   start=(k == 0), stop=(k == KD - 1))
                                elif wv is not None:
                                    w = min(512, v_cols)
                                    _, t, v = job
                                    mm = pe.matmul(psP[slot][:, 0:w], xT[p][:, k, t * P:(t + 1) * P],
                                                   wvs[:, k, v * w:(v + 1) * w], start=(k == 0), stop=(k == KD - 1))
                                else:
                                    t = job[1]
                                    mm = pe.matmul(psP[slot][:, 0:E], xT[p][:, k, t * P:(t + 1) * P], wg[:, k, :],
                                                   start=(k == 0), stop=(k == KD - 1))
                            mm.then_inc(pu_ready, 1)
                    if front:
                        c, p, r = front
                        pe.wait_ge(xn_ready, c + 1)
                        wait(pe, xT_ready, c - 1)
                        for t in range(CT):
                            for k in range(KD):
                                mm = pe.transpose(psX[p][:, t, k, :], xn[p][:, t, k * P:(k + 1) * P], G["ident"][:])
                        mm.then_inc(turned, 1)

                two_halves(pe, NC, step)

            @block.scalar
            def _(act):
                def step(front, back):
                    if front:
                        c, p, r = front
                        for q in range(passes):
                            act.wait_ge(var_ready, c * passes + q + 1)
                            src = mv[:, :, 1:2] if not (norm == "rms" or (norm == "ln_rms" and q)) else ms[:, :, 1:2]
                            act.activation(sd[:], src, ACT.Sqrt, bias=G["eps"][:]).then_inc(sd_ready, 1)
                    if back:
                        c, p, r = back
                        if isinstance(c, int) and c == 0:
                            act.wait_ge(w_ld, n_loads)
                        for s in range(NS):
                            b, uses = set_buffer(back, s)
                            us = SETS[s]
                            if not rope:
                                wait(act, f_out[b], uses * store_per_use)
                                for i, u in enumerate(us):
                                    act.wait_ge(pu_ready, c * NU + u + 1)
                                    slot = (p * NU + u) % RP
                                    bias = bfs[:, u:u + 1] if bf is not None else 0.0
                                    act.activation(fo[b][:, i, :], psP[slot][:, 0:C], ACT.Identity if bf is not None
                                                   else ACT.Copy, bias=bias).then_inc(act_free, 1)
                                if wide is not None:
                                    continue
                                act.drain()
                            else:
                                act.wait_ge(f_ready, c * NS + s + 1)
                                wait(act, f_out[b], uses * store_per_use)
                            act.activation(parts[b][:, :, 0, :], fo[b][:], ACT.Copy).then_inc(h_ready, 1)
                            act.wait_ge(r_ready, c * NS + s + 1)
                            act.activation(parts[b][:, :, 1, :], rr[b][:], ACT.Copy).then_inc(m_ready, 1)
                    if front:
                        c, p, r = front
                        act.wait_ge(turned, c + 1)
                        wait(act, pu_ready, (c - 1) * NU)
                        if fscale is None:
                            act.activation(xT[p][:].rearrange("p k (t q) -> p t k q", q=P), psX[p][:], ACT.Copy
                                           ).then_inc(xT_ready, 1)
                        else:
                            act.activation(xT[p][:, 0, :].rearrange("p (t q) -> p t q", q=P), psX[p][:, :, 0, :],
                                           ACT.Copy, scale=fsc[:, 0:1])
                            act.activation(xT[p][:, 1, :].rearrange("p (t q) -> p t q", q=P), psX[p][:, :, 1, :],
                                           ACT.Copy, scale=fsc[:, 1:2]).then_inc(xT_ready, 1)

                two_halves(act, NC, step)

            @block.vector
            def _(dve):
                if HPG:
                    for p in range(2):
                        dve.memset(vst[p][:, :, :, hd:hd + 1], 1.0)
                dve.wait_ge(w_ld, n_loads)
                dve.drain()

                def moments(src, c, q, rms):
                    for t in range(CT):
                        dve.bn_stats(stats[:, t, :], src(t))
                    dve.drain()
                    for t in range(CT):
                        ins = dve.bn_aggr(mv[:, t, :], stats[:, t, :])
                    if rms:
                        dve.drain()
                        dve.tensor_tensor(ms[:, :, 0:1], mv[:, :, 0:1], mv[:, :, 0:1], ALU.mult)
                        dve.drain()
                        ins = dve.tensor_tensor(ms[:, :, 1:2], ms[:, :, 0:1], mv[:, :, 1:2], ALU.add)
                    ins.then_inc(var_ready, 1)
                    dve.wait_ge(sd_ready, c * passes + q + 1)
                    dve.reciprocal(rs[:], sd[:])
                    dve.drain()

                def step(front, back):
                    if front:
                        c, p, r = front
                        rows = resid[:, bass.ds(c * CT, CT), :]
                        row = lambda t: resid[:, bass.ds(c * CT + t, 1), :].rearrange("p t d -> p (t d)")
                        if attn:
                            dve.wait_ge(y_ready, c + 1)
                            dve.tensor_tensor(rows, psY[p][:], rows, ALU.add).then_inc(y_free, 1)
                            if attn[2] is not None:
                                dve.drain()
                                dve.tensor_tensor(rows, rows, bo[:], ALU.add)
                            dve.drain()
                        keep = None
                        moments(row, c, 0, norm == "rms")
                        wait(dve, turned, c - 1)
                        for t in range(CT):
                            if norm == "rms":
                                ins = dve.tensor_scalar(xn[p][:, t, :], row(t), rs[:, t, :], None, ALU.mult)
                            else:
                                ins = dve.tensor_scalar(xn[p][:, t, :], row(t), mv[:, t, 0:1], rs[:, t, :],
                                                        ALU.subtract, ALU.mult)
                        if norm == "ln":
                            ins.then_inc(xn_ready, 1)
                        elif norm == "rms":
                            dve.drain()
                            dve.tensor_tensor(xn[p][:], xn[p][:], ln2s[:], ALU.mult).then_inc(xn_ready, 1)
                            dve.drain()
                            dve.tensor_copy(G["Z"][:, bass.ds(c * CT, CT), :], xn[p][:])
                        elif norm == "ln_ln":
                            ins.then_inc(xn_ready, 1)
                            dve.drain()
                            dve.tensor_copy(G["Y"][:, bass.ds(c * CT, CT), :], xn[p][:])
                            moments(lambda t: xn[p][:, t, :], c, 1, False)
                            for t in range(CT):
                                dve.tensor_scalar(G["Z"][:, bass.ds(c * CT + t, 1), :], xn[p][:, t:t + 1, :],
                                                  mv[:, t, 0:1], rs[:, t, :], ALU.subtract, ALU.mult)
                        elif norm == "ln_rms":
                            dve.drain()
                            dve.tensor_copy(G["Y"][:, bass.ds(c * CT, CT), :], xn[p][:])
                            moments(lambda t: xn[p][:, t, :], c, 1, True)
                            for t in range(CT):
                                ins = dve.tensor_scalar(xn[p][:, t, :], xn[p][:, t, :], rs[:, t, :], None, ALU.mult)
                            ins.then_inc(xn_ready, 1)
                        dve.drain()
                    if back:
                        c, p, r = back
                        for s in range(NS):
                            b, uses = set_buffer(back, s)
                            if rope:
                                for i, u in enumerate(SETS[s]):
                                    for k, (tt, tab) in enumerate(((t1, cos), (t2, sin))):
                                        n = 2 * u + k
                                        dve.wait_ge(pu_ready, c * NU + n + 1)
                                        slot = (p * NU + n) % RP
                                        m = u + k * n_units
                                        dve.scalar_tensor_tensor(tt[:, i, :], psP[slot][:, 0:C], bfs[:, m:m + 1],
                                                                 tab[:, bass.ds(c * C, C)], ALU.add, ALU.mult
                                                                 ).then_inc(dve_free, 1)
                                dve.drain()
                                wait(dve, h_ready, c - 1)
                                dve.tensor_tensor(fo[b][:], t1[:], t2[:], ALU.add).then_inc(f_ready, 1)
                            if wide is not None:
                                continue
                            dve.wait_ge(h_ready, c * NS + s + 1)
                            dve.tensor_tensor(rr[b][:], fo[b][:], parts[b][:, :, 0, :], ALU.subtract
                                              ).then_inc(r_ready, 1)
                            dve.wait_ge(m_ready, c * NS + s + 1)
                            dve.tensor_tensor(parts[b][:, :, 2, :], rr[b][:], parts[b][:, :, 1, :], ALU.subtract
                                              ).then_inc(parts_ready, 1)
                        if wv is not None:
                            wait(dve, v_out[p], r * 16 * CT)
                        if n_rows_units:
                            for t in range(CT):
                                for v in range(v_parts):
                                    n = n_units + n_rot + t * v_parts + v
                                    dve.wait_ge(pu_ready, c * NU + n + 1)
                                    slot = (p * NU + n) % RP
                                    if wv is not None:
                                        w = min(512, v_cols)
                                        hp = w // hd
                                        out = vst[p][:, t, v * hp:(v + 1) * hp, 0:hd]
                                        src = psP[slot][:, 0:w].rearrange("p (h r) -> p h r", r=hd)
                                        if bv is not None:
                                            dve.tensor_tensor(out, src, bvs[:, v * w:(v + 1) * w].rearrange(
                                                "p (h r) -> p h r", r=hd), ALU.add).then_inc(dve_free, 1)
                                        else:
                                            dve.tensor_copy(out, src).then_inc(dve_free, 1)
                                    else:
                                        dve.tensor_copy(G["logits"][:, bass.ds(c * CT + t, 1), :],
                                                        psP[slot][:, 0:E].rearrange("p (a e) -> p a e", a=1)
                                                        ).then_inc(dve_free, 1)
                        dve.drain()

                two_halves(dve, NC, step)



def context_stage(nc, G, tag, ctxT, wk, bk, wv, bv, mask, k_out, v_out, mask_out):
    W = B * SC
    with Stage(nc, tag) as st:
        cT, wks, wvs = st.sb("ctxT", [P, KD, W]), st.sb("wk", [P, KD, D]), st.sb("wv", [P, KD, D])
        bks, bvs = st.sb("bk", [P, KD]), st.sb("bv", [SC, D])
        f, r = st.sb("f", [P, KD, W]), st.sb("r", [P, KD, W])
        parts = st.sb("parts", [P, KD, 3, W], BF16)
        v = st.sb("v", [SC, B, HEADS, 17])
        psK = [st.ps(f"psK{m}", [P, 512]) for m in range(KD)]
        psV = [st.ps(f"psV{b}", [P, 512]) for b in range(B)]
        loaded, ready, stored, done = st.sem("loaded"), st.sem("ready"), st.sem("stored"), st.sem("done")
        n = 6
        if mask is not None:
            mi, mf = st.sb("mi", [P, W], I32), st.sb("mf", [P, W])
            mb = st.sb("mb", [1, B, 4, SC], BF16)
            n += 1
        with st.block() as block:
            @block.sync
            def _(sp):
                sp.dma_start(cT[:], ctxT.rearrange("(k p) t -> p k t", p=P)).then_inc(loaded, 16)
                sp.dma_start(wks[:], wk.rearrange("(k p) n -> p k n", p=P)).then_inc(loaded, 16)
                sp.dma_start(wvs[:], wv.rearrange("(k p) n -> p k n", p=P)).then_inc(loaded, 16)
                sp.dma_start(bks[:], bk).then_inc(loaded, 16)
                sp.dma_start(bvs[:], bv.partition_broadcast(SC)).then_inc(loaded, 16)
                if mask is not None:
                    sp.dma_start(mi[:], mask.rearrange("b a s -> (b a s)").partition_broadcast(P)).then_inc(loaded, 16)
                sp.wait_ge(done, 1)
                for hg in range(HEADS // 4):
                    at = hg % 2 * 64
                    for b in range(B):
                        sp.dma_start(k_out[:, hg, b].rearrange("i f s -> f i s"),
                                     parts[at:at + 64, hg // 2, :, b * SC:(b + 1) * SC]).then_inc(stored, 16)
                for b in range(B):
                    sp.dma_start(v_out[:, b].rearrange("g p x -> p g x"),
                                 v[:, b].rearrange("p (g h) x -> p g (h x)", h=4)).then_inc(stored, 16)
                if mask is not None:
                    for hg in range(HEADS // 4):
                        sp.dma_start(mask_out[hg * B:(hg + 1) * B].rearrange("(a b) h s -> a b h s", a=1), mb[:]
                                     ).then_inc(stored, 16)
                sp.wait_ge(stored, 16 * (HEADS // 4 * B + B + (HEADS // 4 if mask is not None else 0)))

            @block.tensor
            def _(pe):
                pe.wait_ge(loaded, 16 * (n - 1))
                for m in range(KD):
                    for k in range(KD):
                        pe.matmul(psK[m][:, 0:W], wks[:, k, m * P:(m + 1) * P], cT[:, k, :], start=(k == 0),
                                  stop=(k == KD - 1))
                for b in range(B):
                    for k in range(KD):
                        mm = pe.matmul(psV[b][0:SC, 0:D], cT[:, k, b * SC:(b + 1) * SC], wvs[:, k, :],
                                       start=(k == 0), stop=(k == KD - 1))
                mm.then_inc(ready, 1)

            @block.vector
            def _(dve):
                dve.memset(v[:, :, :, 16:17], 1.0)
                dve.wait_ge(loaded, 16 * (n - 1))
                if mask is not None:
                    dve.tensor_scalar(mf[:], mi[:], 0.0, None, ALU.not_equal)
                    dve.drain()
                    for b in range(B):
                        for h in range(4):
                            dve.tensor_scalar(mb[:, b, h, :], mf[0:1, b * SC:(b + 1) * SC], -MASKED, MASKED,
                                              ALU.mult, ALU.add)
                dve.wait_ge(ready, 1)
                for m in range(KD):
                    dve.tensor_scalar(f[:, m, :], psK[m][:, 0:W], bks[:, m:m + 1], None, ALU.add)
                    if mask is not None:
                        dve.drain()
                        dve.tensor_tensor(f[:, m, :], f[:, m, :], mf[:], ALU.mult)
                dve.drain()
                dve.tensor_copy(parts[:, :, 0, :], f[:])
                dve.drain()
                dve.tensor_tensor(r[:], f[:], parts[:, :, 0, :], ALU.subtract)
                dve.drain()
                dve.tensor_copy(parts[:, :, 1, :], r[:])
                dve.drain()
                dve.tensor_tensor(parts[:, :, 2, :], r[:], parts[:, :, 1, :], ALU.subtract)
                for b in range(B):
                    ins = dve.tensor_tensor(v[:, b, :, 0:16], psV[b][0:SC, 0:D].rearrange("p (h r) -> p h r", r=16),
                                            bvs[:].rearrange("p (h r) -> p h r", r=16), ALU.add)
                dve.drain()
                dve.memset(G["tick"][:], 0.0).then_inc(done, 1)



Q_PARTS = (0, 0, 1, 1, 0, 2)
K_PARTS = (0, 1, 0, 1, 2, 0)


def spread(costs_front, costs_back, first):
    work, total = np.cumsum(costs_back[first:]), sum(costs_front)
    done = np.cumsum(costs_front)
    return [0] * first + [int(np.searchsorted(done, w / work[-1] * total * (1 + 1e-9), side="right")) for w in work]


def attention_stage(nc, G, tag, *, q, k, v, o, causal=False, cross=False, mask=None, sums=None):
    H, hd = 4, 16
    n_groups = (HEADS // H) * B
    KT = [(0, SC)] if cross else [(i * P, P) for i in range(S // P)]
    NK = SC if cross else S
    QT = S // P
    scale = float(hd) ** -0.5
    base = len(Q_PARTS) * 16
    K1 = base + (mask is not None)
    K2 = K1 + 3
    units1 = [(None, h) for h in range(H)] if cross else [(t, h) for t in range(QT) for h in range(H)]
    NS = len(units1)
    ugs = [(qh, i, max(0, k0 - 512 * qh) if causal else 0) for qh in range(2) for i, (k0, _) in enumerate(KT)
           if not causal or k0 < 512 * (qh + 1)]
    NUG, NST = len(ugs), len(ugs) * H
    HALF = [ug[0] for ug in ugs].index(1) * H
    RING = 3
    VC = H * (hd + 1)
    VT = 1 if cross else QT
    n_turns = 1 if cross else 2
    TR = H * QT // n_turns
    if not cross:
        due = spread([(t + 1) * P if causal else S for t, _ in units1],
                     [512 - ugs[u // H][2] for u in range(NST)], 0)
        INVERT_AT = NS // 2 if causal else NS // 4

    with Stage(nc, tag) as st:
        qs = [st.sb(f"qs{p}", [P, 2, H, 512], BF16) for p in range(3)]
        ks = [st.sb(f"ks{p}", [P, H, SC] if cross else [P, 2, H, 512], BF16) for p in range(3)]
        vs = [st.sb(f"vs{p}", [P, VT, H, hd + 1]) for p in range(3)]
        pr = [st.sb(f"probs{r}", [P, H, 512]) for r in range(RING)]
        osb = st.sb("osb", [P, S])
        rec = st.sb("rec", [P, S])
        on = [st.sb(f"on{p}", [P, S]) for p in range(3)]
        if sums is not None:
            sm, inv = st.sb("sums", [P, H * S // P]), st.sb("inverses", [P, H * S // P])
        mx = st.sb("mx", [P, 2, H, QT // 2])
        neg = st.sb("neg", [TR, P])
        nres = st.sb("nres", [TR, P])
        nparts = [[st.sb(f"nparts{p}{w}", [TR, 3, P], BF16) for w in range(n_turns)] for p in range(3)]
        ps1 = [st.ps(f"rows{p}", [P, S]) for p in range(2)]
        ps2 = [st.ps(f"cols{p}", [P, 512]) for p in range(2)]
        psO = st.ps("out", [P, S])
        ld = [st.sem(f"loaded{p}") for p in range(3)]
        mld = [[st.sem(f"max_placed{p}{w}") for w in range(n_turns)] for p in range(3)]
        if sums is not None:
            sums_out, sums_in = st.sem("sums_out"), st.sem("sums_in")
            inv_out, inv_in = st.sem("inverses_out"), st.sem("inverses_in")
        ones_set = st.sem("ones_set")
        s_ready, s_free = st.sem("rows_ready"), st.sem("rows_free")
        mt_ready, mt_done, neg_ready = st.sem("max_turned"), st.sem("max_read"), st.sem("neg_ready")
        st_ready, ex_done, pv_done = st.sem("cols_ready"), st.sem("exp_done"), st.sem("pv_done")
        o_copied, lb_ready = st.sem("out_copied"), st.sem("sums_ready")
        rec_done, o_done = st.sem("sums_inverted"), st.sem("out_done")
        stored = [st.sem(f"stored{p}") for p in range(3)]
        n_ld = 2 * len(Q_PARTS) + (mask is not None) + 1

        with st.block() as block:
            @block.sync
            def _(sp):
                sp.wait_ge(ones_set, 1)

                def load(p, g):
                    for i in range(len(Q_PARTS)):
                        rows = slice(16 * i, 16 * i + 16)
                        yield (qs[p][rows].rearrange("r a h t -> r (a h) t"),
                               q.rearrange("i g o f t -> i (g o) f t")[Q_PARTS[i], bass.ds(2 * g, 2)].rearrange(
                                   "a (h r) t -> r (a h) t", r=16))
                        if cross:
                            yield (ks[p][rows],
                                   k.rearrange("i g b f s -> i (g b) f s")[K_PARTS[i], bass.ds(g, 1)].rearrange(
                                       "o (h r) s -> r (o h) s", r=16))
                        else:
                            yield (ks[p][rows].rearrange("r a h t -> r (a h) t"),
                                   k.rearrange("i g o f t -> i (g o) f t")[K_PARTS[i], bass.ds(2 * g, 2)].rearrange(
                                       "a (h r) t -> r (a h) t", r=16))
                    if mask is not None:
                        yield ks[p][base:base + 1, :, :], mask[bass.ds(g, 1), :, :]
                    if cross:
                        yield (vs[p][0:SC, 0].rearrange("p h x -> p (h x)"),
                               v.rearrange("g b p x -> (g b) p x")[bass.ds(g, 1)].rearrange("o p x -> p (o x)"))
                    else:
                        yield (vs[p][:].rearrange("p (a t) h x -> p a (t h x)", a=2),
                               v.rearrange("g o p t x -> (g o) p (t x)")[bass.ds(2 * g, 2)].rearrange("a p x -> p a x"))

                def exchange(g, p):
                    sp.wait_ge(o_copied, g + 1)
                    sp.dma_start(sums[0, p].rearrange("(h t) -> h t", h=H), osb[hd:P:32, :]).then_inc(sums_out, 16)
                    sp.wait_ge(sums_out, 16 * (g + 1))
                    sp.dma_start(sm[:], sums[0, p].rearrange("(p x) -> p x", p=P)).then_inc(sums_in, 16)
                    sp.wait_ge(rec_done, g + 1)
                    sp.dma_start(sums[1, p].rearrange("(p x) -> p x", p=P), inv[:]).then_inc(inv_out, 16)
                    sp.wait_ge(inv_out, 16 * (g + 1))
                    wait(sp, o_done, g)
                    for h in range(H):
                        sp.dma_start(rec[32 * h:32 * h + hd, :], sums[1, p, h * S:(h + 1) * S].partition_broadcast(hd)
                                     ).then_inc(inv_in, 16)

                def place(piece, w):
                    g, p, r = piece
                    sp.wait_ge(neg_ready, n_turns * g + w + 1)
                    for i in range(3):
                        dst = qs[p][K1 + i:K1 + i + 1]
                        dst = dst if n_turns == 1 else dst[:, w:w + 1]
                        sp.dma_start(dst.rearrange("p a h (t q) -> p (a h t) q", q=P),
                                     nparts[p][w][:, i, :]).then_inc(mld[p][w], 16)

                def step(front, back):
                    first = back and isinstance(back[0], int) and back[0] == 0
                    if n_turns == 2 and back and not first:
                        place(back, 0)
                    if front:
                        g, p, r = front
                        wait(sp, pv_done, (g - 2) * NUG)
                        for dst, src in load(p, g):
                            sp.dma_start(dst, src).then_inc(ld[p], 16)
                    if back:
                        if n_turns == 1 or first:
                            place(back, 0)
                        if n_turns == 2:
                            place(back, 1)
                        if sums is not None and not first:
                            exchange(back[0] - 1, (back[1] + 2) % 3)

                in_thirds(sp, n_groups, step)
                if sums is not None:
                    exchange(n_groups - 1, (n_groups - 1) % 3)

            @block.gpsimd
            def _(pool):
                def step(front, back):
                    if back:
                        g, p, r = back
                        if sums is not None:
                            pool.wait_ge(inv_in, 16 * H * (g + 1))
                        else:
                            pool.wait_ge(rec_done, g + 1)
                        wait(pool, stored[p], r * H * 16)
                        pool.tensor_tensor(on[p][:], osb[:], rec[:], ALU.mult).then_inc(o_done, 1)
                        pool.wait_ge(o_done, g + 1)
                        for h in range(H):
                            pool.dma_start(o.rearrange("g o f t -> (g o) f t")[bass.ds(2 * g, 2), 16 * h:16 * h + 16]
                                           .rearrange("a f t -> f a t"),
                                           on[p][32 * h:32 * h + 16, :].rearrange("f (a t) -> f a t", a=2)
                                           ).then_inc(stored[p], 16)

                in_thirds(pool, n_groups, step)
                for p in range(3):
                    pool.wait_ge(stored[p], (n_groups - p + 2) // 3 * H * 16)

            @block.tensor
            def _(pe):
                pe.wait_ge(ones_set, 1)

                def rows_unit(front, s):
                    g, p, r = front
                    t, h = units1[s]
                    dst = ps1[s % 2]
                    if s >= 2:
                        pe.wait_ge(s_free, g * NS + s - 1)
                    elif s == 1:
                        wait(pe, mt_done, n_turns * g)
                    elif cross:
                        wait(pe, rec_done, g - 2)
                    else:
                        wait(pe, s_free, g * NS - 1)
                    if n_turns == 2 and s == NS // 2 + 1:
                        pe.wait_ge(mt_done, n_turns * g + 1)
                    if cross:
                        for t in range(QT):
                            at = 512 * (t // 4) + SC * (t % 4)
                            mm = pe.matmul(dst[:, at:at + SC], qs[p][0:K1, t // 4, h, t % 4 * P:(t % 4 + 1) * P],
                                           ks[p][0:K1, h, :], start=True, stop=True)
                    else:
                        n = (t + 1) * P if causal else S
                        for a in range(0, n, 512):
                            b = min(n, a + 512)
                            diag = causal and b == n
                            mm = pe.matmul(dst[:, a:b], qs[p][0:K1, t // 4, h, t % 4 * P:(t % 4 + 1) * P],
                                           ks[p][0:K1, a // 512, h, 0:b - a], start=True, stop=not diag)
                            if diag:
                                mm = pe.matmul(dst[:, n - P:n], G["identb"][:], G["maskS"][:], start=False, stop=True)
                    mm.then_inc(s_ready, 1)

                def rows_units(front, first, last):
                    for s in range(first, last):
                        rows_unit(front, s)
                        if n_turns == 2 and s == NS // 2:
                            turn_max(front, 0)

                def turn_max(front, w):
                    g = front[0]
                    pe.wait_ge(s_free, g * NS + (w + 1) * NS // n_turns)
                    part = (mx[:] if n_turns == 1 else mx[:, w:w + 1]).rearrange("p a h t -> p (a h t)")
                    pe.transpose(ps1[1][0:TR, 0:P], part, G["ident"][:]).then_inc(mt_ready, 1)

                def cols_unit(back, u):
                    g, p, r = back
                    qh, i, c0 = ugs[u // H]
                    h = u % H
                    k0, rows = KT[i]
                    dst = ps2[u % 2]
                    if u >= 2:
                        pe.wait_ge(ex_done, g * NST + u - 1)
                    if u == 0 or (u == HALF and n_turns == 2):
                        pe.wait_ge(mld[p][u // HALF], 16 * 3 * (r + 1))
                    diag = causal and k0 >= 512 * qh
                    keys = ks[p][0:K2, h, :] if cross else ks[p][0:K2, k0 // 512, h, k0 % 512:k0 % 512 + rows]
                    mm = pe.matmul(dst[0:rows, 0:512 - c0], keys,
                                   qs[p][0:K2, qh, h, c0:512], start=True, stop=not diag)
                    if diag:
                        mm = pe.matmul(dst[:, 0:P], G["identb"][:], G["maskT"][:], start=False, stop=True)
                    mm.then_inc(st_ready, 1)

                def values_unit(back, ug, part=None):
                    g, p, r = back
                    qh, i, c0 = ugs[ug]
                    rows = KT[i][1]
                    last = ug + 1 == NUG or ugs[ug + 1][0] != qh
                    if part != 1:
                        pe.wait_ge(ex_done, g * NST + (ug + 1) * H)
                        if ug == 0:
                            wait(pe, o_copied, g)
                    whole = part is None or i == 0
                    mid = (c0 + 512) // 2
                    a, b = (c0, 512) if whole else ((c0, mid) if part == 0 else (mid, 512))
                    if not (part == 1 and whole):
                        for h in range(H):
                            mm = pe.matmul(psO[32 * h:32 * h + hd + 1, 512 * qh + a:512 * qh + b],
                                           vs[p][0:rows, i, h, :], pr[ug % RING][0:rows, h, a:b],
                                           start=(i == 0), stop=last and (whole or part == 1))
                        if whole or part == 1:
                            mm.then_inc(pv_done, 1)

                def spread_sums(g):
                    pe.wait_ge(o_copied, g + 1)
                    for a in range(0, S, 512):
                        mm = pe.matmul(ps1[0][:, a:a + 512], G["sel16"][:], osb[:, a:a + 512], start=True, stop=True)
                    mm.then_inc(lb_ready, 1)

                def step(front, back):
                    if front and (cross or not back):
                        pe.wait_ge(ld[front[1]], 16 * n_ld * (front[2] + 1))
                        rows_units(front, 0, NS)
                    if not back:
                        turn_max(front, n_turns - 1)
                        return
                    g = back[0]
                    later = not isinstance(g, int) or g > 0
                    s = 0
                    for u in range(NST):
                        cols_unit(back, u)
                        if cross:
                            if u == H - 1:
                                if front:
                                    turn_max(front, 0)
                                if later:
                                    spread_sums(g - 1)
                            if u % H == H - 1 and u >= H:
                                values_unit(back, u // H - 1)
                            continue
                        if u % 2 and u >= H:
                            values_unit(back, u // H - 1, u % H // 2)
                        if front and due[u] > s:
                            if s == 0:
                                pe.wait_ge(ld[front[1]], 16 * n_ld * (front[2] + 1))
                            rows_units(front, s, due[u])
                            s = due[u]
                    values_unit(back, NUG - 1)
                    if front and not cross:
                        turn_max(front, 1)
                    if not front and cross:
                        spread_sums(g)

                in_thirds(pe, n_groups, step)

            @block.scalar
            def _(act):
                def step(front, back):
                    if not back:
                        return
                    g, p, r = back
                    for u in range(NST):
                        ug, h = u // H, u % H
                        qh, i, c0 = ugs[ug]
                        rows = KT[i][1]
                        act.wait_ge(st_ready, g * NST + u + 1)
                        if h == 0 and ug >= RING:
                            act.wait_ge(pv_done, g * NUG + ug - RING + 1)
                        act.activation(pr[ug % RING][0:rows, h, c0:512], ps2[u % 2][0:rows, 0:512 - c0], ACT.Exp,
                                       scale=scale).then_inc(ex_done, 1)
                    act.wait_ge(pv_done, (g + 1) * NUG)
                    wait(act, o_done, g)
                    act.activation(osb[:], psO[:], ACT.Copy).then_inc(o_copied, 1)

                in_thirds(act, n_groups, step)

            @block.vector
            def _(dve):
                for p in range(3):
                    dve.memset(ks[p][base:K2], 1.0)
                    dve.memset(qs[p][base:K2], 1.0)
                if sums is not None:
                    dve.memset(rec[:], 0.0)
                dve.memset(psO[:], 0.0)
                dve.drain()
                dve.memset(G["tick"][:], 0.0).then_inc(ones_set, 1)

                def invert_sums(g):
                    if sums is not None:
                        dve.wait_ge(sums_in, 16 * (g + 1))
                        wait(dve, inv_out, 16 * g)
                        dve.reciprocal(inv[:], sm[:]).then_inc(rec_done, 1)
                        return
                    dve.wait_ge(lb_ready, g + 1)
                    wait(dve, o_done, g)
                    dve.reciprocal(rec[:], ps1[0][:]).then_inc(rec_done, 1)

                def negate_max(front, w):
                    g, p, r = front
                    wait(dve, mld[p][w], 16 * 3 * r)
                    dve.wait_ge(mt_ready, n_turns * g + w + 1)
                    dve.tensor_scalar(neg[:], ps1[1][0:TR, 0:P], -1.0, None, ALU.mult).then_inc(mt_done, 1)
                    dve.drain()
                    parts = nparts[p][w]
                    dve.tensor_copy(parts[:, 0, :], neg[:])
                    dve.drain()
                    dve.tensor_tensor(nres[:], neg[:], parts[:, 0, :], ALU.subtract)
                    dve.drain()
                    dve.tensor_copy(parts[:, 1, :], nres[:])
                    dve.drain()
                    dve.tensor_tensor(parts[:, 2, :], nres[:], parts[:, 1, :], ALU.subtract).then_inc(neg_ready, 1)

                def maxima(front, invert=None):
                    g, p, r = front
                    for s, (t, h) in enumerate(units1):
                        if invert is not None and s == INVERT_AT:
                            invert_sums(invert)
                        dve.wait_ge(s_ready, g * NS + s + 1)
                        if cross:
                            view = ps1[s % 2][:].rearrange("p (a n) -> p a n", a=2)[:, :, 0:4 * SC]
                            dve.tensor_reduce(mx[:, :, h, :], view.rearrange("p a (b n) -> p a b n", b=4), AX.X,
                                              ALU.max).then_inc(s_free, 1)
                        else:
                            n = (t + 1) * P if causal else S
                            at = mx[:, t // 4, h, t % 4:t % 4 + 1]
                            dve.tensor_reduce(at, ps1[s % 2][:, 0:n], AX.X, ALU.max).then_inc(s_free, 1)
                        if n_turns == 2 and s == NS // 2:
                            negate_max(front, 0)
                    negate_max(front, n_turns - 1)

                def step(front, back):
                    later = back and (not isinstance(back[0], int) or back[0] > 0)
                    if front and cross:
                        maxima(front)
                        if later:
                            invert_sums(back[0] - 1)
                    elif front:
                        maxima(front, back[0] - 1 if later else None)
                    else:
                        invert_sums(back[0] - 1)
                        invert_sums(back[0])

                in_thirds(dve, n_groups, step)


def wide_attention_stage(nc, G, tag, *, q, k, v, o):
    hd = 64
    n_groups = HEADS * B
    QT = S // P
    scale = float(hd) ** -0.5
    NS = QT
    NST = 2 * QT
    RING = 8
    NADD = NST - 2
    added_at = lambda u: u + 1 if u < 2 else u - 1
    FIRST_ROWS, LAST_ROWS = 5, 13
    due = [min(NS, max(0, -(-NS * (u + 1 - FIRST_ROWS) // (LAST_ROWS - FIRST_ROWS)))) for u in range(NST)]
    TURN = LAST_ROWS + 1

    with Stage(nc, tag) as st:
        qs, ks = st.sb("qs", [hd, S], BF16), st.sb("ks", [hd, S], BF16)
        qf = [st.sb(f"qf{p}", [65, S]) for p in range(2)]
        kf = [st.sb(f"kf{p}", [65, S]) for p in range(2)]
        vs = [st.sb(f"vs{p}", [P, QT, hd + 1]) for p in range(2)]
        pr = [st.sb(f"probs{r}", [P, 512]) for r in range(RING)]
        sums = [st.sb(f"sums{h}", [P, 512]) for h in range(2)]
        osb = st.sb("osb", [P, 512])
        rec = st.sb("rec", [P, 512])
        on = [st.sb(f"on{p}", [P, 512]) for p in range(2)]
        mx = st.sb("mx", [P, QT])
        neg = [st.sb(f"neg{p}", [QT, P]) for p in range(2)]
        ps1 = [st.ps(f"rows{p}", [P, S]) for p in range(2)]
        ps2 = [st.ps(f"cols{p}", [P, 512]) for p in range(2)]
        psO = st.ps("out", [P, 512])
        psL = st.ps("sums_spread", [P, 512])
        ld = [st.sem(f"loaded{p}") for p in range(2)]
        vld = [st.sem(f"values_loaded{p}") for p in range(2)]
        mld = [st.sem(f"max_placed{p}") for p in range(2)]
        ones_set, cast = st.sem("ones_set"), st.sem("cast")
        s_ready, s_free = st.sem("rows_ready"), st.sem("rows_free")
        mt_ready, neg_ready = st.sem("max_turned"), st.sem("neg_ready")
        st_ready, ex_done, pv_done = st.sem("cols_ready"), st.sem("exp_done"), st.sem("pv_done")
        added, lb_ready = st.sem("exp_added"), st.sem("sums_ready")
        o_copied, rec_done, o_done = st.sem("out_copied"), st.sem("sums_inverted"), st.sem("out_done")
        stored = [st.sem(f"stored{p}") for p in range(2)]
        n_ld = 2

        with st.block() as block:
            @block.sync
            def _(sp):
                sp.wait_ge(ones_set, 1)

                def step(front, back):
                    if front:
                        g, p, r = front
                        feats, cols = bass.ds(r * 64, 64), slice(p * S, (p + 1) * S)
                        wait(sp, st_ready, (g - 1) * NST)
                        sp.dma_start(kf[p][0:64, :], k[feats, cols]).then_inc(ld[p], 16)
                        sp.dma_start(qf[p][0:64, :], q[feats, cols]).then_inc(ld[p], 16)
                        wait(sp, pv_done, (g - 1) * QT)
                        sp.dma_start(vs[p][:].rearrange("p t x -> p (t x)"),
                                     v[bass.ds(r, 1), :, p * QT:(p + 1) * QT, :].rearrange("g p t x -> p (g t x)")
                                     ).then_inc(vld[p], 16)
                        sp.wait_ge(neg_ready, g + 1)
                        sp.dma_start(qf[p][64:65, :].rearrange("p (t q) -> p t q", q=P),
                                     neg[p][:]).then_inc(mld[p], 16)

                two_halves(sp, n_groups, step)

            @block.gpsimd
            def _(pool):
                def step(front, back):
                    if back:
                        g, p, r = back
                        for u in range(2, NST):
                            i, h = u // 2, u % 2
                            if i == 1:
                                wait(pool, lb_ready, g)
                            elif h == 0:
                                pool.drain()
                            pool.wait_ge(ex_done, g * NST + u + 1)
                            pool.tensor_tensor(sums[h][:], pr[h][:] if i == 1 else sums[h][:], pr[u % RING][:],
                                               ALU.add).then_inc(added, 1)
                            if u == NST // 2 and (not isinstance(g, int) or g > 0):
                                store(g - 1, 1 - p, r if p else r - 1)
                        if not front:
                            store(g, p, r)

                def store(g, p, r):
                    pool.wait_ge(o_done, g + 1)
                    for h in range(2):
                        pool.dma_start(o[bass.ds(r * 64, 64), p * S + 512 * h:p * S + 512 * (h + 1)],
                                       on[p][64 * h:64 * (h + 1), :]).then_inc(stored[p], 16)

                two_halves(pool, n_groups, step)
                for p in range(2):
                    pool.wait_ge(stored[p], n_groups // 2 * 2 * 16)

            @block.tensor
            def _(pe):
                pe.wait_ge(ones_set, 1)

                def rows_unit(front, s):
                    g, p, r = front
                    if s == 0:
                        pe.wait_ge(cast, g + 1)
                    if s >= 2:
                        pe.wait_ge(s_free, g * NS + s - 1)
                    elif s == 1:
                        wait(pe, neg_ready, g)
                    else:
                        wait(pe, s_free, g * NS - 1)
                    for a in range(0, S, 512):
                        mm = pe.matmul(ps1[s % 2][:, a:a + 512], qs[:, s * P:(s + 1) * P], ks[:, a:a + 512],
                                       start=True, stop=True)
                    mm.then_inc(s_ready, 1)

                def turn_max(front):
                    pe.wait_ge(s_free, (front[0] + 1) * NS)
                    pe.transpose(ps1[1][0:QT, 0:P], mx[:], G["ident"][:]).then_inc(mt_ready, 1)

                def cols_unit(back, u):
                    g, p, r = back
                    i, h = u // 2, u % 2
                    if u >= 2:
                        pe.wait_ge(ex_done, g * NST + u - 1)
                    pe.matmul(ps2[u % 2][:], kf[p][:, i * P:(i + 1) * P], qf[p][:, 512 * h:512 * (h + 1)],
                              start=True, stop=True).then_inc(st_ready, 1)

                def values_unit(back, i):
                    g, p, r = back
                    pe.wait_ge(ex_done, g * NST + 2 * i + 2)
                    if i == 0:
                        pe.wait_ge(vld[p], 16 * (r + 1))
                        wait(pe, o_copied, g)
                    for h in range(2):
                        mm = pe.matmul(psO[64 * h:64 * (h + 1), :], vs[p][:, i, 0:hd], pr[(2 * i + h) % RING][:],
                                       start=(i == 0), stop=(i == QT - 1))
                    mm.then_inc(pv_done, 1)

                def spread_sums(g):
                    pe.wait_ge(added, (g + 1) * NADD)
                    wait(pe, rec_done, g)
                    for h in range(2):
                        mm = pe.matmul(psL[64 * h:64 * (h + 1), :], G["ones"][:, 0:64], sums[h][:],
                                       start=True, stop=True)
                    mm.then_inc(lb_ready, 1)

                def step(front, back):
                    if not back:
                        for s in range(NS):
                            rows_unit(front, s)
                        turn_max(front)
                        return
                    g, p, r = back
                    later = not isinstance(g, int) or g > 0
                    s = 0
                    pe.wait_ge(mld[p], 16 * (r + 1))
                    for u in range(NST):
                        cols_unit(back, u)
                        if u == 1 and later:
                            spread_sums(g - 1)
                        if u % 2 and u >= 3:
                            values_unit(back, u // 2 - 1)
                        if front:
                            for s in range(s, due[u]):
                                rows_unit(front, s)
                            s = due[u]
                            if u == TURN:
                                turn_max(front)
                    values_unit(back, QT - 1)
                    if not front:
                        spread_sums(g)

                two_halves(pe, n_groups, step)

            @block.scalar
            def _(act):
                def step(front, back):
                    if not back:
                        return
                    g, p, r = back
                    for u in range(NST):
                        act.wait_ge(st_ready, g * NST + u + 1)
                        if u >= RING:
                            act.wait_ge(pv_done, g * QT + (u - RING) // 2 + 1)
                            act.wait_ge(added, g * NADD + added_at(u - RING))
                        elif not isinstance(g, int) or g > 0:
                            last = max(w for w in range(NST) if w % RING == u)
                            act.wait_ge(pv_done, g * QT - QT + last // 2 + 1)
                            act.wait_ge(added, g * NADD - NADD + added_at(last))
                        act.activation(pr[u % RING][:], ps2[u % 2][:], ACT.Exp, scale=scale).then_inc(ex_done, 1)
                    act.wait_ge(pv_done, (g + 1) * QT)
                    wait(act, o_done, g)
                    act.activation(osb[:], psO[:], ACT.Copy).then_inc(o_copied, 1)

                two_halves(act, n_groups, step)

            @block.vector
            def _(dve):
                for p in range(2):
                    dve.memset(kf[p][64:65, :], 1.0)
                dve.drain()
                dve.memset(G["tick"][:], 0.0).then_inc(ones_set, 1)

                def normalize(g, p, r):
                    dve.wait_ge(lb_ready, g + 1)
                    dve.reciprocal(rec[:], psL[:]).then_inc(rec_done, 1)
                    dve.drain()
                    wait(dve, stored[p], r * 2 * 16)
                    dve.wait_ge(o_copied, g + 1)
                    dve.tensor_tensor(on[p][:], osb[:], rec[:], ALU.mult).then_inc(o_done, 1)

                def step(front, back):
                    if front:
                        g, p, r = front
                        if back and (not isinstance(g, int) or g > 1):
                            normalize(g - 2, p, r - 1)
                        dve.wait_ge(ld[p], 16 * n_ld * (r + 1))
                        wait(dve, s_ready, g * NS)
                        dve.tensor_copy(qs[:], qf[p][0:hd, :])
                        dve.tensor_copy(ks[:], kf[p][0:hd, :]).then_inc(cast, 1)
                        for s in range(NS):
                            dve.wait_ge(s_ready, g * NS + s + 1)
                            dve.tensor_reduce(mx[:, s:s + 1], ps1[s % 2][:], AX.X, ALU.max).then_inc(s_free, 1)
                        wait(dve, mld[p], 16 * r)
                        dve.wait_ge(mt_ready, g + 1)
                        dve.tensor_scalar(neg[p][:], ps1[1][0:QT, 0:P], -1.0, None, ALU.mult).then_inc(neg_ready, 1)
                    elif back:
                        g, p, r = back
                        normalize(g - 1, 1 - p, r)
                        normalize(g, p, r)

                two_halves(dve, n_groups, step)



def n_pieces(K):
    n = K * T // R + E - 1
    return n + n % 2


def route_stage(nc, G, tag, K, rows, sorted_rows, table, place, weight):
    NJ = n_pieces(K)
    KN = K * NT
    with Stage(nc, tag) as st:
        lg = G["logits"]
        iota_i, iota = st.sb("iota_i", [P, NT, E], I32), st.sb("iota", [P, NT, E])
        start_i, starts = st.sb("start_i", [P, NJ], I32), st.sb("starts", [P, NJ])
        top = st.sb("top", [P, K, NT])
        eq, cand, l2 = st.sb("eq", [P, NT, E]), st.sb("cand", [P, NT, E]), st.sb("l2", [P, NT, E])
        first = st.sb("first", [P, NT])
        oh = st.sb("onehot", [P, KN, E])
        tot = [st.sb(f"tot{i}", [P, KN, E]) for i in range(2)]
        count, count_i = st.sb("count", [P, E]), st.sb("count_i", [P, E], I32)
        basee = st.sb("base", [P, E])
        pos = st.sb("pos", [P, KN, E])
        posr = st.sb("posr", [P, KN])
        ex, owner = st.sb("ex", [P, NT]), st.sb("owner", [P, NJ])
        ge = st.sb("ge", [P, NJ])
        zero = st.sb("zero", [P, 2, D])
        psB, psT_ = st.ps("before", [P, KN * E]), st.ps("totals", [P, KN * E])
        iotas, oh_ready, counted = st.sem("iotas"), st.sem("oh_ready"), st.sem("counted")
        exp_in, exp_out = st.sem("exp_in"), st.sem("exp_out")
        zeroed, cleared, placed, sent = st.sem("zeroed"), st.sem("cleared"), st.sem("placed"), st.sem("sent")

        with st.block() as block:
            @block.gpsimd
            def _(pool):
                pool.iota(iota_i[:], pattern=[[0, NT], [1, E]], base=0, channel_multiplier=0)
                pool.iota(start_i[:], pattern=[[R, NJ]], base=0, channel_multiplier=0).then_inc(iotas, 1)
                pool.wait_ge(placed, 1)
                pool.wait_ge(cleared, NJ * 16)
                for k in range(K):
                    for t in range(NT):
                        pool.indirect_dma_start(
                            sorted_rows, bass.IndirectOffsetOnAxis(ap=place[:, k * NT + t:k * NT + t + 1], axis=0),
                            rows[:, t, :], None).then_inc(sent, 16)
                pool.wait_ge(sent, K * NT * 16)

            @block.sync
            def _(sp):
                sp.wait_ge(zeroed, 1)
                for j in range(NJ):
                    sp.dma_start(sorted_rows[j * R:(j + 1) * R, :].rearrange("(t p) d -> p t d", p=P), zero[:]
                                 ).then_inc(cleared, 16)
                sp.wait_ge(cleared, NJ * 16)

            @block.tensor
            def _(pe):
                pe.wait_ge(oh_ready, 1)
                flat = oh[:].rearrange("p s e -> p (s e)")
                pe.matmul(psB[:], G["lower"][:], flat, start=True, stop=True)
                pe.matmul(psT_[:], G["ones"][:], flat, start=True, stop=True).then_inc(counted, 1)

            @block.scalar
            def _(act):
                act.wait_ge(exp_in, 1)
                act.activation(ex[:], first[:], ACT.Exp).then_inc(exp_out, 1)

            @block.vector
            def _(dve):
                def op(ins):
                    dve.drain()

                op(dve.memset(zero[:], 0.0))
                dve.memset(G["tick"][:], 0.0).then_inc(zeroed, 1)
                dve.wait_ge(iotas, 1)
                op(dve.tensor_copy(iota[:], iota_i[:]))
                op(dve.tensor_copy(starts[:], start_i[:]))
                op(dve.tensor_copy(l2[:], lg[:]))
                for k in range(K):
                    sel = oh[:, k * NT:(k + 1) * NT, :]
                    op(dve.tensor_reduce(top[:, k, :], l2[:], AX.X, ALU.max))
                    op(dve.tensor_tensor(eq[:], l2[:], top[:, k, :].unsqueeze(2).broadcast_to([P, NT, E]), ALU.is_equal))
                    op(dve.tensor_scalar(cand[:], iota[:], -float(E), None, ALU.add))
                    op(dve.tensor_tensor(cand[:], cand[:], eq[:], ALU.mult))
                    op(dve.tensor_reduce(first[:], cand[:], AX.X, ALU.min))
                    op(dve.tensor_scalar(first[:], first[:], float(E), None, ALU.add))
                    op(dve.tensor_tensor(sel, iota[:], first[:].unsqueeze(2).broadcast_to([P, NT, E]), ALU.is_equal))
                    if k + 1 < K:
                        op(dve.scalar_tensor_tensor(l2[:].rearrange("p t e -> p (t e)"), sel.rearrange("p t e -> p (t e)"),
                                                    NEG, l2[:].rearrange("p t e -> p (t e)"), ALU.mult, ALU.add))
                dve.memset(G["tick"][:], 0.0).then_inc(oh_ready, 1)
                if K == 1:
                    op(dve.tensor_scalar(first[:], top[:, 0, :], -1.0, None, ALU.mult))
                else:
                    op(dve.tensor_tensor(first[:], top[:, 1, :], top[:, 0, :], ALU.subtract))
                dve.memset(G["tick"][:], 0.0).then_inc(exp_in, 1)
                dve.wait_ge(counted, 1)
                op(dve.tensor_copy(tot[0][:].rearrange("p s e -> p (s e)"), psT_[:]))
                a, d = 0, 1
                while d < KN:
                    dve.tensor_copy(tot[1 - a][:, 0:d, :], tot[a][:, 0:d, :])
                    op(dve.tensor_tensor(tot[1 - a][:, d:, :], tot[a][:, d:, :], tot[a][:, 0:KN - d, :], ALU.add))
                    a, d = 1 - a, 2 * d
                op(dve.tensor_scalar(count_i[:], tot[a][:, KN - 1, :], float(R - 1), None, ALU.add))
                shift = R.bit_length() - 1
                op(dve.tensor_scalar(count_i[:], count_i[:], shift, shift, ALU.logical_shift_right,
                                     ALU.logical_shift_left))
                op(dve.tensor_copy(count[:], count_i[:]))
                op(dve.memset(basee[:], 0.0))
                for e in range(1, E):
                    op(dve.tensor_tensor(basee[:, e:e + 1], basee[:, e - 1:e], count[:, e - 1:e], ALU.add))
                op(dve.tensor_tensor(pos[:], psB[:].rearrange("p (s e) -> p s e", e=E),
                                     basee[:].unsqueeze(1).broadcast_to([P, KN, E]), ALU.add))
                op(dve.tensor_tensor(pos[:, 1:, :], pos[:, 1:, :], tot[a][:, 0:KN - 1, :], ALU.add))
                op(dve.tensor_tensor(pos[:], pos[:], oh[:], ALU.mult))
                op(dve.tensor_reduce(posr[:], pos[:], AX.X, ALU.add))
                op(dve.tensor_copy(place[:], posr[:]))
                dve.memset(G["tick"][:], 0.0).then_inc(placed, 1)
                op(dve.memset(owner[:], 0.0))
                for e in range(1, E):
                    op(dve.tensor_scalar(ge[:], starts[:], basee[:, e:e + 1], None, ALU.is_ge))
                    op(dve.tensor_tensor(owner[:], owner[:], ge[:], ALU.add))
                op(dve.tensor_copy(table[:], owner[0:1, :]))
                dve.wait_ge(exp_out, 1)
                op(dve.tensor_scalar(first[:], ex[:], 1.0, None, ALU.add))
                op(dve.reciprocal(weight[:, 0, :], first[:]))
                if K == 2:
                    op(dve.tensor_tensor(weight[:, 1, :], ex[:], weight[:, 0, :], ALU.mult))


def expert_stage(nc, G, tag, K, sorted_rows, results, table, *, F, w1, w2, w3=None, b1=None, b2=None, g=None, b=None):
    NJ = n_pieces(K)
    NF = F // P
    RT = R // P
    UP = NF * (2 if w3 is not None else 1)
    affine = g is not None
    with Stage(nc, tag) as st:
        xg = [st.sb(f"xg{p}", [P, RT, D]) for p in range(2)]
        xT = [st.sb(f"xT{p}", [P, KD, R]) for p in range(2)]
        w1s = [st.sb(f"w1_{p}", [P, KD, F]) for p in range(2)]
        w3s = [st.sb(f"w3_{p}", [P, KD, F]) for p in range(2)] if w3 is not None else None
        w2s = [st.sb(f"w2_{p}", [P, NF, D]) for p in range(2)]
        if affine:
            gb = [st.sb(f"gb{p}", [P, 2, KD]) for p in range(2)]
            b1s = [st.sb(f"b1_{p}", [P, NF]) for p in range(2)]
            b2s = [st.sb(f"b2_{p}", [P, RT, D]) for p in range(2)]
        gate = st.sb("gated", [P, 2, R])
        h = [st.sb(f"h{p}", [P, NF, R]) for p in range(2)]
        yo = [st.sb(f"y{p}", [P, RT, D]) for p in range(2)]
        psX = [st.ps(f"psX{p}", [P, RT, KD, P]) for p in range(2)]
        psU = [st.ps(f"psU{i}", [P, 512]) for i in range(4)]
        psD = [st.ps(f"psD{p}", [P, RT, D]) for p in range(2)]
        ld = [st.sem(f"loaded{p}") for p in range(2)]
        turned, xT_ready = st.sem("turned"), st.sem("xT_ready")
        u_ready, u_free, gated = st.sem("up_ready"), st.sem("up_free"), st.sem("gate_ready")
        d_ready, y_ready = st.sem("down_ready"), st.sem("y_ready")
        stored = [st.sem(f"stored{p}") for p in range(2)]
        n_ld = 16 * (4 if not affine else 8)

        with st.block() as block:
            @block.sync
            def _(sp):
                def step(front, back):
                    if front:
                        j, p, r = front
                        e = sp.value_load(table[0:1, bass.ds(j, 1)], min_val=0, max_val=E - 1)
                        wait(sp, d_ready, j - 1)
                        sp.dma_start(xg[p][:], sorted_rows[bass.ds(j * R, R), :].rearrange("(t p) d -> p t d", p=P)
                                     ).then_inc(ld[p], 16)
                        pairs = [(w1s[p], w1)] + ([(w3s[p], w3)] if w3 is not None else []) + [(w2s[p], w2)]
                        for dst, src in pairs:
                            sp.dma_start(dst[:], src[bass.ds(e, 1), :, :].rearrange("e (k p) n -> p (e k) n", p=P)
                                         ).then_inc(ld[p], 16)
                        if affine:
                            for i, src in enumerate((g, b)):
                                sp.dma_start(gb[p][:, i, :], src[bass.ds(e, 1), :, :].rearrange("e p k -> p (e k)")
                                             ).then_inc(ld[p], 16)
                            sp.dma_start(b1s[p][:], b1[bass.ds(e, 1), :, :].rearrange("e p k -> p (e k)")
                                         ).then_inc(ld[p], 16)
                            for t in range(RT):
                                sp.dma_start(b2s[p][:, t, :], b2[bass.ds(e, 1), :].broadcast_to([P, D])
                                             ).then_inc(ld[p], 16)
                    if back:
                        j, p, r = back
                        sp.wait_ge(y_ready, j + 1)
                        sp.dma_start(results[bass.ds(j * R, R), :].rearrange("(t p) d -> p t d", p=P), yo[p][:]
                                     ).then_inc(stored[p], 16)

                two_halves(sp, NJ, step)
                for p in range(2):
                    sp.wait_ge(stored[p], NJ // 2 * 16)

            @block.tensor
            def _(pe):
                def step(front, back):
                    if back:
                        j, p, r = back
                        pe.wait_ge(xT_ready, j + 1)
                        for n in range(UP):
                            if not (isinstance(j, int) and j == 0 and n < 4):
                                pe.wait_ge(u_free, j * UP + n - 3)
                            ws = w1s if w3 is None or n % 2 == 0 else w3s
                            m = n if w3 is None else n // 2
                            for k in range(KD):
                                mm = pe.matmul(psU[n % 4][:, 0:R], ws[p][:, k, m * P:(m + 1) * P], xT[p][:, k, :],
                                               start=(k == 0), stop=(k == KD - 1))
                            mm.then_inc(u_ready, 1)
                        pe.wait_ge(u_free, (j + 1) * UP)
                        wait(pe, y_ready, j - 1)
                        for t in range(RT):
                            for m in range(NF):
                                mm = pe.matmul(psD[p][:, t, :], h[p][:, m, t * P:(t + 1) * P], w2s[p][:, m, :],
                                               start=(m == 0), stop=(m == NF - 1))
                        mm.then_inc(d_ready, 1)
                    if front:
                        j, p, r = front
                        pe.wait_ge(ld[p], n_ld * (r + 1))
                        wait(pe, xT_ready, j - 1)
                        for t in range(RT):
                            for k in range(KD):
                                mm = pe.transpose(psX[p][:, t, k, :], xg[p][:, t, k * P:(k + 1) * P], G["ident"][:])
                        mm.then_inc(turned, 1)

                two_halves(pe, NJ, step)

            @block.scalar
            def _(act):
                def step(front, back):
                    if back:
                        j, p, r = back
                        for m in range(NF if w3 is not None else 0):
                            act.wait_ge(u_ready, j * UP + 2 * m + 1)
                            if m >= 2:
                                act.wait_ge(u_free, j * UP + 2 * (m - 1))
                            act.activation(gate[:, m % 2, :], psU[2 * m % 4][:, 0:R], ACT.Silu).then_inc(gated, 1)
                    if front:
                        j, p, r = front
                        act.wait_ge(turned, j + 1)
                        wait(act, d_ready, j - 1)
                        for k in range(KD):
                            dst = xT[p][:, k, :].rearrange("p (t q) -> p t q", q=P)
                            if affine:
                                ins = act.activation(dst, psX[p][:, :, k, :], ACT.Identity, scale=gb[p][:, 0, k:k + 1],
                                                     bias=gb[p][:, 1, k:k + 1])
                            else:
                                ins = act.activation(dst, psX[p][:, :, k, :], ACT.Copy)
                        ins.then_inc(xT_ready, 1)

                two_halves(act, NJ, step)

            @block.vector
            def _(dve):
                def step(front, back):
                    if not back:
                        return
                    j, p, r = back
                    if w3 is None:
                        for n in range(UP):
                            dve.wait_ge(u_ready, j * UP + n + 1)
                            dve.tensor_scalar(h[p][:, n, :], psU[n % 4][:, 0:R], b1s[p][:, n:n + 1], 0.0, ALU.add,
                                              ALU.max).then_inc(u_free, 1)
                    else:
                        for m in range(NF):
                            dve.wait_ge(gated, j * NF + m + 1)
                            dve.wait_ge(u_ready, j * UP + 2 * m + 2)
                            dve.tensor_tensor(h[p][:, m, :], psU[(2 * m + 1) % 4][:, 0:R], gate[:, m % 2, :],
                                              ALU.mult).then_inc(u_free, 2)
                    dve.wait_ge(d_ready, j + 1)
                    wait(dve, stored[p], 16 * r)
                    if affine:
                        dve.tensor_tensor(yo[p][:], psD[p][:], b2s[p][:], ALU.add).then_inc(y_ready, 1)
                    else:
                        dve.tensor_copy(yo[p][:], psD[p][:]).then_inc(y_ready, 1)

                two_halves(dve, NJ, step)


def combine_stage(nc, G, tag, K, results, place, weight, add, out=None):
    with Stage(nc, tag) as st:
        got = st.sb("got", [P, K * NT, D])
        fetched, ready, stored = st.sem("fetched"), st.sem("ready"), st.sem("stored")
        X = G["X"]
        with st.block() as block:
            @block.gpsimd
            def _(pool):
                for t in range(NT):
                    for k in range(K):
                        pool.indirect_dma_start(
                            got[:, t * K + k, :], None, results,
                            bass.IndirectOffsetOnAxis(ap=place[:, k * NT + t:k * NT + t + 1], axis=0)
                        ).then_inc(fetched, 16)

            @block.vector
            def _(dve):
                dve.tensor_tensor(X[:], X[:], add[:], ALU.add)
                dve.drain()
                dve.wait_ge(fetched, 16 * K * NT)
                for k in range(K):
                    for t in range(NT):
                        ins = dve.scalar_tensor_tensor(X[:, t, :], got[:, t * K + k, :], weight[:, k, t:t + 1],
                                                       X[:, t, :], ALU.mult, ALU.add)
                        if k == K - 1:
                            ins.then_inc(ready, 1)
                    dve.drain()

            @block.sync
            def _(sp):
                if out is not None:
                    for t in range(NT):
                        sp.wait_ge(ready, t + 1)
                        sp.dma_start(out[t * P:(t + 1) * P, :], X[:, t, :]).then_inc(stored, 16)
                    sp.wait_ge(stored, 16 * NT)



def decoder(nc, A, out):
    G = {"cos": A["cos"], "sin": A["sin"]}
    Q16 = nc.dram_tensor("q16_scratch", (3, HEADS // 4, 2 * B, 64, 512), BF16, kind="Internal").ap()
    K16 = nc.dram_tensor("k16_scratch", (3, HEADS // 4, 2 * B, 64, 512), BF16, kind="Internal").ap()
    V16 = nc.dram_tensor("v16_scratch", (HEADS // 4, 2 * B, P, 4, 4 * 17), F32, kind="Internal").ap()
    QKW = nc.dram_tensor("qk_wide_scratch", (2048, T), F32, kind="Internal").ap()
    VW = nc.dram_tensor("vw_scratch", (HEADS, P, NT, 65), F32, kind="Internal").ap()
    CK = [nc.dram_tensor(f"ctx_k_scratch{i}", (3, HEADS // 4, B, 64, SC), BF16, kind="Internal").ap() for i in range(2)]
    CV = [nc.dram_tensor(f"ctx_v_scratch{i}", (HEADS // 4, B, SC, 4 * 17), F32, kind="Internal").ap() for i in range(2)]
    CM = nc.dram_tensor("mask_scratch", (HEADS // 4 * B, 4, SC), BF16, kind="Internal").ap()
    OA = nc.dram_tensor("attn_scratch", (HEADS // 4, 2 * B, 64, 512), F32, kind="Internal").ap()
    SU = nc.dram_tensor("sums_scratch", (2, 3, 4 * S), F32, kind="Internal").ap()
    OW = nc.dram_tensor("attn_wide_scratch", (1024, T), F32, kind="Internal").ap()
    SR = nc.dram_tensor("sorted_scratch", (n_pieces(2) * R, D), F32, kind="Internal").ap()
    RE = nc.dram_tensor("results_scratch", (n_pieces(2) * R, D), F32, kind="Internal").ap()

    def units(*scratches):
        return [[scr[:, 2 * m + e] for e in range(2)] for scr in scratches for m in range(2)]

    a16 = dict(q=Q16, k=K16, v=V16, o=OA, sums=SU)

    with Stage(nc, "g") as g:
        for name in ("X", "Y", "Z"):
            G[name] = g.sb(name, [P, NT, D])
        G["ident"], G["lower"], G["ones"], G["sel16"] = (g.sb(n, [P, P]) for n in ("ident", "lower", "ones", "sel16"))
        G["sel64"] = g.sb("sel64", [P, 64])
        G["identb"], G["maskS"], G["maskT"] = (g.sb(n, [P, P], BF16) for n in ("identb", "maskSb", "maskTb"))
        G["eps"], G["tick"] = g.sb("eps", [P, 1]), g.sb("tick", [1, 1])
        G["logits"] = g.sb("logits", [P, NT, E])
        place = [g.sb(f"place{k}", [P, k * NT], I32) for k in (1, 2)]
        weight = [g.sb(f"weight{k}", [P, k, NT]) for k in (1, 2)]
        table = [g.sb(f"table{k}", [1, n_pieces(k)], I32) for k in (1, 2)]

        setup_stage(nc, G, A["x"])
        token_stage(nc, G, "t0", norm="ln", resid=G["X"], units=units(Q16, K16), rope=True, wf=A["wf0"], bf=A["bf0"],
                    wv=A["wv0"], bv=A["bv0"], outs=V16)
        attention_stage(nc, G, "a0", causal=True, **a16)
        context_stage(nc, G, "c1", A["ctxT"], A["wk1"], A["bk1"], A["wv1"], A["bv1"], A["mask"], CK[0], CV[0], CM)
        token_stage(nc, G, "t1", norm="ln", attn=(OA, A["wo0"], A["bo0"]), resid=G["X"], units=units(Q16),
                    wf=A["wq1"], bf=A["bq1"])
        attention_stage(nc, G, "a1", q=Q16, k=CK[0], v=CV[0], o=OA, cross=True, mask=CM)
        token_stage(nc, G, "t2", norm="ln_ln", attn=(OA, A["wo1"], A["bo1"]), resid=G["X"], gate=A["cent"])
        route_stage(nc, G, "r2", 1, G["Z"], SR[0:n_pieces(1) * R, :], table[0], place[0], weight[0])
        expert_stage(nc, G, "e2", 1, SR, RE, table[0], F=1024, w1=A["w1_2"], w2=A["w2_2"], b1=A["b1_2"], b2=A["b2_2"],
                     g=A["g_2"], b=A["b_2"])
        combine_stage(nc, G, "m2", 1, RE[0:n_pieces(1) * R, :], place[0], weight[0], G["Y"])
        token_stage(nc, G, "t3", norm="ln", resid=G["X"], units=[{}] * 16, wide=QKW, wf=A["wf3"],
                    bf=A["bf3"], wv=A["wv3"], bv=A["bv3"], outs=VW, heads_group=1, hd=64)
        wide_attention_stage(nc, G, "a3", q=QKW[0:1024], k=QKW[1024:2048], v=VW, o=OW)
        context_stage(nc, G, "c4", A["ctxT"], A["wk4"], A["bk4"], A["wv4"], A["bv4"], None, CK[1], CV[1], None)
        token_stage(nc, G, "t4", norm="ln", attn=(OW, A["wo3"], A["bo3"]), resid=G["X"], units=units(Q16),
                    wf=A["wq4"], bf=A["bq4"])
        attention_stage(nc, G, "a4", q=Q16, k=CK[1], v=CV[1], o=OA, cross=True)
        token_stage(nc, G, "t5", norm="ln_rms", attn=(OA, A["wo4"], A["bo4"]), resid=G["X"], units=units(Q16, K16),
                    wf=A["wf5"], fscale=A["ln1"], wv=A["wv5"], outs=V16)
        attention_stage(nc, G, "a5", **a16)
        token_stage(nc, G, "t6", norm="rms", attn=(OA, A["wo5"], None), resid=G["Y"], ln2=A["ln2"], gate=A["gate"])
        route_stage(nc, G, "r6", 2, G["Z"], SR, table[1], place[1], weight[1])
        expert_stage(nc, G, "e6", 2, SR, RE, table[1], F=512, w1=A["w1_6"], w3=A["w3_6"], w2=A["w2_6"])
        combine_stage(nc, G, "m6", 2, RE, place[1], weight[1], G["Y"], out)



def layout(inputs):
    a = {k: np.asarray(v) for k, v in inputs.items()}
    c = np.ascontiguousarray
    per_part = lambda v: c(v.reshape(-1, P).T)
    swap = np.arange(D) ^ 1
    w, bias = a["L0_attn_w_attn"], a["L0_attn_b_attn"]
    wq, wk, bq, bk = w[:, :D], w[:, D:2 * D], bias[:D], bias[D:2 * D]
    hd = D // HEADS
    inv = (np.float32(1.0) / np.float32(10000.0) ** (np.arange(0, hd, 2, dtype=np.float32) / np.float32(hd))
           ).astype(np.float32)
    freqs = np.repeat(np.arange(S, dtype=np.float32)[:, None] * inv[None, :], 2, axis=-1)
    sign = np.where(np.arange(hd) % 2 == 0, -1.0, 1.0).astype(np.float32)
    table = lambda t: c(np.tile(t.T.astype(np.float32), (P // hd, B)))
    out = {
        "x": c(a["x"].reshape(T, D)),
        "ctxT": c(a["ctx_1024"].reshape(B * SC, D).T),
        "mask": c(a["mask_Bx1xS2_if1"]),
        "cos": table(np.cos(freqs)), "sin": table(np.sin(freqs) * sign),
        "wf0": c(np.concatenate([wq, wk, wq[:, swap], wk[:, swap]], 1)),
        "bf0": per_part(np.concatenate([bq, bk, bq[swap], bk[swap]])),
        "wv0": c(w[:, 2 * D:]), "bv0": c(bias[2 * D:]),
        "wo0": a["L0_attn_w_proj"], "bo0": a["L0_attn_b_proj"],
        "wq1": c(a["L0_xattn_Wq"].T), "bq1": per_part(a["L0_xattn_bq"]),
        "wk1": c(a["L0_xattn_Wk"].T), "bk1": per_part(a["L0_xattn_bk"]),
        "wv1": c(a["L0_xattn_Wv"].T), "bv1": a["L0_xattn_bv"],
        "wo1": c(a["L0_xattn_Wo"].T), "bo1": a["L0_xattn_bo"],
        "cent": c(a["L0_ffn_centroids"].T),
        "w1_2": c(a["L0_ffn_w1"].transpose(0, 2, 1)), "w2_2": c(a["L0_ffn_w2"].transpose(0, 2, 1)),
        "b1_2": c(a["L0_ffn_b1"].reshape(E, -1, P).transpose(0, 2, 1)), "b2_2": a["L0_ffn_b2"],
        "g_2": c(a["L0_ffn_ln_g"].reshape(E, -1, P).transpose(0, 2, 1)),
        "b_2": c(a["L0_ffn_ln_b"].reshape(E, -1, P).transpose(0, 2, 1)),
        "wf3": c(a["L1_attn_W_qkv"][:, :2048]), "bf3": per_part(a["L1_attn_b_qkv"][:2048]),
        "wv3": c(a["L1_attn_W_qkv"][:, 2048:]), "bv3": c(a["L1_attn_b_qkv"][2048:]),
        "wo3": a["L1_attn_W_out"], "bo3": a["L1_attn_b_out"],
        "wq4": c(a["L1_xattn_w_q"].T), "bq4": per_part(a["L1_xattn_b_q"]),
        "wk4": c(a["L1_xattn_w_k"].T), "bk4": per_part(a["L1_xattn_b_k"]),
        "wv4": c(a["L1_xattn_w_v"].T), "bv4": a["L1_xattn_b_v"],
        "wo4": c(a["L1_xattn_w_o"].T), "bo4": a["L1_xattn_b_o"],
        "ln1": per_part(a["L1_ffn_ln1_w"]), "ln2": a["L1_ffn_ln2_w"],
        "wf5": c(np.concatenate([a["L1_ffn_wq"].T, a["L1_ffn_wk"].T], 1)), "wv5": c(a["L1_ffn_wv"].T),
        "wo5": c(a["L1_ffn_wo"].T), "gate": c(a["L1_ffn_gate_w"].T),
        "w1_6": c(a["L1_ffn_w1"].transpose(0, 2, 1)), "w3_6": c(a["L1_ffn_w3"].transpose(0, 2, 1)),
        "w2_6": c(a["L1_ffn_w2"].transpose(0, 2, 1)),
    }
    return out


def kernel(**inputs):
    import concourse.bacc as bacc
    from concourse.bass_utils import run_bass_kernel_spmd

    nc = bacc.Bacc("TRN2", target_bir_lowering=False, num_devices=1)
    arrays, args = {}, {}
    for name, a in layout(inputs).items():
        arrays[f"in_{name}"] = a
        args[name] = nc.dram_tensor(f"in_{name}", a.shape, mybir.dt.from_np(a.dtype), kind="ExternalInput").ap()
    out = nc.dram_tensor("out", (T, D), F32, kind="ExternalOutput").ap()
    decoder(nc, args, out)
    r = run_bass_kernel_spmd(nc, [arrays], core_ids=[0])
    return r.results[0]["out"].reshape(B, S, D)
```

```python
import numpy as np
import concourse.bass as bass
from concourse import mybir
from contextlib import ExitStack

F32 = mybir.dt.float32
BF16 = mybir.dt.bfloat16
I32 = mybir.dt.int32
ALU = mybir.AluOpType
ACT = mybir.ActivationFunctionType
AX = mybir.AxisListType

B, S, D = 2, 1024, 256
T = B * S
P = 128
NT = T // P
KD = D // P
C = 256
NC = T // C
CT = C // P
SC = 77
HEADS = 16
E = 8
R = 256
NEG = -1.0e30
MASKED = -4.0e9
EPS = 1e-5


def two_halves(eng, n, step):
    step((0, 0, 0), None)
    step((1, 1, 0), (0, 0, 0))
    with eng.Fori(0, n // 2 - 1) as i:
        step((2 * i + 2, 0, i + 1), (2 * i + 1, 1, i))
        step((2 * i + 3, 1, i + 1), (2 * i + 2, 0, i + 1))
    step(None, (n - 1, 1, n // 2 - 1))


def in_stages(eng, n, step):
    step((0, 0, 0), None, None)
    step((1, 1, 0), (0, 0, 0), None)
    step((2, 0, 1), (1, 1, 0), (0, 0, 0))
    with eng.Fori(0, n // 2 - 2) as i:
        step((2 * i + 3, 1, i + 1), (2 * i + 2, 0, i + 1), (2 * i + 1, 1, i))
        step((2 * i + 4, 0, i + 2), (2 * i + 3, 1, i + 1), (2 * i + 2, 0, i + 1))
    step((n - 1, 1, n // 2 - 1), (n - 2, 0, n // 2 - 1), (n - 3, 1, n // 2 - 2))
    step(None, (n - 1, 1, n // 2 - 1), (n - 2, 0, n // 2 - 1))
    step(None, None, (n - 1, 1, n // 2 - 1))


def in_thirds(eng, n, step):
    assert (n - 2) % 3 == 0
    step((0, 0, 0), None)
    step((1, 1, 0), (0, 0, 0))
    with eng.Fori(0, (n - 2) // 3) as i:
        step((3 * i + 2, 2, i), (3 * i + 1, 1, i))
        step((3 * i + 3, 0, i + 1), (3 * i + 2, 2, i))
        step((3 * i + 4, 1, i + 1), (3 * i + 3, 0, i + 1))
    step(None, (n - 1, 1, (n - 2) // 3))


def wait(eng, sem, value):
    if not isinstance(value, int) or value > 0:
        eng.wait_ge(sem, value)


class Stage:

    def __init__(self, nc, name):
        self.nc, self.name, self.ctx, self.sems = nc, name, ExitStack(), []

    def __enter__(self):
        return self

    def __exit__(self, *_):
        if self.sems:
            self.nc.clear_and_free_semaphores(self.sems)
            self.nc.all_engine_barrier()
        self.ctx.close()

    def sb(self, name, shape, dt=F32):
        return self.ctx.enter_context(self.nc.sbuf_tensor(f"{self.name}_{name}", shape, dt))

    def ps(self, name, shape, dt=F32):
        return self.ctx.enter_context(self.nc.psum_tensor(f"{self.name}_{name}", shape, dt))

    def sem(self, name):
        self.sems.append(self.nc.alloc_semaphore(name=f"{self.name}_{name}"))
        return self.sems[-1]

    def block(self):
        return self.nc.Block()



def setup_stage(nc, G, x):
    with Stage(nc, "init") as st:
        filled, shaped, done = st.sem("filled"), st.sem("shaped"), st.sem("done")
        mS = st.sb("maskS", [P, P])
        mT = st.sb("maskT", [P, P])
        with st.block() as block:
            @block.sync
            def _(sp):
                sp.dma_start(G["X"][:], x.rearrange("(t p) d -> p t d", p=P)).then_inc(G["x_loaded"], 16)

            @block.gpsimd
            def _(pool):
                for t in (G["ident"], mS, mT, G["sel16"]):
                    pool.memset(t[:], 0.0).then_inc(filled, 1)
                pool.memset(G["eps"][:], EPS)
                pool.memset(G["lower"][:], 1.0).then_inc(filled, 1)
                pool.memset(G["ones"][:], 1.0)
                pool.wait_ge(filled, 5)

                def select(t, view, pattern, base, mult, op, fill):
                    pool.affine_select(out=view, in_=view, compare_op=op, fill=fill, base=base,
                                       pattern=pattern, channel_multiplier=mult).then_inc(shaped, 1)

                select(None, G["ident"][:], [[-1, P]], 0, 1, ALU.not_equal, 1.0)
                select(None, mS[:], [[-1, P]], 0, 1, ALU.is_ge, NEG)
                select(None, mT[:], [[1, P]], 0, -1, ALU.is_ge, NEG)
                select(None, G["sel16"][:].rearrange("p (a r) -> p a r", r=32), [[-32, 4], [0, 32]], -16, 1,
                       ALU.not_equal, 1.0)
                select(None, G["lower"][:], [[1, P]], 0, -1, ALU.is_gt, 0.0)

            @block.vector
            def _(dve):
                dve.wait_ge(shaped, 5)
                dve.tensor_copy(G["identb"][:], G["ident"][:])
                dve.tensor_copy(G["maskS"][:], mS[:])
                dve.tensor_copy(G["maskT"][:], mT[:]).then_inc(done, 1)



def token_stage(nc, G, tag, *, norm, attn=None, resid=None, units=(), rope=False, wide=None,
                wf=None, bf=None, fscale=None, wv=None, bv=None, heads_group=4, hd=16, outs=None, gate=None,
                ln2=None, x_loaded=None):
    kf = attn[1].shape[0] // P if attn else 0
    narrow = attn is not None and len(attn[0].shape) == 4
    n_units = len(units)
    n_rot = n_units if rope else 0
    v_cols = wv.shape[1] if wv is not None else 0
    v_parts = max(1, v_cols // 512)
    n_rows_units = CT * v_parts if wv is not None else (CT if gate is not None else 0)
    NU = n_units + n_rot + n_rows_units
    SETS = [list(range(s, min(s + 4, n_units))) for s in range(0, n_units, 4)]
    NS = len(SETS)
    USET = len(SETS[0]) if SETS else 0
    RP = 4 if NU >= 4 else 2
    assert 2 * NU % RP == 0 and (NS <= 1 or NS % 2 == 0)
    passes = 1 if norm in ("ln", "rms") else 2
    dve_frees = [u >= n_units + n_rot for u in range(NU)]

    with Stage(nc, tag) as st:
        if attn:
            ot = [st.sb(f"attnT{p}", [P, kf, C]) for p in range(2)]
            wo = st.sb("wo", [P, kf, D])
            bo = st.sb("bo", [P, CT, D])
        nf = wf.shape[1] if wf is not None else 0
        wfs = st.sb("wf", [P, KD, nf]) if nf else None
        bfs = st.sb("bf", [P, nf // P]) if bf is not None else None
        fsc = st.sb("fscale", [P, KD]) if fscale is not None else None
        wvs = st.sb("wv", [P, KD, v_cols]) if wv is not None else None
        bvs = st.sb("bv", [P, v_cols]) if bv is not None else None
        wg = st.sb("wg", [P, KD, E]) if gate is not None else None
        ln2s = st.sb("ln2", [P, CT, D]) if ln2 is not None else None
        if rope:
            cos = st.sb("cos", [P, 1, T])
            sin = st.sb("sin", [P, 1, T])
            straight = [st.sb(f"straight{p}", [P, 4, C]) for p in range(2)]
            swapped = [st.sb(f"swapped{p}", [P, 4, C]) for p in range(2)]
        xn = [st.sb(f"xn{p}", [P, CT, D]) for p in range(2)]
        xT = [st.sb(f"xT{p}", [P, KD, C]) for p in range(2)]
        stats = st.sb("stats", [P, CT, 6])
        mv = st.sb("mv", [P, CT, 2])
        ms = st.sb("ms", [P, CT, 2])
        sd = st.sb("sd", [P, CT, 1])
        rs = st.sb("rs", [P, CT, 1])
        if NS:
            fo = [st.sb(f"f{p}", [P, USET, C]) for p in range(2)]
        if NS and wide is None:
            rr = [st.sb(f"r{p}", [P, USET, C]) for p in range(2)]
            parts = [st.sb(f"parts{p}", [P, USET, 3, C], BF16) for p in range(2)]
        HPG = v_cols // hd if wv is not None else 0
        if HPG:
            vst = [st.sb(f"v{p}", [P, CT, HPG, hd + 1]) for p in range(2)]
        psY = [st.ps(f"psY{p}", [P, CT, D]) for p in range(2)]
        psX = [st.ps(f"psX{p}", [P, CT, KD, P]) for p in range(2)]
        psP = [st.ps(f"psP{p}", [P, 512]) for p in range(RP)]

        w_ld, first_ld, o_ld = st.sem("weights_loaded"), st.sem("first_weights_loaded"), [st.sem(f"attn_loaded{p}") for p in range(2)]
        y_ready, y_free = st.sem("y_ready"), st.sem("y_free")
        var_ready, sd_ready = st.sem("var_ready"), st.sem("sd_ready")
        xn_ready, turned, xT_ready = st.sem("xn_ready"), st.sem("turned"), st.sem("xT_ready")
        pu_ready, act_free, dve_free = st.sem("proj_ready"), st.sem("proj_free_act"), st.sem("proj_free_dve")
        parts_ready, rotated = st.sem("parts_ready"), st.sem("rotated")
        f_out = [st.sem(f"f_stored{p}") for p in range(2)]
        v_out = [st.sem(f"v_stored{p}") for p in range(2)]
        kept = st.sem("kept")

        loads, first_loads = [], []
        if attn:
            first_loads += [(wo[:], attn[1].rearrange("(k p) n -> p k n", p=P))]
            if attn[2] is not None:
                first_loads += [(bo[:, t, :], attn[2].partition_broadcast(P)) for t in range(CT)]
        if nf:
            loads += [(wfs[:], wf.rearrange("(k p) n -> p k n", p=P))]
        if bf is not None:
            loads += [(bfs[:], bf)]
        if fscale is not None:
            first_loads += [(fsc[:], fscale)]
        if wv is not None:
            loads += [(wvs[:], wv.rearrange("(k p) n -> p k n", p=P))]
        if bv is not None:
            loads += [(bvs[:], bv.partition_broadcast(P))]
        if gate is not None:
            loads += [(wg[:], gate.rearrange("(k p) n -> p k n", p=P))]
        if ln2 is not None:
            first_loads += [(ln2s[:, t, :], ln2.partition_broadcast(P)) for t in range(CT)]
        if rope:
            loads += [(cos[:, 0, :], G["cos"]), (sin[:, 0, :], G["sin"])]
        n_loads, n_first_loads = 16 * len(loads), 16 * len(first_loads)

        def set_buffer(piece, s):
            c, p, r = piece
            return (p, r) if NS == 1 else (s % 2, c * (NS // 2) + s // 2)

        def stores(piece, s):
            c, p, r = piece
            b = set_buffer(piece, s)[0]
            if wide is not None:
                dst = wide[SETS[s][0] * P:(SETS[s][-1] + 1) * P, bass.ds(c * C, C)]
                yield dst.rearrange("(i p) t -> p i t", p=P), fo[b][:]
                return
            for i, u in enumerate(SETS[s]):
                for e, dst in enumerate(units[u]):
                    yield (dst[:, bass.ds(r, 1), :, C * p:C * (p + 1)].rearrange("i o f t -> f (i o) t"),
                           parts[b][64 * e:64 * (e + 1), i, :, :])

        n_store = [16 if wide is not None else 16 * sum(len(units[u]) for u in us) for us in SETS]
        store_per_use = n_store[0] if SETS else 0
        assert all(n == store_per_use for n in n_store)

        def store_sets(eng, piece):
            c, p, r = piece
            for s in range(NS):
                b = set_buffer(piece, s)[0]
                if wide is not None:
                    eng.wait_ge(act_free, c * n_units + SETS[s][-1] + 1)
                else:
                    eng.wait_ge(parts_ready, c * NS + s + 1)
                for dst, src in stores(piece, s):
                    eng.dma_start(dst, src).then_inc(f_out[b], 16)

        def store_values(eng, piece):
            c, p, r = piece
            if wv is not None:
                eng.wait_ge(dve_free, (c + 1) * sum(dve_frees))
                for t in range(CT):
                    dst = (outs[:, :, bass.ds(c * CT + t, 1), :].rearrange("g p t x -> p g (t x)") if wide is not None
                           else outs[:, bass.ds(r, 1), :, p * CT + t, :].rearrange("g o p x -> p g (o x)"))
                    eng.dma_start(dst,
                                  vst[p][:, t].rearrange("p (g h) x -> p g (h x)", h=heads_group)
                                  ).then_inc(v_out[p], 16)

        def all_stored(eng):
            for p in range(2):
                if NS:
                    eng.wait_ge(f_out[p], (NC // 2 if NS == 1 else NC * NS // 2) * store_per_use)
                if wv is not None:
                    eng.wait_ge(v_out[p], NC // 2 * 16 * CT)

        with st.block() as block:
            @block.sync
            def _(sp):
                for dst, src in first_loads:
                    sp.dma_start(dst, src).then_inc(first_ld, 16)

                def step(front, back):
                    if front and attn:
                        c, p, r = front
                        wait(sp, y_ready, c - 1)
                        if narrow:
                            view = attn[0].rearrange("(k e) o f t -> e k o f t", e=2)
                            for e in range(2):
                                sp.dma_start(ot[p][64 * e:64 * (e + 1), :, :],
                                             view[e, :, bass.ds(r, 1), :, C * p:C * (p + 1)].rearrange(
                                                 "k o f t -> f (k o) t")).then_inc(o_ld[p], 16)
                        else:
                            sp.dma_start(ot[p][:], attn[0][:, bass.ds(c * C, C)].rearrange("(k p) t -> p k t", p=P)
                                         ).then_inc(o_ld[p], 16)
                    if not back:
                        for dst, src in loads:
                            sp.dma_start(dst, src).then_inc(w_ld, 16)
                    elif wide is not None:
                        store_sets(sp, back)
                        store_values(sp, back)

                two_halves(sp, NC, step)
                if wide is not None:
                    all_stored(sp)
                if first_loads:
                    sp.wait_ge(first_ld, n_first_loads)
                sp.wait_ge(w_ld, n_loads)

            @block.gpsimd
            def _(pool):
                if outs is None and not NS or wide is not None:
                    return

                def step(front, middle, back):
                    if back:
                        store_sets(pool, back)
                    if middle:
                        store_values(pool, middle)

                in_stages(pool, NC, step)
                all_stored(pool)

            @block.tensor
            def _(pe):
                def freed(piece, u):
                    c, p, r = piece
                    if u < 0:
                        c, u = c - 1, u + NU
                    same = dve_frees[u]
                    count = c * dve_frees.count(same) + dve_frees[:u + 1].count(same)
                    return (dve_free if same else act_free), count

                def step(first, front, back):
                    if first and attn:
                        c, p, r = first
                        if isinstance(c, int) and c == 0:
                            pe.wait_ge(first_ld, n_first_loads)
                        pe.wait_ge(o_ld[p], 16 * (1 + narrow) * (r + 1))
                        wait(pe, y_free, c - 1)
                        for t in range(CT):
                            for k in range(kf):
                                mm = pe.matmul(psY[p][:, t, :], ot[p][:, k, t * P:(t + 1) * P], wo[:, k, :],
                                               start=(k == 0), stop=(k == kf - 1))
                        mm.then_inc(y_ready, 1)
                    if back:
                        c, p, r = back
                        if isinstance(c, int) and c == 0:
                            pe.wait_ge(w_ld, n_loads)
                        pe.wait_ge(xT_ready, c + 1)
                        jobs = []
                        for u in range(n_units):
                            jobs.append(("f", u))
                            if rope:
                                jobs.append(("f", n_units + u))
                        for t in range(CT):
                            for v in range(v_parts):
                                jobs.append(("v", t, v))
                        for n, job in enumerate(jobs[:NU]):
                            slot = (p * NU + n) % RP
                            if not (isinstance(c, int) and c == 0 and n < RP):
                                pe.wait_ge(*freed(back, n - RP))
                            for k in range(KD):
                                if job[0] == "f":
                                    m = job[1]
                                    mm = pe.matmul(psP[slot][:, 0:C], wfs[:, k, m * P:(m + 1) * P], xT[p][:, k, :],
                                                   start=(k == 0), stop=(k == KD - 1))
                                elif wv is not None:
                                    w = min(512, v_cols)
                                    _, t, v = job
                                    mm = pe.matmul(psP[slot][:, 0:w], xT[p][:, k, t * P:(t + 1) * P],
                                                   wvs[:, k, v * w:(v + 1) * w], start=(k == 0), stop=(k == KD - 1))
                                else:
                                    t = job[1]
                                    mm = pe.matmul(psP[slot][:, 0:E], xT[p][:, k, t * P:(t + 1) * P], wg[:, k, :],
                                                   start=(k == 0), stop=(k == KD - 1))
                            mm.then_inc(pu_ready, 1)
                    if front:
                        c, p, r = front
                        pe.wait_ge(xn_ready, c + 1)
                        wait(pe, xT_ready, c - 1)
                        for t in range(CT):
                            for k in range(KD):
                                mm = pe.transpose(psX[p][:, t, k, :], xn[p][:, t, k * P:(k + 1) * P], G["ident"][:])
                        mm.then_inc(turned, 1)

                in_stages(pe, NC, step)

            @block.scalar
            def _(act):
                def step(front, back):
                    if front:
                        c, p, r = front
                        for q in range(passes):
                            act.wait_ge(var_ready, c * passes + q + 1)
                            src = mv[:, :, 1:2] if not (norm == "rms" or (norm == "ln_rms" and q)) else ms[:, :, 1:2]
                            act.activation(sd[:], src, ACT.Sqrt, bias=G["eps"][:]).then_inc(sd_ready, 1)
                    if back:
                        c, p, r = back
                        if isinstance(c, int) and c == 0:
                            act.wait_ge(w_ld, n_loads)
                        for s in range(NS):
                            b, uses = set_buffer(back, s)
                            us = SETS[s]
                            if rope:
                                wait(act, rotated, c - 1)
                                for n in range(2 * n_units):
                                    act.wait_ge(pu_ready, c * NU + n + 1)
                                    m = n // 2 + n % 2 * n_units
                                    act.activation((swapped if n % 2 else straight)[p][:, n // 2, :],
                                                   psP[(p * NU + n) % RP][:, 0:C], ACT.Identity, bias=bfs[:, m:m + 1]
                                                   ).then_inc(act_free, 1)
                            else:
                                if wide is not None:
                                    wait(act, f_out[b], uses * store_per_use)
                                else:
                                    wait(act, parts_ready, c - 1)
                                for i, u in enumerate(us):
                                    act.wait_ge(pu_ready, c * NU + u + 1)
                                    slot = (p * NU + u) % RP
                                    bias = bfs[:, u:u + 1] if bf is not None else 0.0
                                    act.activation(fo[b][:, i, :], psP[slot][:, 0:C], ACT.Identity if bf is not None
                                                   else ACT.Copy, bias=bias).then_inc(act_free, 1)
                    if front:
                        c, p, r = front
                        act.wait_ge(turned, c + 1)
                        wait(act, pu_ready, (c - 1) * NU)
                        if fscale is None:
                            act.activation(xT[p][:].rearrange("p k (t q) -> p t k q", q=P), psX[p][:], ACT.Copy
                                           ).then_inc(xT_ready, 1)
                        else:
                            act.activation(xT[p][:, 0, :].rearrange("p (t q) -> p t q", q=P), psX[p][:, :, 0, :],
                                           ACT.Copy, scale=fsc[:, 0:1])
                            act.activation(xT[p][:, 1, :].rearrange("p (t q) -> p t q", q=P), psX[p][:, :, 1, :],
                                           ACT.Copy, scale=fsc[:, 1:2]).then_inc(xT_ready, 1)

                two_halves(act, NC, step)

            @block.vector
            def _(dve):
                if HPG:
                    for p in range(2):
                        dve.memset(vst[p][:, :, :, hd:hd + 1], 1.0)
                if first_loads:
                    dve.wait_ge(first_ld, n_first_loads)
                if x_loaded is not None:
                    dve.wait_ge(x_loaded, 16)
                dve.drain()

                def moments(src, c, q, rms):
                    for t in range(CT):
                        dve.bn_stats(stats[:, t, :], src(t))
                    dve.drain()
                    for t in range(CT):
                        ins = dve.bn_aggr(mv[:, t, :], stats[:, t, :])
                    if rms:
                        dve.drain()
                        dve.tensor_tensor(ms[:, :, 0:1], mv[:, :, 0:1], mv[:, :, 0:1], ALU.mult)
                        dve.drain()
                        ins = dve.tensor_tensor(ms[:, :, 1:2], ms[:, :, 0:1], mv[:, :, 1:2], ALU.add)
                    ins.then_inc(var_ready, 1)
                    dve.wait_ge(sd_ready, c * passes + q + 1)
                    dve.reciprocal(rs[:], sd[:])
                    dve.drain()

                def step(front, middle, back):
                    if front:
                        c, p, r = front
                        rows = resid[:, bass.ds(c * CT, CT), :]
                        row = lambda t: resid[:, bass.ds(c * CT + t, 1), :].rearrange("p t d -> p (t d)")
                        if attn:
                            dve.wait_ge(y_ready, c + 1)
                            dve.tensor_tensor(rows, psY[p][:], rows, ALU.add).then_inc(y_free, 1)
                            if attn[2] is not None:
                                dve.drain()
                                dve.tensor_tensor(rows, rows, bo[:], ALU.add)
                            dve.drain()
                        keep = None
                        moments(row, c, 0, norm == "rms")
                        wait(dve, turned, c - 1)
                        for t in range(CT):
                            if norm == "rms":
                                ins = dve.tensor_scalar(xn[p][:, t, :], row(t), rs[:, t, :], None, ALU.mult)
                            else:
                                ins = dve.tensor_scalar(xn[p][:, t, :], row(t), mv[:, t, 0:1], rs[:, t, :],
                                                        ALU.subtract, ALU.mult)
                        if norm == "ln":
                            ins.then_inc(xn_ready, 1)
                        elif norm == "rms":
                            dve.drain()
                            dve.tensor_tensor(xn[p][:], xn[p][:], ln2s[:], ALU.mult).then_inc(xn_ready, 1)
                            dve.drain()
                            dve.tensor_copy(G["Z"][:, bass.ds(c * CT, CT), :], xn[p][:])
                        elif norm == "ln_ln":
                            ins.then_inc(xn_ready, 1)
                            dve.drain()
                            dve.tensor_copy(G["Y"][:, bass.ds(c * CT, CT), :], xn[p][:])
                            moments(lambda t: xn[p][:, t, :], c, 1, False)
                            for t in range(CT):
                                dve.tensor_scalar(G["Z"][:, bass.ds(c * CT + t, 1), :], xn[p][:, t:t + 1, :],
                                                  mv[:, t, 0:1], rs[:, t, :], ALU.subtract, ALU.mult)
                        elif norm == "ln_rms":
                            dve.drain()
                            dve.tensor_copy(G["Y"][:, bass.ds(c * CT, CT), :], xn[p][:])
                            moments(lambda t: xn[p][:, t, :], c, 1, True)
                            for t in range(CT):
                                ins = dve.tensor_scalar(xn[p][:, t, :], xn[p][:, t, :], rs[:, t, :], None, ALU.mult)
                            ins.then_inc(xn_ready, 1)
                        dve.drain()
                    if back:
                        c, p, r = back
                        if isinstance(c, int) and c == 0:
                            dve.wait_ge(w_ld, n_loads)
                        for s in range(NS):
                            b, uses = set_buffer(back, s)
                            if rope:
                                dve.wait_ge(act_free, (c + 1) * 2 * n_units)
                                for src, tab in ((straight[p], cos), (swapped[p], sin)):
                                    dve.tensor_tensor(src[:], src[:],
                                                      tab[:, :, bass.ds(c * C, C)].broadcast_to([P, 4, C]), ALU.mult)
                                dve.drain()
                                dve.tensor_tensor(fo[b][:], straight[p][:], swapped[p][:], ALU.add
                                                  ).then_inc(rotated, 1)
                                dve.drain()
                            if wide is not None:
                                continue
                            wait(dve, f_out[b], uses * store_per_use)
                            if not rope:
                                dve.wait_ge(act_free, c * n_units + SETS[s][-1] + 1)
                            dve.tensor_copy(parts[b][:, :, 0, :], fo[b][:])
                            dve.drain()
                            dve.tensor_tensor(rr[b][:], fo[b][:], parts[b][:, :, 0, :], ALU.subtract)
                            dve.drain()
                            dve.tensor_copy(parts[b][:, :, 1, :], rr[b][:])
                            dve.drain()
                            dve.tensor_tensor(parts[b][:, :, 2, :], rr[b][:], parts[b][:, :, 1, :], ALU.subtract
                                              ).then_inc(parts_ready, 1)
                    if middle and n_rows_units:
                        c, p, r = middle
                        if isinstance(c, int) and c == 0:
                            dve.wait_ge(w_ld, n_loads)
                        if wv is not None:
                            wait(dve, v_out[p], r * 16 * CT)
                        if n_rows_units:
                            for t in range(CT):
                                for v in range(v_parts):
                                    n = n_units + n_rot + t * v_parts + v
                                    dve.wait_ge(pu_ready, c * NU + n + 1)
                                    slot = (p * NU + n) % RP
                                    if wv is not None:
                                        w = min(512, v_cols)
                                        hp = w // hd
                                        out = vst[p][:, t, v * hp:(v + 1) * hp, 0:hd]
                                        src = psP[slot][:, 0:w].rearrange("p (h r) -> p h r", r=hd)
                                        if bv is not None:
                                            dve.tensor_tensor(out, src, bvs[:, v * w:(v + 1) * w].rearrange(
                                                "p (h r) -> p h r", r=hd), ALU.add).then_inc(dve_free, 1)
                                        else:
                                            dve.tensor_copy(out, src).then_inc(dve_free, 1)
                                    else:
                                        dve.tensor_copy(G["logits"][:, bass.ds(c * CT + t, 1), :],
                                                        psP[slot][:, 0:E].rearrange("p (a e) -> p a e", a=1)
                                                        ).then_inc(dve_free, 1)
                    dve.drain()

                in_stages(dve, NC, step)



def context_stage(nc, G, tag, ctxT, layers, mask, mask_out):
    W = B * SC
    NL = len(layers)
    with Stage(nc, tag) as st:
        cT = st.sb("ctxT", [P, KD, W])
        wks, wvs = ([st.sb(f"{n}{l}", [P, KD, D]) for l in range(NL)] for n in ("wk", "wv"))
        bks, bvs = [st.sb(f"bk{l}", [P, KD]) for l in range(NL)], [st.sb(f"bv{l}", [SC, D]) for l in range(NL)]
        f, r = st.sb("f", [P, KD, W]), st.sb("r", [P, KD, W])
        parts = [st.sb(f"parts{l}", [P, KD, 3, W], BF16) for l in range(NL)]
        v = [st.sb(f"v{l}", [SC, B, HEADS, 17]) for l in range(NL)]
        psK = [[st.ps(f"psK{l}{m}", [P, 512]) for m in range(KD)] for l in range(NL)]
        psV = [[st.ps(f"psV{l}{b}", [P, 512]) for b in range(B)] for l in range(NL)]
        mi, mf = st.sb("mi", [P, W], I32), st.sb("mf", [P, W])
        mb = st.sb("mb", [1, B, 4, SC], BF16)
        loaded, ready, stored, done = st.sem("loaded"), st.sem("ready"), st.sem("stored"), st.sem("done")
        n_loads = 16 * (2 + 4 * NL)
        with st.block() as block:
            @block.sync
            def _(sp):
                sp.dma_start(cT[:], ctxT.rearrange("(k p) t -> p k t", p=P)).then_inc(loaded, 16)
                sp.dma_start(mi[:], mask.rearrange("b a s -> (b a s)").partition_broadcast(P)).then_inc(loaded, 16)
                for l, (wk, bk, wv, bv, _, _) in enumerate(layers):
                    sp.dma_start(wks[l][:], wk.rearrange("(k p) n -> p k n", p=P)).then_inc(loaded, 16)
                    sp.dma_start(wvs[l][:], wv.rearrange("(k p) n -> p k n", p=P)).then_inc(loaded, 16)
                    sp.dma_start(bks[l][:], bk).then_inc(loaded, 16)
                    sp.dma_start(bvs[l][:], bv.partition_broadcast(SC)).then_inc(loaded, 16)
                n = 0
                for l, (_, _, _, _, k_out, v_out) in enumerate(layers):
                    sp.wait_ge(done, l + 1)
                    for hg in range(HEADS // 4):
                        at = hg % 2 * 64
                        for b in range(B):
                            sp.dma_start(k_out[:, hg, b].rearrange("i f s -> f i s"),
                                         parts[l][at:at + 64, hg // 2, :, b * SC:(b + 1) * SC]).then_inc(stored, 16)
                            n += 1
                        if l == 0:
                            sp.dma_start(mask_out[hg * B:(hg + 1) * B].rearrange("(a b) h s -> a b h s", a=1), mb[:]
                                         ).then_inc(stored, 16)
                            n += 1
                    for b in range(B):
                        sp.dma_start(v_out[:, b].rearrange("g p x -> p g x"),
                                     v[l][:, b].rearrange("p (g h) x -> p g (h x)", h=4)).then_inc(stored, 16)
                        n += 1
                sp.wait_ge(stored, 16 * n)

            @block.tensor
            def _(pe):
                pe.wait_ge(loaded, n_loads)
                for l in range(NL):
                    for m in range(KD):
                        for k in range(KD):
                            pe.matmul(psK[l][m][:, 0:W], wks[l][:, k, m * P:(m + 1) * P], cT[:, k, :],
                                      start=(k == 0), stop=(k == KD - 1))
                    for b in range(B):
                        for k in range(KD):
                            mm = pe.matmul(psV[l][b][0:SC, 0:D], cT[:, k, b * SC:(b + 1) * SC], wvs[l][:, k, :],
                                           start=(k == 0), stop=(k == KD - 1))
                    mm.then_inc(ready, 1)

            @block.vector
            def _(dve):
                for l in range(NL):
                    dve.memset(v[l][:, :, :, 16:17], 1.0)
                dve.wait_ge(loaded, n_loads)
                dve.tensor_scalar(mf[:], mi[:], 0.0, None, ALU.not_equal)
                dve.drain()
                for b in range(B):
                    for h in range(4):
                        dve.tensor_scalar(mb[:, b, h, :], mf[0:1, b * SC:(b + 1) * SC], -MASKED, MASKED,
                                          ALU.mult, ALU.add)
                for l in range(NL):
                    dve.wait_ge(ready, l + 1)
                    for m in range(KD):
                        dve.tensor_scalar(f[:, m, :], psK[l][m][:, 0:W], bks[l][:, m:m + 1], None, ALU.add)
                        if l == 0:
                            dve.drain()
                            dve.tensor_tensor(f[:, m, :], f[:, m, :], mf[:], ALU.mult)
                    dve.drain()
                    dve.tensor_copy(parts[l][:, :, 0, :], f[:])
                    dve.drain()
                    dve.tensor_tensor(r[:], f[:], parts[l][:, :, 0, :], ALU.subtract)
                    dve.drain()
                    dve.tensor_copy(parts[l][:, :, 1, :], r[:])
                    dve.drain()
                    dve.tensor_tensor(parts[l][:, :, 2, :], r[:], parts[l][:, :, 1, :], ALU.subtract)
                    for b in range(B):
                        dve.tensor_tensor(v[l][:, b, :, 0:16], psV[l][b][0:SC, 0:D].rearrange("p (h r) -> p h r", r=16),
                                          bvs[l][:].rearrange("p (h r) -> p h r", r=16), ALU.add)
                    dve.drain()
                    dve.memset(G["tick"][:], 0.0).then_inc(done, 1)



Q_PARTS = (0, 0, 1, 1, 0, 2)
K_PARTS = (0, 1, 0, 1, 2, 0)


def spread(costs_front, costs_back, first):
    work, total = np.cumsum(costs_back[first:]), sum(costs_front)
    done = np.cumsum(costs_front)
    return [0] * first + [int(np.searchsorted(done, w / work[-1] * total * (1 + 1e-9), side="right")) for w in work]


def attention_stage(nc, G, tag, *, q, k, v, o, causal=False, cross=False, mask=None, sums=None):
    H, hd = 4, 16
    n_groups = (HEADS // H) * B
    KT = [(0, SC)] if cross else [(i * P, P) for i in range(S // P)]
    NK = SC if cross else S
    QT = S // P
    scale = float(hd) ** -0.5
    base = len(Q_PARTS) * 16
    K1 = base + (mask is not None)
    K2 = K1 + 3
    units1 = [(None, h) for h in range(H)] if cross else [(t, h) for t in range(QT) for h in range(H)]
    NS = len(units1)
    ugs = [(qh, i, max(0, k0 - 512 * qh) if causal else 0) for qh in range(2) for i, (k0, _) in enumerate(KT)
           if not causal or k0 < 512 * (qh + 1)]
    NUG, NST = len(ugs), len(ugs) * H
    HALF = [ug[0] for ug in ugs].index(1) * H
    RING = 3
    VC = H * (hd + 1)
    VT = 1 if cross else QT
    n_turns = 1 if cross else 2
    TR = H * QT // n_turns
    if not cross:
        due = spread([(t + 1) * P if causal else S for t, _ in units1],
                     [512 - ugs[u // H][2] for u in range(NST)], 5)
        INVERT_AT = NS // 2 if causal else NS // 4

    with Stage(nc, tag) as st:
        qs = [st.sb(f"qs{p}", [P, 2, H, 512], BF16) for p in range(3)]
        ks = [st.sb(f"ks{p}", [P, H, SC] if cross else [P, 2, H, 512], BF16) for p in range(3)]
        vs = [st.sb(f"vs{p}", [P, VT, H, hd + 1]) for p in range(3)]
        pr = [st.sb(f"probs{r}", [P, H, 512]) for r in range(RING)]
        osb = [st.sb(f"osb{p}", [P, S]) for p in range(3)]
        pool_tick = st.sb("pool_tick", [1, 1])
        if cross:
            inv_q = st.sb("inverses_q", [P, QT, H, 1])
            on_q = st.sb("outputs_q", [P, QT // 2, 2, H, hd])
        else:
            rec = st.sb("rec", [P, S])
        on = [st.sb(f"on{p}", [P, S]) for p in range(3)]
        if sums is not None:
            sm, inv = st.sb("sums", [P, H * S // P]), st.sb("inverses", [P, H * S // P])
        mx = st.sb("mx", [P, 2, H, QT // 2])
        neg = st.sb("neg", [TR, P])
        nres = st.sb("nres", [TR, P])
        nparts = [[st.sb(f"nparts{p}{w}", [TR, 3, P], BF16) for w in range(n_turns)] for p in range(3)]
        ps1 = [st.ps(f"rows{p}", [P, S]) for p in range(2)]
        ps2 = [st.ps(f"cols{p}", [P, 512]) for p in range(2)]
        psO = st.ps("out", [P, S])
        ld = [st.sem(f"loaded{p}") for p in range(3)]
        mld = [[st.sem(f"max_placed{p}{w}") for w in range(n_turns)] for p in range(3)]
        if sums is not None:
            sums_out, sums_in = st.sem("sums_out"), st.sem("sums_in")
            inv_out, inv_in = st.sem("inverses_out"), st.sem("inverses_in")
        ones_set = [st.sem("first_ones_set"), st.sem("other_ones_set")]
        out_zeroed = st.sem("out_zeroed")
        s_ready, s_free = st.sem("rows_ready"), st.sem("rows_free")
        mt_ready, mt_done, neg_ready = st.sem("max_turned"), st.sem("max_read"), st.sem("neg_ready")
        st_ready, ex_done, pv_done = st.sem("cols_ready"), st.sem("exp_done"), st.sem("pv_done")
        o_copied = st.sem("out_copied")
        o_turned, q_done, o_back = st.sem("out_turned"), st.sem("out_q_done"), st.sem("out_turned_back")
        n_st = 1 if cross else H
        rec_done, o_done = st.sem("sums_inverted"), st.sem("out_done")
        stored = [st.sem(f"stored{p}") for p in range(3)]
        n_ld = 2 * len(Q_PARTS) + (mask is not None) + 1

        with st.block() as block:
            @block.sync
            def _(sp):
                def load(p, g):
                    for i in range(len(Q_PARTS)):
                        rows = slice(16 * i, 16 * i + 16)
                        yield (qs[p][rows].rearrange("r a h t -> r (a h) t"),
                               q.rearrange("i g o f t -> i (g o) f t")[Q_PARTS[i], bass.ds(2 * g, 2)].rearrange(
                                   "a (h r) t -> r (a h) t", r=16))
                        if cross:
                            yield (ks[p][rows],
                                   k.rearrange("i g b f s -> i (g b) f s")[K_PARTS[i], bass.ds(g, 1)].rearrange(
                                       "o (h r) s -> r (o h) s", r=16))
                        else:
                            yield (ks[p][rows].rearrange("r a h t -> r (a h) t"),
                                   k.rearrange("i g o f t -> i (g o) f t")[K_PARTS[i], bass.ds(2 * g, 2)].rearrange(
                                       "a (h r) t -> r (a h) t", r=16))
                    if cross:
                        yield (vs[p][0:SC, 0].rearrange("p h x -> p (h x)"),
                               v.rearrange("g b p x -> (g b) p x")[bass.ds(g, 1)].rearrange("o p x -> p (o x)"))
                    else:
                        yield (vs[p][:].rearrange("p (a t) h x -> p a (t h x)", a=2),
                               v.rearrange("g o p t x -> (g o) p (t x)")[bass.ds(2 * g, 2)].rearrange("a p x -> p a x"))

                def exchange(g, p):
                    sp.wait_ge(o_copied, g + 1)
                    sp.dma_start(sums[0, p].rearrange("(h t) -> h t", h=H), osb[p][hd:P:32, :]).then_inc(sums_out, 16)
                    sp.wait_ge(sums_out, 16 * (g + 1))
                    sp.dma_start(sm[:], sums[0, p].rearrange("(p x) -> p x", p=P)).then_inc(sums_in, 16)
                    sp.wait_ge(rec_done, g + 1)
                    sp.dma_start(sums[1, p].rearrange("(p x) -> p x", p=P), inv[:]).then_inc(inv_out, 16)
                    sp.wait_ge(inv_out, 16 * (g + 1))
                    wait(sp, o_done, g)
                    for h in range(H):
                        sp.dma_start(rec[32 * h:32 * h + hd, :], sums[1, p, h * S:(h + 1) * S].partition_broadcast(hd)
                                     ).then_inc(inv_in, 16)

                def place(piece, w):
                    g, p, r = piece
                    sp.wait_ge(neg_ready, n_turns * g + w + 1)
                    for i in range(3):
                        dst = qs[p][K1 + i:K1 + i + 1]
                        dst = dst if n_turns == 1 else dst[:, w:w + 1]
                        sp.dma_start(dst.rearrange("p a h (t q) -> p (a h t) q", q=P),
                                     nparts[p][w][:, i, :]).then_inc(mld[p][w], 16)

                def step(front, back):
                    first = back and isinstance(back[0], int) and back[0] == 0
                    if n_turns == 2 and back and not first:
                        place(back, 0)
                    if front:
                        g, p, r = front
                        wait(sp, pv_done, (g - 2) * NUG)
                        for dst, src in load(p, g):
                            sp.dma_start(dst, src).then_inc(ld[p], 16)
                        if mask is not None:
                            sp.wait_ge(ones_set[min(p, 1)], 1)
                            sp.dma_start(ks[p][base:base + 1, :, :], mask[bass.ds(g, 1), :, :]).then_inc(ld[p], 16)
                    if back:
                        if n_turns == 1 or first:
                            place(back, 0)
                        if n_turns == 2:
                            place(back, 1)
                        if sums is not None and not first:
                            exchange(back[0] - 1, (back[1] + 2) % 3)

                in_thirds(sp, n_groups, step)
                if sums is not None:
                    exchange(n_groups - 1, (n_groups - 1) % 3)

            @block.gpsimd
            def _(pool):
                for p in (1, 2):
                    pool.memset(ks[p][base:K2], 1.0)
                    pool.drain()
                    if mask is not None:
                        pool.memset(qs[p][base:K2], 1.0)
                        pool.drain()
                if sums is not None:
                    pool.memset(rec[:], 0.0)
                    pool.drain()
                pool.memset(pool_tick[:], 0.0).then_inc(ones_set[1], 1)

                def step(front, back):
                    if back:
                        g, p, r = back
                        if not cross:
                            pool.wait_ge(inv_in, 16 * H * (g + 1))
                            wait(pool, stored[p], r * n_st * 16)
                            pool.tensor_tensor(on[p][:], osb[p][:], rec[:], ALU.mult).then_inc(o_done, 1)
                        pool.wait_ge(o_done, g + 1)
                        if cross:
                            pool.dma_start(o.rearrange("g o f t -> (g o f) t")[bass.ds(P * g, P)], on[p][:, 0:512]
                                           ).then_inc(stored[p], 16)
                            return
                        for h in range(H):
                            pool.dma_start(o.rearrange("g o f t -> (g o) f t")[bass.ds(2 * g, 2), 16 * h:16 * h + 16]
                                           .rearrange("a f t -> f a t"),
                                           on[p][32 * h:32 * h + 16, :].rearrange("f (a t) -> f a t", a=2)
                                           ).then_inc(stored[p], 16)

                in_thirds(pool, n_groups, step)
                for p in range(3):
                    pool.wait_ge(stored[p], (n_groups - p + 2) // 3 * n_st * 16)

            @block.tensor
            def _(pe):
                def rows_unit(front, s):
                    g, p, r = front
                    t, h = units1[s]
                    dst = ps1[(s + cross) % 2]
                    if s >= 2:
                        pe.wait_ge(s_free, g * NS + s - 1)
                    elif cross and s == 0:
                        wait(pe, q_done, g - 2)
                    elif cross:
                        wait(pe, mt_done, g)
                        wait(pe, o_done, g - 2)
                    elif s == 1:
                        wait(pe, mt_done, n_turns * g)
                    else:
                        wait(pe, s_free, g * NS - 1)
                    if n_turns == 2 and s == NS // 2 + 1:
                        pe.wait_ge(mt_done, n_turns * g + 1)
                    if cross:
                        for t in range(QT):
                            at = 512 * (t // 4) + SC * (t % 4)
                            mm = pe.matmul(dst[:, at:at + SC], qs[p][0:K1, t // 4, h, t % 4 * P:(t % 4 + 1) * P],
                                           ks[p][0:K1, h, :], start=True, stop=True)
                    else:
                        n = (t + 1) * P if causal else S
                        for a in range(0, n, 512):
                            b = min(n, a + 512)
                            diag = causal and b == n
                            mm = pe.matmul(dst[:, a:b], qs[p][0:K1, t // 4, h, t % 4 * P:(t % 4 + 1) * P],
                                           ks[p][0:K1, a // 512, h, 0:b - a], start=True, stop=not diag)
                            if diag:
                                mm = pe.matmul(dst[:, n - P:n], G["identb"][:], G["maskS"][:], start=False, stop=True)
                    mm.then_inc(s_ready, 1)

                def rows_units(front, first, last):
                    for s in range(first, last):
                        rows_unit(front, s)
                        if n_turns == 2 and s == NS // 2:
                            turn_max(front, 0)

                def turn_max(front, w):
                    g = front[0]
                    pe.wait_ge(s_free, g * NS + (w + 1) * NS // n_turns)
                    part = (mx[:] if n_turns == 1 else mx[:, w:w + 1]).rearrange("p a h t -> p (a h t)")
                    pe.transpose(ps1[1 - cross][0:TR, 0:P], part, G["ident"][:]).then_inc(mt_ready, 1)

                def cols_unit(back, u):
                    g, p, r = back
                    qh, i, c0 = ugs[u // H]
                    h = u % H
                    k0, rows = KT[i]
                    dst = ps2[u % 2]
                    if u >= 2:
                        pe.wait_ge(ex_done, g * NST + u - 1)
                    if u == 0 or (u == HALF and n_turns == 2):
                        pe.wait_ge(mld[p][u // HALF], 16 * 3 * (r + 1))
                    diag = causal and k0 >= 512 * qh
                    keys = ks[p][0:K2, h, :] if cross else ks[p][0:K2, k0 // 512, h, k0 % 512:k0 % 512 + rows]
                    mm = pe.matmul(dst[0:rows, 0:512 - c0], keys,
                                   qs[p][0:K2, qh, h, c0:512], start=True, stop=not diag)
                    if diag:
                        mm = pe.matmul(dst[:, 0:P], G["identb"][:], G["maskT"][:], start=False, stop=True)
                    mm.then_inc(st_ready, 1)

                def values_unit(back, ug, part=None):
                    g, p, r = back
                    qh, i, c0 = ugs[ug]
                    rows = KT[i][1]
                    last = ug + 1 == NUG or ugs[ug + 1][0] != qh
                    if part != 1:
                        pe.wait_ge(ex_done, g * NST + (ug + 1) * H)
                        if ug == 0:
                            wait(pe, o_copied, g)
                    whole = part is None or i == 0
                    mid = (c0 + 512) // 2
                    a, b = (c0, 512) if whole else ((c0, mid) if part == 0 else (mid, 512))
                    if not (part == 1 and whole):
                        for h in range(H):
                            mm = pe.matmul(psO[32 * h:32 * h + hd + 1, 512 * qh + a:512 * qh + b],
                                           vs[p][0:rows, i, h, :], pr[ug % RING][0:rows, h, a:b],
                                           start=(i == 0), stop=last and (whole or part == 1))
                        if whole or part == 1:
                            mm.then_inc(pv_done, 1)

                def turn_outputs(g, p):
                    pe.wait_ge(o_copied, g + 1)
                    wait(pe, q_done, g)
                    for n in range(QT):
                        mm = pe.transpose(ps1[1][:, n * P:(n + 1) * P], osb[p][:, n * P:(n + 1) * P], G["ident"][:])
                    mm.then_inc(o_turned, 1)

                def turn_back(g, n_max):
                    pe.wait_ge(q_done, g + 1)
                    pe.wait_ge(mt_done, n_max)
                    wait(pe, o_done, g)
                    for n in range(QT // 2):
                        mm = pe.transpose(ps1[0][:, n * P:(n + 1) * P],
                                          on_q[:, n].rearrange("p a h r -> p (a h r)"), G["ident"][:])
                    mm.then_inc(o_back, 1)

                def step(front, back):
                    if front and (cross or not back):
                        pe.wait_ge(ld[front[1]], 16 * n_ld * (front[2] + 1))
                        rows_units(front, 0, NS)
                    if not back:
                        turn_max(front, n_turns - 1)
                        pe.wait_ge(ones_set[0], 1)
                        pe.wait_ge(ones_set[1], 1)
                        pe.wait_ge(out_zeroed, 1)
                        return
                    g, p, r = back
                    later = not isinstance(g, int) or g > 0
                    s = 0
                    for u in range(NST):
                        cols_unit(back, u)
                        if cross:
                            if u == H - 1:
                                if front:
                                    turn_max(front, 0)
                                if later:
                                    turn_outputs(g - 1, (p + 2) % 3)
                            if u == 2 * H - 1:
                                values_unit(back, 0)
                                if later:
                                    turn_back(g - 1, g + 2 if front else g + 1)
                            continue
                        if u % 2 and u >= H:
                            values_unit(back, u // H - 1, u % H // 2)
                        if front and due[u] > s:
                            if s == 0:
                                pe.wait_ge(ld[front[1]], 16 * n_ld * (front[2] + 1))
                            rows_units(front, s, due[u])
                            s = due[u]
                    values_unit(back, NUG - 1)
                    if front and not cross:
                        turn_max(front, 1)
                    if not front and cross:
                        turn_outputs(g, p)
                        turn_back(g, g + 1)

                in_thirds(pe, n_groups, step)

            @block.scalar
            def _(act):
                def finish(g, p, r):
                    act.wait_ge(o_back, g + 1)
                    wait(act, stored[p], r * n_st * 16)
                    act.activation(on[p][:, 0:512], ps1[0][:, 0:512], ACT.Copy).then_inc(o_done, 1)

                def step(front, back):
                    if not back:
                        return
                    g, p, r = back
                    for u in range(NST):
                        ug, h = u // H, u % H
                        qh, i, c0 = ugs[ug]
                        rows = KT[i][1]
                        act.wait_ge(st_ready, g * NST + u + 1)
                        if h == 0 and ug >= RING:
                            act.wait_ge(pv_done, g * NUG + ug - RING + 1)
                        act.activation(pr[ug % RING][0:rows, h, c0:512], ps2[u % 2][0:rows, 0:512 - c0], ACT.Exp,
                                       scale=scale).then_inc(ex_done, 1)
                    act.wait_ge(pv_done, (g + 1) * NUG)
                    if cross:
                        if not isinstance(g, int) or g > 0:
                            finish(g - 1, (p + 2) % 3, r if p else r - 1)
                    else:
                        wait(act, o_done, g - 1)
                    act.activation(osb[p][:], psO[:], ACT.Copy).then_inc(o_copied, 1)
                    if cross and not front:
                        finish(g, p, r)

                in_thirds(act, n_groups, step)

            @block.vector
            def _(dve):
                dve.memset(ks[0][base:K2], 1.0)
                if mask is not None:
                    dve.memset(qs[0][base:K2], 1.0)
                dve.drain()
                dve.memset(G["tick"][:], 0.0).then_inc(ones_set[0], 1)
                dve.memset(psO[:], 0.0).then_inc(out_zeroed, 1)

                def invert_sums(g):
                    dve.wait_ge(sums_in, 16 * (g + 1))
                    wait(dve, inv_out, 16 * g)
                    dve.reciprocal(inv[:], sm[:]).then_inc(rec_done, 1)

                def divide(g):
                    dve.wait_ge(o_turned, g + 1)
                    turned = ps1[1][:].rearrange("p (n h x) -> p n h x", n=QT, h=H)
                    dve.reciprocal(inv_q[:], turned[:, :, :, hd:hd + 1])
                    dve.drain()
                    wait(dve, o_back, g)
                    for a in range(2):
                        tiles = slice(QT // 2 * a, QT // 2 * (a + 1))
                        ins = dve.tensor_tensor(on_q[:, :, a], turned[:, tiles, :, 0:hd],
                                                inv_q[:, tiles].broadcast_to([P, QT // 2, H, hd]), ALU.mult)
                    ins.then_inc(q_done, 1)

                def negate_max(front, w):
                    g, p, r = front
                    wait(dve, mld[p][w], 16 * 3 * r)
                    dve.wait_ge(mt_ready, n_turns * g + w + 1)
                    dve.tensor_scalar(neg[:], ps1[1 - cross][0:TR, 0:P], -1.0, None, ALU.mult).then_inc(mt_done, 1)
                    dve.drain()
                    parts = nparts[p][w]
                    dve.tensor_copy(parts[:, 0, :], neg[:])
                    dve.drain()
                    dve.tensor_tensor(nres[:], neg[:], parts[:, 0, :], ALU.subtract)
                    dve.drain()
                    dve.tensor_copy(parts[:, 1, :], nres[:])
                    dve.drain()
                    dve.tensor_tensor(parts[:, 2, :], nres[:], parts[:, 1, :], ALU.subtract).then_inc(neg_ready, 1)

                def maxima(front, invert=None):
                    g, p, r = front
                    for s, (t, h) in enumerate(units1):
                        if invert is not None and s == INVERT_AT:
                            invert_sums(invert)
                        dve.wait_ge(s_ready, g * NS + s + 1)
                        if cross:
                            view = ps1[(s + cross) % 2][:].rearrange("p (a n) -> p a n", a=2)[:, :, 0:4 * SC]
                            dve.tensor_reduce(mx[:, :, h, :], view.rearrange("p a (b n) -> p a b n", b=4), AX.X,
                                              ALU.max).then_inc(s_free, 1)
                        else:
                            n = (t + 1) * P if causal else S
                            at = mx[:, t // 4, h, t % 4:t % 4 + 1]
                            dve.tensor_reduce(at, ps1[(s + cross) % 2][:, 0:n], AX.X, ALU.max).then_inc(s_free, 1)
                        if n_turns == 2 and s == NS // 2:
                            negate_max(front, 0)
                    negate_max(front, n_turns - 1)

                def step(front, back):
                    g = back[0] if back else 0
                    later = not isinstance(g, int) or g > 0
                    if front and cross:
                        maxima(front)
                        if later:
                            divide(g - 1)
                    elif front:
                        maxima(front, g - 1 if later else None)
                    elif cross:
                        divide(g - 1)
                        divide(g)
                    else:
                        invert_sums(g - 1)
                        invert_sums(g)

                in_thirds(dve, n_groups, step)


def wide_attention_stage(nc, G, tag, *, q, k, v, o):
    hd = 64
    n_groups = HEADS * B
    QT = S // P
    scale = float(hd) ** -0.5
    NS = QT
    NST = 2 * QT
    RING = 8
    NADD = NST - 2
    added_at = lambda u: u + 1 if u < 2 else u - 1
    FIRST_ROWS, LAST_ROWS = 6, 13
    due = [min(NS, max(0, -(-NS * (u + 1 - FIRST_ROWS) // (LAST_ROWS - FIRST_ROWS)))) for u in range(NST)]
    TURN = LAST_ROWS + 1

    with Stage(nc, tag) as st:
        qs, ks = st.sb("qs", [hd, S], BF16), st.sb("ks", [hd, S], BF16)
        qf = [st.sb(f"qf{p}", [65, S]) for p in range(2)]
        kf = [st.sb(f"kf{p}", [65, S]) for p in range(2)]
        vs = [st.sb(f"vs{p}", [P, QT, hd + 1]) for p in range(2)]
        pr = [st.sb(f"probs{r}", [P, 512]) for r in range(RING)]
        sums = [st.sb(f"sums{h}", [P, 512]) for h in range(2)]
        osb = st.sb("osb", [P, 512])
        rec = st.sb("rec", [P, 512])
        on = [st.sb(f"on{p}", [P, 512]) for p in range(2)]
        mx = st.sb("mx", [P, QT])
        neg = [st.sb(f"neg{p}", [QT, P]) for p in range(2)]
        ps1 = [st.ps(f"rows{p}", [P, S]) for p in range(2)]
        ps2 = [st.ps(f"cols{p}", [P, 512]) for p in range(2)]
        psO = st.ps("out", [P, 512])
        psL = st.ps("sums_spread", [P, 512])
        ld = [st.sem(f"loaded{p}") for p in range(2)]
        vld = [st.sem(f"values_loaded{p}") for p in range(2)]
        mld = [st.sem(f"max_placed{p}") for p in range(2)]
        ones_set, cast = st.sem("ones_set"), st.sem("cast")
        s_ready, s_free = st.sem("rows_ready"), st.sem("rows_free")
        mt_ready, neg_ready = st.sem("max_turned"), st.sem("neg_ready")
        st_ready, ex_done, pv_done = st.sem("cols_ready"), st.sem("exp_done"), st.sem("pv_done")
        added, lb_ready = st.sem("exp_added"), st.sem("sums_ready")
        o_copied, rec_done, o_done = st.sem("out_copied"), st.sem("sums_inverted"), st.sem("out_done")
        stored = [st.sem(f"stored{p}") for p in range(2)]
        n_ld = 2

        with st.block() as block:
            @block.sync
            def _(sp):
                sp.wait_ge(ones_set, 1)

                def step(front, back):
                    if front:
                        g, p, r = front
                        feats, cols = bass.ds(r * 64, 64), slice(p * S, (p + 1) * S)
                        wait(sp, st_ready, (g - 1) * NST)
                        sp.dma_start(kf[p][0:64, :], k[feats, cols]).then_inc(ld[p], 16)
                        sp.dma_start(qf[p][0:64, :], q[feats, cols]).then_inc(ld[p], 16)
                        wait(sp, pv_done, (g - 1) * QT)
                        sp.dma_start(vs[p][:].rearrange("p t x -> p (t x)"),
                                     v[bass.ds(r, 1), :, p * QT:(p + 1) * QT, :].rearrange("g p t x -> p (g t x)")
                                     ).then_inc(vld[p], 16)
                        sp.wait_ge(neg_ready, g + 1)
                        sp.dma_start(qf[p][64:65, :].rearrange("p (t q) -> p t q", q=P),
                                     neg[p][:]).then_inc(mld[p], 16)

                two_halves(sp, n_groups, step)

            @block.gpsimd
            def _(pool):
                def step(front, back):
                    if back:
                        g, p, r = back
                        for u in range(2, NST):
                            i, h = u // 2, u % 2
                            if i == 1:
                                wait(pool, lb_ready, g)
                            elif h == 0:
                                pool.drain()
                            pool.wait_ge(ex_done, g * NST + u + 1)
                            pool.tensor_tensor(sums[h][:], pr[h][:] if i == 1 else sums[h][:], pr[u % RING][:],
                                               ALU.add).then_inc(added, 1)
                            if u == NST // 2 and (not isinstance(g, int) or g > 0):
                                store(g - 1, 1 - p, r if p else r - 1)
                        if not front:
                            store(g, p, r)

                def store(g, p, r):
                    pool.wait_ge(o_done, g + 1)
                    for h in range(2):
                        pool.dma_start(o[bass.ds(r * 64, 64), p * S + 512 * h:p * S + 512 * (h + 1)],
                                       on[p][64 * h:64 * (h + 1), :]).then_inc(stored[p], 16)

                two_halves(pool, n_groups, step)
                for p in range(2):
                    pool.wait_ge(stored[p], n_groups // 2 * 2 * 16)

            @block.tensor
            def _(pe):
                pe.wait_ge(ones_set, 1)

                def rows_unit(front, s):
                    g, p, r = front
                    if s == 0:
                        pe.wait_ge(cast, g + 1)
                    if s >= 2:
                        pe.wait_ge(s_free, g * NS + s - 1)
                    elif s == 1:
                        wait(pe, neg_ready, g)
                    else:
                        wait(pe, s_free, g * NS - 1)
                    for a in range(0, S, 512):
                        mm = pe.matmul(ps1[s % 2][:, a:a + 512], qs[:, s * P:(s + 1) * P], ks[:, a:a + 512],
                                       start=True, stop=True)
                    mm.then_inc(s_ready, 1)

                def turn_max(front):
                    pe.wait_ge(s_free, (front[0] + 1) * NS)
                    pe.transpose(ps1[1][0:QT, 0:P], mx[:], G["ident"][:]).then_inc(mt_ready, 1)

                def cols_unit(back, u):
                    g, p, r = back
                    i, h = u // 2, u % 2
                    if u >= 2:
                        pe.wait_ge(ex_done, g * NST + u - 1)
                    pe.matmul(ps2[u % 2][:], kf[p][:, i * P:(i + 1) * P], qf[p][:, 512 * h:512 * (h + 1)],
                              start=True, stop=True).then_inc(st_ready, 1)

                def values_unit(back, i):
                    g, p, r = back
                    pe.wait_ge(ex_done, g * NST + 2 * i + 2)
                    if i == 0:
                        pe.wait_ge(vld[p], 16 * (r + 1))
                        wait(pe, o_copied, g)
                    for h in range(2):
                        mm = pe.matmul(psO[64 * h:64 * (h + 1), :], vs[p][:, i, 0:hd], pr[(2 * i + h) % RING][:],
                                       start=(i == 0), stop=(i == QT - 1))
                    mm.then_inc(pv_done, 1)

                def spread_sums(g):
                    pe.wait_ge(added, (g + 1) * NADD)
                    wait(pe, rec_done, g)
                    for h in range(2):
                        mm = pe.matmul(psL[64 * h:64 * (h + 1), :], G["ones"][:, 0:64], sums[h][:],
                                       start=True, stop=True)
                    mm.then_inc(lb_ready, 1)

                def step(front, back):
                    if not back:
                        for s in range(NS):
                            rows_unit(front, s)
                        turn_max(front)
                        return
                    g, p, r = back
                    later = not isinstance(g, int) or g > 0
                    s = 0
                    pe.wait_ge(mld[p], 16 * (r + 1))
                    for u in range(NST):
                        cols_unit(back, u)
                        if u == 1 and later:
                            spread_sums(g - 1)
                        if u % 2 and u >= 3:
                            values_unit(back, u // 2 - 1)
                        if front:
                            for s in range(s, due[u]):
                                rows_unit(front, s)
                            s = due[u]
                            if u == TURN:
                                turn_max(front)
                    values_unit(back, QT - 1)
                    if not front:
                        spread_sums(g)

                two_halves(pe, n_groups, step)

            @block.scalar
            def _(act):
                def step(front, back):
                    if not back:
                        return
                    g, p, r = back
                    for u in range(NST):
                        act.wait_ge(st_ready, g * NST + u + 1)
                        if u >= RING:
                            act.wait_ge(pv_done, g * QT + (u - RING) // 2 + 1)
                            act.wait_ge(added, g * NADD + added_at(u - RING))
                        elif not isinstance(g, int) or g > 0:
                            last = max(w for w in range(NST) if w % RING == u)
                            act.wait_ge(pv_done, g * QT - QT + last // 2 + 1)
                            act.wait_ge(added, g * NADD - NADD + added_at(last))
                        act.activation(pr[u % RING][:], ps2[u % 2][:], ACT.Exp, scale=scale).then_inc(ex_done, 1)
                    act.wait_ge(pv_done, (g + 1) * QT)
                    wait(act, o_done, g)
                    act.activation(osb[:], psO[:], ACT.Copy).then_inc(o_copied, 1)

                two_halves(act, n_groups, step)

            @block.vector
            def _(dve):
                for p in range(2):
                    dve.memset(kf[p][64:65, :], 1.0)
                dve.drain()
                dve.memset(G["tick"][:], 0.0).then_inc(ones_set, 1)

                def normalize(g, p, r):
                    dve.wait_ge(lb_ready, g + 1)
                    dve.reciprocal(rec[:], psL[:]).then_inc(rec_done, 1)
                    dve.drain()
                    wait(dve, stored[p], r * 2 * 16)
                    dve.wait_ge(o_copied, g + 1)
                    dve.tensor_tensor(on[p][:], osb[:], rec[:], ALU.mult).then_inc(o_done, 1)

                def step(front, back):
                    if front:
                        g, p, r = front
                        if back and (not isinstance(g, int) or g > 1):
                            normalize(g - 2, p, r - 1)
                        dve.wait_ge(ld[p], 16 * n_ld * (r + 1))
                        wait(dve, s_ready, g * NS)
                        dve.tensor_copy(qs[:], qf[p][0:hd, :])
                        dve.tensor_copy(ks[:], kf[p][0:hd, :]).then_inc(cast, 1)
                        for s in range(NS):
                            dve.wait_ge(s_ready, g * NS + s + 1)
                            dve.tensor_reduce(mx[:, s:s + 1], ps1[s % 2][:], AX.X, ALU.max).then_inc(s_free, 1)
                        wait(dve, mld[p], 16 * r)
                        dve.wait_ge(mt_ready, g + 1)
                        dve.tensor_scalar(neg[p][:], ps1[1][0:QT, 0:P], -1.0, None, ALU.mult).then_inc(neg_ready, 1)
                    elif back:
                        g, p, r = back
                        normalize(g - 1, 1 - p, r)
                        normalize(g, p, r)

                two_halves(dve, n_groups, step)



def n_pieces(K):
    n = K * T // R + E - 1
    return n + n % 2


def route_stage(nc, G, tag, K, rows, sorted_rows, table, place, weight):
    NJ = n_pieces(K)
    KN = K * NT
    with Stage(nc, tag) as st:
        lg = G["logits"]
        iota_i, iota = st.sb("iota_i", [P, NT, E], I32), st.sb("iota", [P, NT, E])
        start_i, starts = st.sb("start_i", [P, NJ], I32), st.sb("starts", [P, NJ])
        top = st.sb("top", [P, K, NT])
        eq, cand, l2 = st.sb("eq", [P, NT, E]), st.sb("cand", [P, NT, E]), st.sb("l2", [P, NT, E])
        first = st.sb("first", [P, NT])
        oh = st.sb("onehot", [P, KN, E])
        tot = [st.sb(f"tot{i}", [P, KN, E]) for i in range(2)]
        count, count_i = st.sb("count", [P, E]), st.sb("count_i", [P, E], I32)
        basee = st.sb("base", [P, E])
        pos = st.sb("pos", [P, KN, E])
        posr = st.sb("posr", [P, KN])
        ex, owner = st.sb("ex", [P, NT]), st.sb("owner", [P, NJ])
        ge = st.sb("ge", [P, NJ])
        zero = st.sb("zero", [P, 2, D])
        psB, psT_ = st.ps("before", [P, KN * E]), st.ps("totals", [P, KN * E])
        iotas, oh_ready, counted = st.sem("iotas"), st.sem("oh_ready"), st.sem("counted")
        exp_in, exp_out = st.sem("exp_in"), st.sem("exp_out")
        zeroed, cleared, placed, sent = st.sem("zeroed"), st.sem("cleared"), st.sem("placed"), st.sem("sent")

        with st.block() as block:
            @block.gpsimd
            def _(pool):
                pool.iota(iota_i[:], pattern=[[0, NT], [1, E]], base=0, channel_multiplier=0)
                pool.iota(start_i[:], pattern=[[R, NJ]], base=0, channel_multiplier=0).then_inc(iotas, 1)
                pool.wait_ge(placed, 1)
                pool.wait_ge(cleared, NJ * 16)
                for k in range(K):
                    for t in range(NT):
                        pool.indirect_dma_start(
                            sorted_rows, bass.IndirectOffsetOnAxis(ap=place[:, k * NT + t:k * NT + t + 1], axis=0),
                            rows[:, t, :], None).then_inc(sent, 16)
                pool.wait_ge(sent, K * NT * 16)

            @block.sync
            def _(sp):
                sp.wait_ge(zeroed, 1)
                for j in range(NJ):
                    sp.dma_start(sorted_rows[j * R:(j + 1) * R, :].rearrange("(t p) d -> p t d", p=P), zero[:]
                                 ).then_inc(cleared, 16)
                sp.wait_ge(cleared, NJ * 16)

            @block.tensor
            def _(pe):
                pe.wait_ge(oh_ready, 1)
                flat = oh[:].rearrange("p s e -> p (s e)")
                pe.matmul(psB[:], G["lower"][:], flat, start=True, stop=True)
                pe.matmul(psT_[:], G["ones"][:], flat, start=True, stop=True).then_inc(counted, 1)

            @block.scalar
            def _(act):
                act.wait_ge(exp_in, 1)
                act.activation(ex[:], first[:], ACT.Exp).then_inc(exp_out, 1)

            @block.vector
            def _(dve):
                def op(ins):
                    dve.drain()

                op(dve.memset(zero[:], 0.0))
                dve.memset(G["tick"][:], 0.0).then_inc(zeroed, 1)
                dve.wait_ge(iotas, 1)
                op(dve.tensor_copy(iota[:], iota_i[:]))
                op(dve.tensor_copy(starts[:], start_i[:]))
                op(dve.tensor_copy(l2[:], lg[:]))
                for k in range(K):
                    sel = oh[:, k * NT:(k + 1) * NT, :]
                    op(dve.tensor_reduce(top[:, k, :], l2[:], AX.X, ALU.max))
                    op(dve.tensor_tensor(eq[:], l2[:], top[:, k, :].unsqueeze(2).broadcast_to([P, NT, E]), ALU.is_equal))
                    op(dve.tensor_scalar(cand[:], iota[:], -float(E), None, ALU.add))
                    op(dve.tensor_tensor(cand[:], cand[:], eq[:], ALU.mult))
                    op(dve.tensor_reduce(first[:], cand[:], AX.X, ALU.min))
                    op(dve.tensor_scalar(first[:], first[:], float(E), None, ALU.add))
                    op(dve.tensor_tensor(sel, iota[:], first[:].unsqueeze(2).broadcast_to([P, NT, E]), ALU.is_equal))
                    if k + 1 < K:
                        op(dve.scalar_tensor_tensor(l2[:].rearrange("p t e -> p (t e)"), sel.rearrange("p t e -> p (t e)"),
                                                    NEG, l2[:].rearrange("p t e -> p (t e)"), ALU.mult, ALU.add))
                dve.memset(G["tick"][:], 0.0).then_inc(oh_ready, 1)
                if K == 1:
                    op(dve.tensor_scalar(first[:], top[:, 0, :], -1.0, None, ALU.mult))
                else:
                    op(dve.tensor_tensor(first[:], top[:, 1, :], top[:, 0, :], ALU.subtract))
                dve.memset(G["tick"][:], 0.0).then_inc(exp_in, 1)
                dve.wait_ge(counted, 1)
                op(dve.tensor_copy(tot[0][:].rearrange("p s e -> p (s e)"), psT_[:]))
                a, d = 0, 1
                while d < KN:
                    dve.tensor_copy(tot[1 - a][:, 0:d, :], tot[a][:, 0:d, :])
                    op(dve.tensor_tensor(tot[1 - a][:, d:, :], tot[a][:, d:, :], tot[a][:, 0:KN - d, :], ALU.add))
                    a, d = 1 - a, 2 * d
                op(dve.tensor_scalar(count_i[:], tot[a][:, KN - 1, :], float(R - 1), None, ALU.add))
                shift = R.bit_length() - 1
                op(dve.tensor_scalar(count_i[:], count_i[:], shift, shift, ALU.logical_shift_right,
                                     ALU.logical_shift_left))
                op(dve.tensor_copy(count[:], count_i[:]))
                op(dve.memset(basee[:], 0.0))
                for e in range(1, E):
                    op(dve.tensor_tensor(basee[:, e:e + 1], basee[:, e - 1:e], count[:, e - 1:e], ALU.add))
                op(dve.tensor_tensor(pos[:], psB[:].rearrange("p (s e) -> p s e", e=E),
                                     basee[:].unsqueeze(1).broadcast_to([P, KN, E]), ALU.add))
                op(dve.tensor_tensor(pos[:, 1:, :], pos[:, 1:, :], tot[a][:, 0:KN - 1, :], ALU.add))
                op(dve.tensor_tensor(pos[:], pos[:], oh[:], ALU.mult))
                op(dve.tensor_reduce(posr[:], pos[:], AX.X, ALU.add))
                op(dve.tensor_copy(place[:], posr[:]))
                dve.memset(G["tick"][:], 0.0).then_inc(placed, 1)
                op(dve.memset(owner[:], 0.0))
                for e in range(1, E):
                    op(dve.tensor_scalar(ge[:], starts[:], basee[:, e:e + 1], None, ALU.is_ge))
                    op(dve.tensor_tensor(owner[:], owner[:], ge[:], ALU.add))
                op(dve.tensor_copy(table[:], owner[0:1, :]))
                dve.wait_ge(exp_out, 1)
                op(dve.tensor_scalar(first[:], ex[:], 1.0, None, ALU.add))
                op(dve.reciprocal(weight[:, 0, :], first[:]))
                if K == 2:
                    op(dve.tensor_tensor(weight[:, 1, :], ex[:], weight[:, 0, :], ALU.mult))


def expert_stage(nc, G, tag, K, sorted_rows, results, table, *, F, w1, w2, w3=None, b1=None, b2=None, g=None, b=None):
    NJ = n_pieces(K)
    NF = F // P
    RT = R // P
    UP = NF * (2 if w3 is not None else 1)
    affine = g is not None
    with Stage(nc, tag) as st:
        xg = [st.sb(f"xg{p}", [P, RT, D]) for p in range(2)]
        xT = [st.sb(f"xT{p}", [P, KD, R]) for p in range(2)]
        w1s = [st.sb(f"w1_{p}", [P, KD, F]) for p in range(2)]
        w3s = [st.sb(f"w3_{p}", [P, KD, F]) for p in range(2)] if w3 is not None else None
        w2s = [st.sb(f"w2_{p}", [P, NF, D]) for p in range(2)]
        if affine:
            gb = [st.sb(f"gb{p}", [P, 2, KD]) for p in range(2)]
            b1s = [st.sb(f"b1_{p}", [P, NF]) for p in range(2)]
            b2s = [st.sb(f"b2_{p}", [P, RT, D]) for p in range(2)]
        gate = st.sb("gated", [P, 2, R])
        h = [st.sb(f"h{p}", [P, NF, R]) for p in range(2)]
        yo = [st.sb(f"y{p}", [P, RT, D]) for p in range(2)]
        psX = [st.ps(f"psX{p}", [P, RT, KD, P]) for p in range(2)]
        psU = [st.ps(f"psU{i}", [P, 512]) for i in range(4)]
        psD = [st.ps(f"psD{p}", [P, RT, D]) for p in range(2)]
        ld = [st.sem(f"loaded{p}") for p in range(2)]
        turned, xT_ready = st.sem("turned"), st.sem("xT_ready")
        u_ready, u_free, gated = st.sem("up_ready"), st.sem("up_free"), st.sem("gate_ready")
        d_ready, y_ready = st.sem("down_ready"), st.sem("y_ready")
        stored = [st.sem(f"stored{p}") for p in range(2)]
        x_ld = [st.sem(f"rows_loaded{p}") for p in range(2)]
        n_x_ld = 16 * (3 if affine else 1)
        n_ld = 16 * (3 + RT if affine else 3)

        with st.block() as block:
            @block.sync
            def _(sp):
                def step(front, back):
                    if front:
                        j, p, r = front
                        e = sp.value_load(table[0:1, bass.ds(j, 1)], min_val=0, max_val=E - 1)
                        wait(sp, d_ready, j - 1)
                        sp.dma_start(xg[p][:], sorted_rows[bass.ds(j * R, R), :].rearrange("(t p) d -> p t d", p=P)
                                     ).then_inc(x_ld[p], 16)
                        if affine:
                            for i, src in enumerate((g, b)):
                                sp.dma_start(gb[p][:, i, :], src[bass.ds(e, 1), :, :].rearrange("e p k -> p (e k)")
                                             ).then_inc(x_ld[p], 16)
                        pairs = [(w1s[p], w1)] + ([(w3s[p], w3)] if w3 is not None else []) + [(w2s[p], w2)]
                        for dst, src in pairs:
                            sp.dma_start(dst[:], src[bass.ds(e, 1), :, :].rearrange("e (k p) n -> p (e k) n", p=P)
                                         ).then_inc(ld[p], 16)
                        if affine:
                            sp.dma_start(b1s[p][:], b1[bass.ds(e, 1), :, :].rearrange("e p k -> p (e k)")
                                         ).then_inc(ld[p], 16)
                            for t in range(RT):
                                sp.dma_start(b2s[p][:, t, :], b2[bass.ds(e, 1), :].broadcast_to([P, D])
                                             ).then_inc(ld[p], 16)
                    if back:
                        j, p, r = back
                        sp.wait_ge(y_ready, j + 1)
                        sp.dma_start(results[bass.ds(j * R, R), :].rearrange("(t p) d -> p t d", p=P), yo[p][:]
                                     ).then_inc(stored[p], 16)

                two_halves(sp, NJ, step)
                for p in range(2):
                    sp.wait_ge(stored[p], NJ // 2 * 16)

            @block.tensor
            def _(pe):
                def turn(front):
                    j, p, r = front
                    pe.wait_ge(x_ld[p], n_x_ld * (r + 1))
                    wait(pe, xT_ready, j - 1)
                    for t in range(RT):
                        for k in range(KD):
                            mm = pe.transpose(psX[p][:, t, k, :], xg[p][:, t, k * P:(k + 1) * P], G["ident"][:])
                    mm.then_inc(turned, 1)

                def step(front, back):
                    if back:
                        j, p, r = back
                        pe.wait_ge(xT_ready, j + 1)
                        pe.wait_ge(ld[p], n_ld * (r + 1))
                        for n in range(UP):
                            if not (isinstance(j, int) and j == 0 and n < 4):
                                pe.wait_ge(u_free, j * UP + n - 3)
                            ws = w1s if w3 is None or n % 2 == 0 else w3s
                            m = n if w3 is None else n // 2
                            for k in range(KD):
                                mm = pe.matmul(psU[n % 4][:, 0:R], ws[p][:, k, m * P:(m + 1) * P], xT[p][:, k, :],
                                               start=(k == 0), stop=(k == KD - 1))
                            mm.then_inc(u_ready, 1)
                        wait(pe, y_ready, j - 1)
                        for t in range(RT):
                            if t == 1 and front:
                                turn(front)
                            for m in range(NF):
                                if t == 0 and (m == 0 or m > NF - 4):
                                    pe.wait_ge(u_free, j * UP + max(m + 1, NF - 3) * (UP // NF))
                                mm = pe.matmul(psD[p][:, t, :], h[p][:, m, t * P:(t + 1) * P], w2s[p][:, m, :],
                                               start=(m == 0), stop=(m == NF - 1))
                        mm.then_inc(d_ready, 1)
                    else:
                        turn(front)

                two_halves(pe, NJ, step)

            @block.scalar
            def _(act):
                def step(front, back):
                    if back:
                        j, p, r = back
                        for m in range(NF if w3 is not None else 0):
                            act.wait_ge(u_ready, j * UP + 2 * m + 1)
                            if m >= 2:
                                act.wait_ge(u_free, j * UP + 2 * (m - 1))
                            act.activation(gate[:, m % 2, :], psU[2 * m % 4][:, 0:R], ACT.Silu).then_inc(gated, 1)
                    if front:
                        j, p, r = front
                        act.wait_ge(turned, j + 1)
                        wait(act, d_ready, j - 1)
                        for k in range(KD):
                            dst = xT[p][:, k, :].rearrange("p (t q) -> p t q", q=P)
                            if affine:
                                ins = act.activation(dst, psX[p][:, :, k, :], ACT.Identity, scale=gb[p][:, 0, k:k + 1],
                                                     bias=gb[p][:, 1, k:k + 1])
                            else:
                                ins = act.activation(dst, psX[p][:, :, k, :], ACT.Copy)
                        ins.then_inc(xT_ready, 1)

                two_halves(act, NJ, step)

            @block.vector
            def _(dve):
                def step(front, back):
                    if not back:
                        return
                    j, p, r = back
                    if w3 is None:
                        for n in range(UP):
                            dve.wait_ge(u_ready, j * UP + n + 1)
                            dve.tensor_scalar(h[p][:, n, :], psU[n % 4][:, 0:R], b1s[p][:, n:n + 1], 0.0, ALU.add,
                                              ALU.max).then_inc(u_free, 1)
                    else:
                        for m in range(NF):
                            dve.wait_ge(gated, j * NF + m + 1)
                            dve.wait_ge(u_ready, j * UP + 2 * m + 2)
                            dve.tensor_tensor(h[p][:, m, :], psU[(2 * m + 1) % 4][:, 0:R], gate[:, m % 2, :],
                                              ALU.mult).then_inc(u_free, 2)
                    dve.wait_ge(d_ready, j + 1)
                    wait(dve, stored[p], 16 * r)
                    if affine:
                        dve.tensor_tensor(yo[p][:], psD[p][:], b2s[p][:], ALU.add).then_inc(y_ready, 1)
                    else:
                        dve.tensor_copy(yo[p][:], psD[p][:]).then_inc(y_ready, 1)

                two_halves(dve, NJ, step)


def combine_stage(nc, G, tag, K, results, place, weight, add, out=None):
    with Stage(nc, tag) as st:
        got = st.sb("got", [P, K * NT, D])
        fetched, ready, stored = st.sem("fetched"), st.sem("ready"), st.sem("stored")
        X = G["X"]
        with st.block() as block:
            @block.gpsimd
            def _(pool):
                for t in range(NT):
                    for k in range(K):
                        pool.indirect_dma_start(
                            got[:, t * K + k, :], None, results,
                            bass.IndirectOffsetOnAxis(ap=place[:, k * NT + t:k * NT + t + 1], axis=0)
                        ).then_inc(fetched, 16)

            @block.vector
            def _(dve):
                dve.tensor_tensor(X[:], X[:], add[:], ALU.add)
                dve.drain()
                dve.wait_ge(fetched, 16 * K * NT)
                for k in range(K):
                    for t in range(NT):
                        ins = dve.scalar_tensor_tensor(X[:, t, :], got[:, t * K + k, :], weight[:, k, t:t + 1],
                                                       X[:, t, :], ALU.mult, ALU.add)
                        if k == K - 1:
                            ins.then_inc(ready, 1)
                    dve.drain()

            @block.sync
            def _(sp):
                if out is not None:
                    for t in range(NT):
                        sp.wait_ge(ready, t + 1)
                        sp.dma_start(out[t * P:(t + 1) * P, :], X[:, t, :]).then_inc(stored, 16)
                    sp.wait_ge(stored, 16 * NT)



def decoder(nc, A, out):
    G = {"cos": A["cos"], "sin": A["sin"]}
    Q16 = nc.dram_tensor("q16_scratch", (3, HEADS // 4, 2 * B, 64, 512), BF16, kind="Internal").ap()
    K16 = nc.dram_tensor("k16_scratch", (3, HEADS // 4, 2 * B, 64, 512), BF16, kind="Internal").ap()
    V16 = nc.dram_tensor("v16_scratch", (HEADS // 4, 2 * B, P, 4, 4 * 17), F32, kind="Internal").ap()
    QKW = nc.dram_tensor("qk_wide_scratch", (2048, T), F32, kind="Internal").ap()
    VW = nc.dram_tensor("vw_scratch", (HEADS, P, NT, 65), F32, kind="Internal").ap()
    CK = [nc.dram_tensor(f"ctx_k_scratch{i}", (3, HEADS // 4, B, 64, SC), BF16, kind="Internal").ap() for i in range(2)]
    CV = [nc.dram_tensor(f"ctx_v_scratch{i}", (HEADS // 4, B, SC, 4 * 17), F32, kind="Internal").ap() for i in range(2)]
    CM = nc.dram_tensor("mask_scratch", (HEADS // 4 * B, 4, SC), BF16, kind="Internal").ap()
    OA = nc.dram_tensor("attn_scratch", (HEADS // 4, 2 * B, 64, 512), F32, kind="Internal").ap()
    SU = nc.dram_tensor("sums_scratch", (2, 3, 4 * S), F32, kind="Internal").ap()
    OW = nc.dram_tensor("attn_wide_scratch", (1024, T), F32, kind="Internal").ap()
    SR = nc.dram_tensor("sorted_scratch", (n_pieces(2) * R, D), F32, kind="Internal").ap()
    RE = nc.dram_tensor("results_scratch", (n_pieces(2) * R, D), F32, kind="Internal").ap()

    def units(*scratches):
        return [[scr[:, 2 * m + e] for e in range(2)] for scr in scratches for m in range(2)]

    a16 = dict(q=Q16, k=K16, v=V16, o=OA, sums=SU)

    with Stage(nc, "g") as g:
        for name in ("X", "Y", "Z"):
            G[name] = g.sb(name, [P, NT, D])
        G["ident"], G["lower"], G["ones"], G["sel16"] = (g.sb(n, [P, P]) for n in ("ident", "lower", "ones", "sel16"))
        G["x_loaded"] = g.sem("x_loaded")
        G["identb"], G["maskS"], G["maskT"] = (g.sb(n, [P, P], BF16) for n in ("identb", "maskSb", "maskTb"))
        G["eps"], G["tick"] = g.sb("eps", [P, 1]), g.sb("tick", [1, 1])
        G["logits"] = g.sb("logits", [P, NT, E])
        place = [g.sb(f"place{k}", [P, k * NT], I32) for k in (1, 2)]
        weight = [g.sb(f"weight{k}", [P, k, NT]) for k in (1, 2)]
        table = [g.sb(f"table{k}", [1, n_pieces(k)], I32) for k in (1, 2)]

        setup_stage(nc, G, A["x"])
        context_stage(nc, G, "c", A["ctxT"], [(A["wk1"], A["bk1"], A["wv1"], A["bv1"], CK[0], CV[0]),
                                              (A["wk4"], A["bk4"], A["wv4"], A["bv4"], CK[1], CV[1])], A["mask"], CM)
        token_stage(nc, G, "t0", x_loaded=G["x_loaded"], norm="ln", resid=G["X"], units=units(Q16, K16), rope=True, wf=A["wf0"], bf=A["bf0"],
                    wv=A["wv0"], bv=A["bv0"], outs=V16)
        attention_stage(nc, G, "a0", causal=True, **a16)
        token_stage(nc, G, "t1", norm="ln", attn=(OA, A["wo0"], A["bo0"]), resid=G["X"], units=units(Q16),
                    wf=A["wq1"], bf=A["bq1"])
        attention_stage(nc, G, "a1", q=Q16, k=CK[0], v=CV[0], o=OA, cross=True, mask=CM)
        token_stage(nc, G, "t2", norm="ln_ln", attn=(OA, A["wo1"], A["bo1"]), resid=G["X"], gate=A["cent"])
        route_stage(nc, G, "r2", 1, G["Z"], SR[0:n_pieces(1) * R, :], table[0], place[0], weight[0])
        expert_stage(nc, G, "e2", 1, SR, RE, table[0], F=1024, w1=A["w1_2"], w2=A["w2_2"], b1=A["b1_2"], b2=A["b2_2"],
                     g=A["g_2"], b=A["b_2"])
        combine_stage(nc, G, "m2", 1, RE[0:n_pieces(1) * R, :], place[0], weight[0], G["Y"])
        token_stage(nc, G, "t3", norm="ln", resid=G["X"], units=[{}] * 16, wide=QKW, wf=A["wf3"],
                    bf=A["bf3"], wv=A["wv3"], bv=A["bv3"], outs=VW, heads_group=1, hd=64)
        wide_attention_stage(nc, G, "a3", q=QKW[0:1024], k=QKW[1024:2048], v=VW, o=OW)
        token_stage(nc, G, "t4", norm="ln", attn=(OW, A["wo3"], A["bo3"]), resid=G["X"], units=units(Q16),
                    wf=A["wq4"], bf=A["bq4"])
        attention_stage(nc, G, "a4", q=Q16, k=CK[1], v=CV[1], o=OA, cross=True)
        token_stage(nc, G, "t5", norm="ln_rms", attn=(OA, A["wo4"], A["bo4"]), resid=G["X"], units=units(Q16, K16),
                    wf=A["wf5"], fscale=A["ln1"], wv=A["wv5"], outs=V16)
        attention_stage(nc, G, "a5", **a16)
        token_stage(nc, G, "t6", norm="rms", attn=(OA, A["wo5"], None), resid=G["Y"], ln2=A["ln2"], gate=A["gate"])
        route_stage(nc, G, "r6", 2, G["Z"], SR, table[1], place[1], weight[1])
        expert_stage(nc, G, "e6", 2, SR, RE, table[1], F=512, w1=A["w1_6"], w3=A["w3_6"], w2=A["w2_6"])
        combine_stage(nc, G, "m6", 2, RE, place[1], weight[1], G["Y"], out)



def layout(inputs):
    a = {k: np.asarray(v) for k, v in inputs.items()}
    c = np.ascontiguousarray
    per_part = lambda v: c(v.reshape(-1, P).T)
    swap = np.arange(D) ^ 1
    w, bias = a["L0_attn_w_attn"], a["L0_attn_b_attn"]
    wq, wk, bq, bk = w[:, :D], w[:, D:2 * D], bias[:D], bias[D:2 * D]
    hd = D // HEADS
    inv = (np.float32(1.0) / np.float32(10000.0) ** (np.arange(0, hd, 2, dtype=np.float32) / np.float32(hd))
           ).astype(np.float32)
    freqs = np.repeat(np.arange(S, dtype=np.float32)[:, None] * inv[None, :], 2, axis=-1)
    sign = np.where(np.arange(hd) % 2 == 0, -1.0, 1.0).astype(np.float32)
    table = lambda t: c(np.tile(t.T.astype(np.float32), (P // hd, B)))
    out = {
        "x": c(a["x"].reshape(T, D)),
        "ctxT": c(a["ctx_1024"].reshape(B * SC, D).T),
        "mask": c(a["mask_Bx1xS2_if1"]),
        "cos": table(np.cos(freqs)), "sin": table(np.sin(freqs) * sign),
        "wf0": c(np.concatenate([wq, wk, wq[:, swap], wk[:, swap]], 1)),
        "bf0": per_part(np.concatenate([bq, bk, bq[swap], bk[swap]])),
        "wv0": c(w[:, 2 * D:]), "bv0": c(bias[2 * D:]),
        "wo0": a["L0_attn_w_proj"], "bo0": a["L0_attn_b_proj"],
        "wq1": c(a["L0_xattn_Wq"].T), "bq1": per_part(a["L0_xattn_bq"]),
        "wk1": c(a["L0_xattn_Wk"].T), "bk1": per_part(a["L0_xattn_bk"]),
        "wv1": c(a["L0_xattn_Wv"].T), "bv1": a["L0_xattn_bv"],
        "wo1": c(a["L0_xattn_Wo"].T), "bo1": a["L0_xattn_bo"],
        "cent": c(a["L0_ffn_centroids"].T),
        "w1_2": c(a["L0_ffn_w1"].transpose(0, 2, 1)), "w2_2": c(a["L0_ffn_w2"].transpose(0, 2, 1)),
        "b1_2": c(a["L0_ffn_b1"].reshape(E, -1, P).transpose(0, 2, 1)), "b2_2": a["L0_ffn_b2"],
        "g_2": c(a["L0_ffn_ln_g"].reshape(E, -1, P).transpose(0, 2, 1)),
        "b_2": c(a["L0_ffn_ln_b"].reshape(E, -1, P).transpose(0, 2, 1)),
        "wf3": c(a["L1_attn_W_qkv"][:, :2048]), "bf3": per_part(a["L1_attn_b_qkv"][:2048]),
        "wv3": c(a["L1_attn_W_qkv"][:, 2048:]), "bv3": c(a["L1_attn_b_qkv"][2048:]),
        "wo3": a["L1_attn_W_out"], "bo3": a["L1_attn_b_out"],
        "wq4": c(a["L1_xattn_w_q"].T), "bq4": per_part(a["L1_xattn_b_q"]),
        "wk4": c(a["L1_xattn_w_k"].T), "bk4": per_part(a["L1_xattn_b_k"]),
        "wv4": c(a["L1_xattn_w_v"].T), "bv4": a["L1_xattn_b_v"],
        "wo4": c(a["L1_xattn_w_o"].T), "bo4": a["L1_xattn_b_o"],
        "ln1": per_part(a["L1_ffn_ln1_w"]), "ln2": a["L1_ffn_ln2_w"],
        "wf5": c(np.concatenate([a["L1_ffn_wq"].T, a["L1_ffn_wk"].T], 1)), "wv5": c(a["L1_ffn_wv"].T),
        "wo5": c(a["L1_ffn_wo"].T), "gate": c(a["L1_ffn_gate_w"].T),
        "w1_6": c(a["L1_ffn_w1"].transpose(0, 2, 1)), "w3_6": c(a["L1_ffn_w3"].transpose(0, 2, 1)),
        "w2_6": c(a["L1_ffn_w2"].transpose(0, 2, 1)),
    }
    return out


def kernel(**inputs):
    import concourse.bacc as bacc
    from concourse.bass_utils import run_bass_kernel_spmd

    nc = bacc.Bacc("TRN2", target_bir_lowering=False, num_devices=1)
    arrays, args = {}, {}
    for name, a in layout(inputs).items():
        arrays[f"in_{name}"] = a
        args[name] = nc.dram_tensor(f"in_{name}", a.shape, mybir.dt.from_np(a.dtype), kind="ExternalInput").ap()
    out = nc.dram_tensor("out", (T, D), F32, kind="ExternalOutput").ap()
    decoder(nc, args, out)
    r = run_bass_kernel_spmd(nc, [arrays], core_ids=[0])
    return r.results[0]["out"].reshape(B, S, D)
```
